# Optimizing a Trainium2 kernel written in Bass

```python
import numpy as np
import jax
import jax.numpy as jnp

def _softmax(x, axis=-1):
    return jax.nn.softmax(x, axis=axis)

def _gelu(x):
    return jax.nn.gelu(x, approximate=True)

def _silu(x):
    return jax.nn.silu(x)

def _sigmoid(x):
    return jax.nn.sigmoid(x)

def _layernorm(x, axis=-1, eps=1e-05):
    m = jnp.mean(x, axis=axis, keepdims=True)
    v = jnp.var(x, axis=axis, keepdims=True)
    return (x - m) / jnp.sqrt(v + eps)

def _scatter_add(tgt, idx, src, axis=0):
    return tgt.at[idx].add(src)

def _segment_sum(src, seg, n):
    return jax.ops.segment_sum(src, seg, n)
kernel_name = 'mk_decoder_preln_d1_seqx_r4_754e92'

def setup_inputs(seed: int=0):
    np.random.seed(seed)
    _w = jnp.asarray

    def _rec_inputs():
        import jax
        import jax.numpy as jnp
        _rk = jax.random.key(seed)
        x = -0.0003929 + 0.9999 * jax.random.normal(jax.random.fold_in(_rk, 1), (8, 512, 256), jnp.float32)
        _lenS = 512 - jax.random.randint(jax.random.fold_in(_rk, 7), (8,), 0, max(1, 512 // 4) + 1, jnp.int32)
        _lenS2 = 64 - jax.random.randint(jax.random.fold_in(_rk, 8), (8,), 0, max(1, 64 // 4) + 1, jnp.int32)
        _ctx_1024P = jax.random.normal(jax.random.fold_in(_rk, 11), (8, 16, 256), jnp.float32)
        _ctx_1024c = jax.random.dirichlet(jax.random.fold_in(_rk, 511), 0.3 * jnp.ones((16,), jnp.float32), (8, 64))
        _ctx_1024t = jnp.einsum('bsk,bkd->bsd', _ctx_1024c, _ctx_1024P)
        _ctx_1024t = _ctx_1024t * jax.lax.rsqrt(jnp.mean(jnp.square(_ctx_1024t)) + 1e-12) * 0.953939
        ctx_1024 = 2.81802e-05 + 1.00001 * (_ctx_1024t + 0.3 * jax.random.normal(jax.random.fold_in(_rk, 611), (8, 64, 256), jnp.float32))
        return (x, ctx_1024)
    x, ctx_1024 = _rec_inputs()

    def _L0_attn_setup():
        import jax, jax.numpy as jnp
        import numpy as np
        B, S, D, H = (2, 512, 256, 16)
        HD = D // H
        key = jax.random.key(seed)
        ks = jax.random.split(key, 5)
        return {'x': jax.random.normal(ks[0], (B, S, D), dtype=jnp.float32), 'qkv_w': jax.random.normal(ks[1], (3 * D, D), dtype=jnp.float32) * (1.0 / np.sqrt(D)), 'qkv_b': jax.random.normal(ks[2], (3 * D,), dtype=jnp.float32) * 0.02, 'proj_w': jax.random.normal(ks[3], (D, D), dtype=jnp.float32) * (1.0 / np.sqrt(D)), 'proj_b': jax.random.normal(ks[4], (D,), dtype=jnp.float32) * 0.02}
    _L0_attn_all = _L0_attn_setup()
    _L0_attn_in = {k: v for k, v in _L0_attn_all.items() if k in ('qkv_w', 'qkv_b', 'proj_w', 'proj_b')}
    del _L0_attn_all

    def _L0_xattn_setup():
        import jax, jax.numpy as jnp
        import numpy as np
        B, S, D = (4, 1024, 256)
        key = jax.random.key(seed)
        kq, kk, kv = jax.random.split(key, 3)
        q = jax.random.normal(kq, (B, S, D), dtype=jnp.float32)
        k = jax.random.normal(kk, (B, S, D), dtype=jnp.float32)
        v = jax.random.normal(kv, (B, S, D), dtype=jnp.float32)
        return {'q': q, 'k': k, 'v': v}
    _L0_xattn_all = _L0_xattn_setup()
    _L0_xattn_in = {k: v for k, v in _L0_xattn_all.items() if k in ()}
    del _L0_xattn_all

    def _L0_ffn_setup():
        import jax, jax.numpy as jnp
        import numpy as np
        B, T, C = (2, 512, 256)
        E, F = (8, 256)
        FS = 512
        TOP_K = 2
        key = jax.random.key(seed)
        ks = jax.random.split(key, 6)
        s = lambda *d: 1.0 / np.sqrt(d[-1])
        return {'hidden_tensor': jax.random.normal(ks[0], (B, T, C), jnp.float32), 'w_router': jax.random.normal(ks[1], (E, C), jnp.float32) * s(C), 'w1_stack': jax.random.normal(ks[2], (E, F, C), jnp.float32) * s(C), 'w2_stack': jax.random.normal(ks[3], (E, C, F), jnp.float32) * s(F), 'ws1': jax.random.normal(ks[4], (FS, C), jnp.float32) * s(C), 'ws2': jax.random.normal(ks[5], (C, FS), jnp.float32) * s(FS)}
    _L0_ffn_all = _L0_ffn_setup()
    _L0_ffn_in = {k: v for k, v in _L0_ffn_all.items() if k in ('w_router', 'w1_stack', 'w2_stack', 'ws1', 'ws2')}
    del _L0_ffn_all
    return {'x': x, 'ctx_1024': ctx_1024, 'L0_attn_qkv_w': _L0_attn_in['qkv_w'], 'L0_attn_qkv_b': _L0_attn_in['qkv_b'], 'L0_attn_proj_w': _L0_attn_in['proj_w'], 'L0_attn_proj_b': _L0_attn_in['proj_b'], 'L0_ffn_w_router': _L0_ffn_in['w_router'], 'L0_ffn_w1_stack': _L0_ffn_in['w1_stack'], 'L0_ffn_w2_stack': _L0_ffn_in['w2_stack'], 'L0_ffn_ws1': _L0_ffn_in['ws1'], 'L0_ffn_ws2': _L0_ffn_in['ws2']}

def reference(x, ctx_1024, L0_attn_qkv_w, L0_attn_qkv_b, L0_attn_proj_w, L0_attn_proj_b, L0_ffn_w_router, L0_ffn_w1_stack, L0_ffn_w2_stack, L0_ffn_ws1, L0_ffn_ws2):
    import jax
    import jax.numpy as jnp

    def _L0_attn_ref(x, qkv_w, qkv_b, proj_w, proj_b):
        import jax, jax.numpy as jnp
        import numpy as np
        B, S, D, H = (2, 512, 256, 16)
        HD = D // H
        b, s, d = x.shape
        qkv = jnp.einsum('bsd,ed->bse', x, qkv_w) + qkv_b
        qkv = qkv.reshape(b, s, 3, H, HD)
        q = jnp.transpose(qkv[:, :, 0], (0, 2, 1, 3))
        k = jnp.transpose(qkv[:, :, 1], (0, 2, 1, 3))
        v = jnp.transpose(qkv[:, :, 2], (0, 2, 1, 3))
        scale = 1.0 / jnp.sqrt(jnp.asarray(HD, dtype=x.dtype))
        scores = jnp.einsum('bhqe,bhke->bhqk', q, k) * scale
        attn = jax.nn.softmax(scores, axis=-1)
        out = jnp.einsum('bhqk,bhke->bhqe', attn, v)
        out = jnp.transpose(out, (0, 2, 1, 3)).reshape(b, s, d)
        out = jnp.einsum('bsd,ed->bse', out, proj_w) + proj_b
        return out

    def _L0_xattn_ref(q, k, v):
        import jax, jax.numpy as jnp
        import numpy as np
        B, S, D = (4, 1024, 256)
        scale = jnp.asarray(q.shape[-1], q.dtype) ** (-0.5)
        logits = jnp.einsum('bqd,bkd->bqk', q, k) * scale
        weights = jax.nn.softmax(logits, axis=-1)
        return jnp.einsum('bqk,bkd->bqd', weights, v)

    def _L0_ffn_ref(hidden_tensor, w_router, w1_stack, w2_stack, ws1, ws2):
        import jax, jax.numpy as jnp
        import numpy as np
        B, T, C = (2, 512, 256)
        E, F = (8, 256)
        FS = 512
        TOP_K = 2
        Bb, Tt, Cc = hidden_tensor.shape
        x = hidden_tensor.reshape(-1, Cc)
        t = x.shape[0]
        logits = x @ w_router.T
        probs = jax.nn.softmax(logits, axis=-1)
        expert_weight, expert_idx = jax.lax.top_k(probs, TOP_K)
        expert_weight = expert_weight / jnp.sum(expert_weight, axis=-1, keepdims=True)
        flat_e = expert_idx.reshape(-1)
        order = jnp.argsort(flat_e, stable=True)
        sorted_e = flat_e[order]
        flat_tok = jnp.repeat(jnp.arange(t), TOP_K)
        sorted_tok = flat_tok[order]
        sorted_w = expert_weight.reshape(-1)[order]
        counts = jnp.bincount(sorted_e, length=E)
        offsets = jnp.concatenate([jnp.zeros((1,), counts.dtype), jnp.cumsum(counts)])
        local_pos = jnp.arange(t * TOP_K) - offsets[sorted_e]
        cap = t * TOP_K
        binned = jnp.zeros((E, cap, Cc), x.dtype).at[sorted_e, local_pos].set(x[sorted_tok])
        inter = jnp.einsum('ecd,efd->ecf', binned, w1_stack)
        inter = jnp.square(jax.nn.relu(inter))
        outb = jnp.einsum('ecf,edf->ecd', inter, w2_stack)
        flat_out = outb[sorted_e, local_pos] * sorted_w[:, None]
        moe_out = jnp.zeros((t, Cc), x.dtype).at[sorted_tok].add(flat_out)
        moe_out = moe_out.reshape(Bb, Tt, Cc)
        sh = jnp.square(jax.nn.relu(jnp.einsum('btc,fc->btf', hidden_tensor, ws1)))
        shared_out = jnp.einsum('btf,cf->btc', sh, ws2)
        return shared_out + moe_out
    x = x + _L0_attn_ref(_layernorm(x, axis=-1), L0_attn_qkv_w, L0_attn_qkv_b, L0_attn_proj_w, L0_attn_proj_b)
    x = x + _L0_xattn_ref(_layernorm(x, axis=-1), ctx_1024, ctx_1024)
    x = x + _L0_ffn_ref(_layernorm(x, axis=-1), L0_ffn_w_router, L0_ffn_w1_stack, L0_ffn_w2_stack, L0_ffn_ws1, L0_ffn_ws2)
    return x

_drawn_inputs = setup_inputs


def setup_inputs(seed=0):
    import zlib

    import numpy as np

    out = dict(_drawn_inputs(seed))
    spreads = {}
    factors = {}
    for name, (base, spread) in spreads.items():
        noise = np.random.default_rng([zlib.crc32(name.encode()), seed]).standard_normal(out[name].shape)
        drawn = base * np.exp(spread * noise) if base else spread * noise
        out[name] = jnp.asarray(drawn.astype(out[name].dtype))
    for name, factor in factors.items():
        out[name] = (out[name] * factor).astype(out[name].dtype)
    return out
```

```python
from contextlib import ExitStack

import concourse.bass as bass
from concourse import mybir

F32 = mybir.dt.float32
BF16 = mybir.dt.bfloat16
ALU = mybir.AluOpType
ACT = mybir.ActivationFunctionType
AX = mybir.AxisListType

B, S, D = 8, 512, 256
H, HD = 16, 16
P = 128
TB = S // P
KD = D // P
GH = 4
NG = H // GH
SLOTS = NG * TB
AHEAD = 7
PARTS_Q = (0, 0, 0, 1, 1, 2)
PARTS_K = (0, 1, 2, 0, 1, 0)
NS = len(PARTS_Q)
KS_ROWS = NS * HD
KM_ROWS = KS_ROWS + 2
SC = 64
E, F = 8, 256
FS = 512
NU = E + FS // F
EPS = 1e-5


def decoder_layer(nc, x, ctx_n, ctx_t, wqk_t, bqk, wv_t, bv, wp_t, bp, wr_t, w1_t, w2_t, ws1_t,
                  ws2_t, ident_d, rank_d, out):
    scratch = nc.dram_tensor("qk_parts", [2, 3, 4, P, S], BF16).ap()
    with ExitStack() as stack:
        def sb(name, shape, dt=F32):
            return stack.enter_context(nc.sbuf_tensor(name, shape, dt))

        def sem(name):
            return stack.enter_context(nc.semaphore(name))

        bank = [stack.enter_context(nc.psum_tensor(f"bank{i}", [P, 512], F32)) for i in range(8)]

        xs = sb("xs", [P, B * TB, D])
        ident = sb("ident", [P, P])
        ctxT = sb("ctxT", [P, KD, B, SC])
        wr = sb("wr", [P, KD, E])
        rank = sb("rank", [P, TB, E])
        st = sb("st", [P, TB, 6])
        mv = sb("mv", [P, TB, 2])
        rstd = sb("rstd", [P, TB])
        var = sb("var", [P, TB])
        minus_half = sb("minus_half", [P, TB])
        xn = sb("xn", [P, TB, D])
        xnT = sb("xnT", [P, KD, S])
        wqk = sb("wqk", [P, KD, 2 * D])
        bqks = sb("bqks", [P, 4])
        wv = sb("wv", [P, KD, D])
        bvs = sb("bvs", [P, D])
        wp = sb("wp", [P, KD, D])
        bps = sb("bps", [P, D])
        QS = [sb(f"QS{i}", [P, H, S], BF16) for i in range(2)]
        KS = [sb(f"KS{i}", [P, H, S], BF16) for i in range(2)]
        VO = [sb(f"VO{i}", [P, TB, H, 32]) for i in range(2)]
        probs = sb("probs", [P, 2, GH, S])
        qk = sb("qk", [P, 4, S])
        rest = sb("rest", [P, 4, S])
        parts = sb("parts", [P, 3, 4, S], BF16)
        mneg = sb("mneg", [P, 2, GH * TB])
        mparts = sb("mparts", [GH * TB, 2, 2, P], BF16)
        o_sb = sb("o_sb", [P, S])
        rden = sb("rden", [P, TB, GH])
        o_nat = sb("o_nat", [P, TB, D])
        oT = sb("oT", [P, KD, S])
        w1s = QS[0][:].rearrange("p h s -> p (h s)").bitcast(F32).rearrange(
            "p (e k f) -> p e k f", e=E, k=KD)
        w2s = KS[0][:].rearrange("p h s -> p (h s)").bitcast(F32).rearrange(
            "p (e k f) -> p e k f", e=E, k=KD)
        sh = rest[:].rearrange("p a b -> p (a b)")
        ws1s = sh[:, 0:KD * FS].rearrange("p (k f) -> p k f", k=KD)
        ws2s = sh[:, KD * FS:].rearrange("p (k f) -> p k f", k=FS // P)
        ctxN = qk[:].rearrange("p a b -> p (a b)").rearrange("p (b d) -> p b d", b=B)
        relu = VO[0][:].rearrange("p t h c -> p (t h c)").rearrange("p (n s) -> p n s", n=4)
        hT = VO[1][:].rearrange("p t h c -> p (t h c)").rearrange("p (u f s) -> p u f s", u=2, f=2)
        xrT = probs[:, 0].rearrange("p (u k) s -> p u k s", u=2)
        pT = o_sb
        px = sb("px", [P, TB, SC])
        xm = sb("xm", [P, TB])
        xb = sb("xb", [P, TB])
        xsum = sb("xsum", [P, TB])
        xr = sb("xr", [P, TB])
        rt = {n: sb("rt_" + n, [P, TB, E]) for n in
              ("d", "e", "eq1", "s1", "oh1", "e2", "eq2", "s2", "oh2", "oh", "w")}
        rc = {n: sb("rc_" + n, [P, TB]) for n in ("m", "m1", "sm1", "m2", "sm2", "den", "r")}
        cw = sb("cw", [P, 2, TB, E])

        x_in = [sem(f"x_in{i}") for i in range(B)]
        w_in = sem("w_in")
        init = sem("init")
        bn_done = sem("bn_done"); mv_done = sem("mv_done")
        rstd_done = sem("rstd_done"); norm_done = sem("norm_done"); xb_done = sem("xb_done")
        tr_done = sem("tr_done"); xnT_done = sem("xnT_done")
        qkmm_done = sem("qkmm_done"); qk_done = sem("qk_done")
        r1_done = sem("r1_done"); q2_done = sem("q2_done"); q3_done = sem("q3_done")
        scr_out = sem("scr_out"); stack_in = sem("stack_in")
        vmm_done = sem("vmm_done"); v_done = sem("v_done")
        mx_ready = sem("mx_ready"); max_done = sem("max_done")
        tm_done = sem("tm_done"); m1_done = sem("m1_done"); m2_done = sem("m2_done")
        mrow_in = [sem(f"mrow_in{i}") for i in range(2)]
        s_ready = sem("s_ready"); exp_done = sem("exp_done"); pv_done = sem("pv_done")
        o_done = sem("o_done"); turn_done = sem("turn_done"); rden_done = sem("rden_done")
        on_done = sem("on_done"); ont_done = sem("ont_done"); oT_done = sem("oT_done"); pj_done = sem("pj_done"); x1_done = sem("x1_done")
        moe_in = sem("moe_in")
        f_bn = sem("f_bn"); f_mv = sem("f_mv"); f_rstd = sem("f_rstd"); f_norm = sem("f_norm")
        f_tr = sem("f_tr"); f_T = sem("f_T")
        lg_done = sem("lg_done"); xm_done = sem("xm_done"); px_done = sem("px_done")
        xr_done = sem("xr_done"); pt_done = sem("pt_done"); pT_done = sem("pT_done")
        xpv_done = sem("xpv_done"); x2_done = sem("x2_done")
        rt_mm = sem("rt_mm"); rt_d = sem("rt_d"); rt_e = sem("rt_e"); rt_step = sem("rt_step")
        cw_done = sem("cw_done"); rt_w = sem("rt_w")
        var_done = sem("var_done"); f_var = sem("f_var"); half_set = sem("half_set")
        h_ready = sem("h_ready"); relu_done = sem("relu_done")
        sq0_done = sem("sq0_done"); sq1_done = sem("sq1_done")
        y_ready = sem("y_ready"); y_done = sem("y_done")
        out_done = sem("out_done")

        def flags(b):
            if isinstance(b, int):
                return b >= 1, b + 1 < B, b + 2 < B
            return True, True, True

        def tile(b, t, n=1):
            return xs[:, bass.ds(b * TB + t, n), :]

        def apart(eng):
            eng.nop(nofuse=True)

        block = stack.enter_context(nc.Block())

        @block.sync
        def _(sp):
            for b in range(2):
                sp.dma_start(xs[:, b * TB:(b + 1) * TB, :], x[b].rearrange("(t p) d -> p t d", p=P)
                             ).then_inc(x_in[b], 16)
            for dst, src in (
                (ident[:], ident_d),
                (wqk[:], wqk_t), (bqks[:], bqk),
                (wv[:], wv_t),
                (wp[:], wp_t),
                (bvs[:], bv.partition_broadcast(P)), (bps[:], bp.partition_broadcast(P)),
                (rank[:], rank_d), (wr[:], wr_t),
                (ctxT[:], ctx_t),
            ):
                sp.dma_start(dst, src).then_inc(w_in, 16)
            for b in range(2, B):
                sp.dma_start(xs[:, b * TB:(b + 1) * TB, :], x[b].rearrange("(t p) d -> p t d", p=P)
                             ).then_inc(x_in[b], 16)

            def scratch_out(a, par, c):
                sp.wait_ge(q3_done, 4 * a + c + 1)
                apart(sp)
                if c == 0 and not (isinstance(a, int) and a < 2):
                    sp.wait_ge(stack_in, 16 * 2 * NS * (a - 1))
                apart(sp)
                sp.dma_start(scratch[par, :, c].rearrange("n p s -> p n s"), parts[:, :, c, :]
                             ).then_inc(scr_out, 16)

            def stack_load(a, par):
                sp.wait_ge(scr_out, 64 * (a + 1))
                apart(sp)
                if not (isinstance(a, int) and a < 2):
                    sp.wait_ge(s_ready, 64 * (a - 1))
                apart(sp)
                for n in range(NS):
                    for dst, part, c in ((QS, PARTS_Q[n], 0), (KS, PARTS_K[n], 2)):
                        src = scratch[par, part, c:c + 2].rearrange(
                            "c (h d) s -> d (c h) s", d=HD)
                        sp.dma_start(dst[par][n * HD:(n + 1) * HD, :, :], src
                                     ).then_inc(stack_in, 16)

            def max_rows(a, par, g):
                sp.wait_ge(m2_done, NG * a + g + 1)
                apart(sp)
                for n in range(2):
                    sp.dma_start(QS[par][KS_ROWS + n:KS_ROWS + n + 1, g * GH:(g + 1) * GH, :],
                                 mparts[:, g % 2, n, :]).then_inc(mrow_in[g % 2], 16)

            def batch(b, par):
                _, nxt, nxt2 = flags(b)
                if nxt:
                    stack_load(b + 1, 1 - par)
                max_rows(b, par, 1)
                max_rows(b, par, 2)
                if nxt2:
                    scratch_out(b + 2, par, 0)
                    scratch_out(b + 2, par, 1)
                max_rows(b, par, 3)
                if nxt2:
                    scratch_out(b + 2, par, 2)
                    scratch_out(b + 2, par, 3)
                if nxt:
                    max_rows(b + 1, 1 - par, 0)

            for c in range(4):
                scratch_out(0, 0, c)
            stack_load(0, 0)
            for c in range(4):
                scratch_out(1, 1, c)
            max_rows(0, 0, 0)
            batch(0, 0)
            with sp.Fori(0, 2) as i:
                for u in range(2):
                    batch(2 * i + 1 + u, (1 + u) % 2)
            batch(5, 1)
            sp.wait_ge(q3_done, 4 * B)
            sp.dma_start(ws1s, ws1_t).then_inc(moe_in, 16)
            sp.dma_start(ws2s, ws2_t).then_inc(moe_in, 16)
            sp.dma_start(ctxN[0:SC], ctx_n).then_inc(moe_in, 16)
            batch(6, 0)
            sp.wait_ge(s_ready, 64 * 7)
            sp.dma_start(w1s, w1_t).then_inc(moe_in, 16)
            sp.dma_start(w2s, w2_t).then_inc(moe_in, 16)
            batch(7, 1)
            with sp.Fori(0, B) as b:
                sp.wait_ge(y_done, NU * TB * (b + 1))
                apart(sp)
                sp.dma_start(out[bass.ds(b, 1)].rearrange("o (t p) d -> p (o t) d", p=P), tile(b, 0, TB)
                             ).then_inc(out_done, 16)
            sp.wait_ge(out_done, 16 * B)

        @block.tensor
        def _(pe):
            def misc_free(prev):
                if prev:
                    pe.wait_ge(prev[0], prev[1])

            def transposes(a, k, prev):
                pe.wait_ge(norm_done, TB * (a + 1))
                misc_free(prev)
                for t in range(TB):
                    mm = pe.transpose(bank[7][:, t * P:(t + 1) * P], xn[:, t, k * P:(k + 1) * P],
                                      ident[:])
                mm.then_inc(tr_done, 1)
                return xnT_done, KD * a + k + 1

            def project_qk(a, c, prev):
                pe.wait_ge(xnT_done, KD * (a + 1))
                misc_free(prev)
                for k in range(KD):
                    mm = pe.matmul(bank[7][:], wqk[:, k, c * P:(c + 1) * P], xnT[:, k, :],
                                   start=(k == 0), stop=(k == KD - 1))
                mm.then_inc(qkmm_done, 1)
                return qk_done, 8 * a + 2 * c + 2

            def project_v(a, i, prev):
                misc_free(prev)
                for t in range(2):
                    for k in range(KD):
                        mm = pe.matmul(bank[7][:, t * D:(t + 1) * D],
                                       xnT[:, k, (2 * i + t) * P:(2 * i + t + 1) * P],
                                       wv[:, k, :], start=(k == 0), stop=(k == KD - 1))
                mm.then_inc(vmm_done, 1)
                return v_done, 4 * a + 2 * i + 2

            def max_scores(a, par, m):
                if m == 0:
                    pe.wait_ge(stack_in, 16 * 2 * NS * (a + 1))
                for q in range(TB):
                    n = 4 * m + q
                    if not (isinstance(a, int) and a == 0 and n < 2):
                        pe.wait_ge(max_done, 64 * a + n - 1)
                    pe.matmul(bank[4 + n % 2][:], QS[par][0:KS_ROWS, m, q * P:(q + 1) * P],
                              KS[par][0:KS_ROWS, m, :], start=True, stop=True
                              ).then_inc(mx_ready, 1)
                    yield

            def turn_max(a, g, prev):
                pe.wait_ge(max_done, 64 * a + 16 * (g + 1))
                misc_free(prev)
                pe.transpose(bank[7][0:GH * TB, 0:P], mneg[:, g % 2, :], ident[:]
                             ).then_inc(tm_done, 1)
                return m2_done, NG * a + g + 1

            def turn_sums(b, g, prev):
                pe.wait_ge(o_done, NG * b + g + 1)
                misc_free(prev)
                for t in range(TB):
                    mm = pe.transpose(bank[7][:, t * P:(t + 1) * P], o_sb[:, t * P:(t + 1) * P],
                                      ident[:])
                mm.then_inc(turn_done, 1)
                return on_done, NG * b + g + 1

            def turn_heads(b, k, prev):
                pe.wait_ge(on_done, NG * (b + 1))
                misc_free(prev)
                for t in range(TB):
                    mm = pe.transpose(bank[7][:, t * P:(t + 1) * P],
                                      o_nat[:, t, k * P:(k + 1) * P], ident[:])
                mm.then_inc(ont_done, 1)
                return oT_done, KD * b + k + 1

            def project_out(b, i, prev):
                pe.wait_ge(oT_done, KD * (b + 1))
                misc_free(prev)
                for t in range(2):
                    for k in range(KD):
                        mm = pe.matmul(bank[7][:, t * D:(t + 1) * D],
                                       oT[:, k, (2 * i + t) * P:(2 * i + t + 1) * P],
                                       wp[:, k, :], start=(k == 0), stop=(k == KD - 1))
                mm.then_inc(pj_done, 1)
                return x1_done, 2 * b + i + 1

            def scores(b, par, s, j):
                g, kb = divmod(s, TB)
                if kb == 0 and j == 0:
                    pe.wait_ge(mrow_in[g % 2], 32 * (2 * b + g // 2 + 1))
                if not (isinstance(b, int) and b == 0 and s == 0):
                    pe.wait_ge(exp_done, 64 * b + 4 * s + j - 3)
                h = g * GH + j
                pe.matmul(bank[j][:], KS[par][0:KM_ROWS, h, kb * P:(kb + 1) * P],
                          QS[par][0:KM_ROWS, h, :], start=True, stop=True).then_inc(s_ready, 1)

            def values(b, par, s):
                g, kb = divmod(s, TB)
                pe.wait_ge(exp_done, 64 * b + 4 * s + 4)
                if s == 0:
                    pe.wait_ge(v_done, 4 * (b + 1))
                if kb == 0 and not (isinstance(b, int) and b == 0 and s == 0):
                    pe.wait_ge(o_done, NG * b + g)
                for j in range(GH):
                    mm = pe.matmul(bank[6][32 * j:32 * j + 32, :], VO[par][:, kb, g * GH + j, :],
                                   probs[:, kb % 2, j, :], start=(kb == 0), stop=(kb == TB - 1))
                mm.then_inc(pv_done, 1)

            def batch(b, par):
                prv, nxt, nxt2 = flags(b)
                prev = (on_done, NG * (b - 1) + 3) if prv else last
                for s in range(SLOTS):
                    m = s + AHEAD
                    ahead = iter(())
                    if m < SLOTS:
                        ahead = max_scores(b, par, m)
                    elif nxt:
                        ahead = max_scores(b + 1, 1 - par, m - SLOTS)
                    for j in range(GH):
                        scores(b, par, s, j)
                        next(ahead, None)
                    for _ in ahead:
                        pass
                    if nxt and s in (1, 2):
                        prev = project_v(b + 1, s - 1, prev)
                    if nxt2 and s in (3, 4):
                        prev = transposes(b + 2, s - 3, prev)
                    if nxt2 and 5 <= s < 9:
                        prev = project_qk(b + 2, s - 5, prev)
                    if s > 0:
                        values(b, par, s - 1)
                    elif prv:
                        values(b - 1, 1 - par, SLOTS - 1)
                    if s % 4 == 1:
                        g = s // 4 + 1
                        if g < NG:
                            prev = turn_max(b, g, prev)
                        elif nxt:
                            prev = turn_max(b + 1, 0, prev)
                    if s % 4 == 2:
                        if s > 2:
                            prev = turn_sums(b, s // 4 - 1, prev)
                        elif prv:
                            prev = turn_sums(b - 1, NG - 1, prev)
                    if prv and s in (3, 4):
                        prev = turn_heads(b - 1, s - 3, prev)
                    if prv and s in (7, 8):
                        prev = project_out(b - 1, s - 7, prev)

            pe.wait_ge(w_in, 16 * 10)
            prev = None
            for k in range(KD):
                prev = transposes(0, k, prev)
            for c in range(4):
                prev = project_qk(0, c, prev)
            for i in range(2):
                prev = project_v(0, i, prev)
            for k in range(KD):
                prev = transposes(1, k, prev)
            for c in range(4):
                prev = project_qk(1, c, prev)
            for m in range(AHEAD):
                for _ in max_scores(0, 0, m):
                    pass
                if m == 4:
                    prev = turn_max(0, 0, prev)
            last = prev
            batch(0, 0)
            with pe.Fori(0, 2) as i:
                for u in range(2):
                    batch(2 * i + 1 + u, (1 + u) % 2)
            for b in (5, 6, 7):
                batch(b, b % 2)
            prev = (on_done, NG * B - 1)
            values(B - 1, 1, SLOTS - 1)
            prev = turn_sums(B - 1, NG - 1, prev)
            for k in range(KD):
                prev = turn_heads(B - 1, k, prev)
            for i in range(2):
                prev = project_out(B - 1, i, prev)

            def front_transposes(a, r):
                pe.wait_ge(f_norm, TB * (2 * a + r + 1))
                if r == 0:
                    if not (isinstance(a, int) and a == 0):
                        pe.wait_ge(rt_d, a)
                    else:
                        pe.wait_ge(o_done, NG * B)
                        pe.wait_ge(x1_done, 2 * B)
                else:
                    pe.wait_ge(x2_done, TB * (a + 1))
                for k in range(KD):
                    for t in range(TB):
                        mm = pe.transpose(bank[6 + k][:, t * P:(t + 1) * P],
                                          xn[:, t, k * P:(k + 1) * P], ident[:])
                    mm.then_inc(f_tr, 1)

            def front_logits(a, ctxTb):
                pe.wait_ge(f_T, KD * (2 * a + 1))
                for t in range(TB):
                    for k in range(KD):
                        mm = pe.matmul(bank[6][:, t * SC:(t + 1) * SC],
                                       xnT[:, k, t * P:(t + 1) * P], ctxTb(k),
                                       start=(k == 0), stop=(k == KD - 1))
                mm.then_inc(lg_done, 1)

            def front_turn(a):
                pe.wait_ge(px_done, TB * (a + 1))
                apart(pe)
                for t in range(TB):
                    mm = pe.transpose(bank[7][0:SC, t * P:(t + 1) * P], px[:, t, :], ident[:])
                mm.then_inc(pt_done, 1)

            def front_values(a, ctxNb):
                pe.wait_ge(pT_done, a + 1)
                for t in range(TB):
                    mm = pe.matmul(bank[6 + t // 2][:, t % 2 * D:(t % 2 + 1) * D],
                                   pT[0:SC, t * P:(t + 1) * P], ctxNb, start=True, stop=True)
                    if t % 2:
                        mm.then_inc(xpv_done, 1)

            def front_router(a, par):
                pe.wait_ge(f_T, KD * (2 * a + 2))
                for t in range(TB):
                    for k in range(KD):
                        mm = pe.matmul(bank[6][:, t * E:(t + 1) * E],
                                       xrT[:, par, k, t * P:(t + 1) * P], wr[:, k, :],
                                       start=(k == 0), stop=(k == KD - 1))
                mm.then_inc(rt_mm, 1)

            def front(a, par, step):
                if step == 1:
                    front_transposes(a, 0)
                if step == 2:
                    front_logits(a, lambda k: ctxT[:, k, bass.ds(a, 1), :])
                if step == 3:
                    front_turn(a)
                if step == 4:
                    front_values(a, ctxN[0:SC, bass.ds(a, 1), :])
                if step == 6:
                    front_transposes(a, 1)
                if step == 7:
                    front_router(a, par)

            def up(b, par, u):
                if u == 0:
                    pe.wait_ge(f_T, KD * (2 * b + 2))
                for f in range(2):
                    n = 2 * u + f
                    if not (isinstance(b, int) and b == 0 and u < 2):
                        pe.wait_ge(sq0_done if f == 0 else sq1_done, NU * b + u - 1)
                    for k in range(KD):
                        w = (ws1s[:, k, (2 * u + f) * P:(2 * u + f + 1) * P] if u < 2
                             else w1s[:, u - 2, k, f * P:(f + 1) * P])
                        mm = pe.matmul(bank[n % 4][:], w, xrT[:, par, k, :],
                                       start=(k == 0), stop=(k == KD - 1))
                    mm.then_inc(h_ready, 1)

            def down(b, u):
                pe.wait_ge(sq0_done, NU * b + u + 1)
                pe.wait_ge(sq1_done, NU * b + u + 1)
                for i in range(2):
                    if not (isinstance(b, int) and b == 0 and u == 0):
                        pe.wait_ge(y_done, TB * (NU * b + u) - 2 + 2 * i)
                    for t in range(2):
                        for f in range(2):
                            w = ws2s[:, 2 * u + f, :] if u < 2 else w2s[:, u - 2, f, :]
                            mm = pe.matmul(bank[4 + i][:, t * D:(t + 1) * D],
                                           hT[:, u % 2, f, (2 * i + t) * P:(2 * i + t + 1) * P],
                                           w, start=(f == 0), stop=(f == 1))
                    mm.then_inc(y_ready, 1)

            def moe_block(b, par):
                nxt = flags(b)[1]
                for u in range(NU):
                    if u + 1 < NU:
                        up(b, par, u + 1)
                    elif nxt:
                        up(b + 1, 1 - par, 0)
                    down(b, u)
                    if nxt:
                        front(b + 1, 1 - par, u)

            pe.wait_ge(moe_in, 16 * 5)
            for step in range(8):
                front(0, 0, step)
            up(0, 0, 0)
            moe_block(0, 0)
            with pe.Fori(0, 3) as i:
                for u in range(2):
                    moe_block(2 * i + 1 + u, (1 + u) % 2)
            moe_block(7, 1)

        @block.scalar
        def _(act):
            def copy_xT(a, k):
                act.wait_ge(tr_done, KD * a + k + 1)
                if not (isinstance(a, int) and a == 0):
                    act.wait_ge(vmm_done, 2 * a)
                act.activation(xnT[:, k, :], bank[7][:], ACT.Copy).then_inc(xnT_done, 1)

            def copy_qk(a, c):
                act.wait_ge(qkmm_done, 4 * a + c + 1)
                if not (isinstance(a, int) and a == 0):
                    act.wait_ge(r1_done, 4 * (a - 1) + c + 1)
                    act.wait_ge(scr_out, 64 * a)
                act.activation(qk[:, c, :], bank[7][:], ACT.Identity, bias=bqks[:, c:c + 1]
                               ).then_inc(qk_done, 1)
                act.activation(parts[:, 0, c, :], bank[7][:], ACT.Identity, bias=bqks[:, c:c + 1]
                               ).then_inc(qk_done, 1)

            def second_part(a, c):
                act.wait_ge(r1_done, 4 * a + c + 1)
                act.activation(parts[:, 1, c, :], rest[:, c, :], ACT.Copy).then_inc(q2_done, 1)

            def copy_o(b, g):
                act.wait_ge(pv_done, SLOTS * b + TB * (g + 1))
                if not (isinstance(b, int) and b == 0 and g == 0):
                    act.wait_ge(turn_done, NG * b + g)
                act.activation(o_sb[:], bank[6][:], ACT.Copy).then_inc(o_done, 1)

            def copy_oT(b, k):
                act.wait_ge(ont_done, KD * b + k + 1)
                if not (isinstance(b, int) and b == 0):
                    act.wait_ge(pj_done, 2 * b)
                act.activation(oT[:, k, :], bank[7][:], ACT.Copy).then_inc(oT_done, 1)

            def batch(b, par):
                prv, nxt, nxt2 = flags(b)
                for s in range(SLOTS):
                    u = SLOTS * b + s
                    for j in range(GH):
                        act.wait_ge(s_ready, 64 * b + 4 * s + j + 1)
                        if j == 0 and not (isinstance(b, int) and b == 0 and s < 2):
                            act.wait_ge(pv_done, u - 1)
                        act.activation(probs[:, s % 2, j, :], bank[j][:], ACT.Exp,
                                       scale=HD ** -0.5).then_inc(exp_done, 1)
                    if nxt2 and s in (3, 4):
                        copy_xT(b + 2, s - 3)
                    if prv and s in (3, 4):
                        copy_oT(b - 1, s - 3)
                    if nxt2 and 5 <= s < 9:
                        copy_qk(b + 2, s - 5)
                    if nxt2 and 6 <= s < 10:
                        second_part(b + 2, s - 6)
                    if s % 4 == 0:
                        if s > 0:
                            copy_o(b, s // 4 - 1)
                        elif prv:
                            copy_o(b - 1, NG - 1)

            act.wait_ge(w_in, 16 * 10)
            for a in range(2):
                for k in range(KD):
                    copy_xT(a, k)
                for c in range(4):
                    copy_qk(a, c)
                for c in range(4):
                    second_part(a, c)
            batch(0, 0)
            with act.Fori(0, 2) as i:
                for u in range(2):
                    batch(2 * i + 1 + u, (1 + u) % 2)
            for b in (5, 6, 7):
                batch(b, b % 2)
            copy_o(B - 1, NG - 1)
            for k in range(KD):
                copy_oT(B - 1, k)

            def front(a, par, step):
                if step == 1:
                    if not (isinstance(a, int) and a == 0):
                        act.wait_ge(lg_done, a)
                    for k in range(KD):
                        act.wait_ge(f_tr, KD * 2 * a + k + 1)
                        act.activation(xnT[:, k, :], bank[6 + k][:], ACT.Copy).then_inc(f_T, 1)
                if step == 2:
                    act.wait_ge(xm_done, 2 * a + 2)
                    if not (isinstance(a, int) and a == 0):
                        act.wait_ge(pt_done, a)
                        act.wait_ge(xr_done, a)
                    for t in range(TB):
                        act.activation(px[:, t, :], bank[6][:, t * SC:(t + 1) * SC], ACT.Exp,
                                       bias=xb[:, t:t + 1], scale=D ** -0.5,
                                       accum_out=xsum[:, t:t + 1]).then_inc(px_done, 1)
                if step == 3:
                    act.wait_ge(pt_done, a + 1)
                    if not (isinstance(a, int) and a == 0):
                        act.wait_ge(xpv_done, 2 * a)
                    act.activation(pT[0:SC, :], bank[7][0:SC, :], ACT.Copy).then_inc(pT_done, 1)
                if step == 6:
                    for k in range(KD):
                        act.wait_ge(f_tr, KD * (2 * a + 1) + k + 1)
                        if not (isinstance(a, int) and a < 2):
                            act.wait_ge(h_ready, 2 * NU * (a - 1))
                            act.wait_ge(rt_mm, a - 1)
                        act.activation(xrT[:, par, k, :], bank[6 + k][:], ACT.Copy
                                       ).then_inc(f_T, 1)
                if step == 7:
                    act.wait_ge(rt_d, a + 1)
                    if not (isinstance(a, int) and a == 0):
                        act.wait_ge(cw_done, a)
                    act.activation(rt["e"][:], rt["d"][:], ACT.Exp).then_inc(rt_e, 1)

            def relus(b, u):
                for f in range(2):
                    n = 2 * u + f
                    act.wait_ge(h_ready, 2 * NU * b + n + 1)
                    if not (isinstance(b, int) and b == 0 and u < 2):
                        act.wait_ge(sq0_done if f == 0 else sq1_done, NU * b + u - 1)
                    act.activation(relu[:, n % 4, :], bank[n % 4][:], ACT.Relu
                                   ).then_inc(relu_done, 1)

            def moe_block(b, par):
                nxt = flags(b)[1]
                for u in range(NU):
                    if u + 1 < NU:
                        relus(b, u + 1)
                    elif nxt:
                        relus(b + 1, 0)
                    if nxt:
                        front(b + 1, 1 - par, u)

            for step in range(8):
                front(0, 0, step)
            relus(0, 0)
            moe_block(0, 0)
            with act.Fori(0, 3) as i:
                for u in range(2):
                    moe_block(2 * i + 1 + u, (1 + u) % 2)
            moe_block(7, 1)

        @block.vector
        def _(dve):
            def stats(a, first):
                if first:
                    dve.wait_ge(x_in[a], 16)
                if not (isinstance(a, int) and a == 0):
                    dve.wait_ge(mv_done, TB * a)
                apart(dve)
                for t in range(TB):
                    dve.bn_stats(st[:, t, :], tile(a, t)[:, 0]).then_inc(bn_done, 1)
                if not (isinstance(a, int) and a == 0):
                    dve.wait_ge(norm_done, TB * a)
                dve.wait_ge(bn_done, TB * (a + 1))
                apart(dve)
                for t in range(TB):
                    dve.bn_aggr(mv[:, t, :], st[:, t, :]).then_inc(mv_done, 1)
                dve.wait_ge(mv_done, TB * (a + 1))
                if not (isinstance(a, int) and a == 0):
                    dve.wait_ge(rstd_done, a)
                dve.tensor_scalar(var[:], mv[:, :, 1], EPS, None, ALU.add).then_inc(var_done, 1)

            def norm(a):
                dve.wait_ge(rstd_done, a + 1)
                if not (isinstance(a, int) and a == 0):
                    dve.wait_ge(tr_done, KD * a)
                for t in range(TB):
                    dve.tensor_scalar(xn[:, t, :], tile(a, t)[:, 0], mv[:, t, 0:1],
                                      rstd[:, t:t + 1], ALU.subtract, ALU.mult
                                      ).then_inc(norm_done, 1)

            def copy_v(a, par, i):
                dve.wait_ge(vmm_done, 2 * a + i + 1)
                if i == 0 and not (isinstance(a, int) and a < 2):
                    dve.wait_ge(pv_done, SLOTS * (a - 1))
                for t in range(2):
                    dve.tensor_tensor(
                        VO[par][:, 2 * i + t, :, 1:1 + HD],
                        bank[7][:, t * D:(t + 1) * D].rearrange("p (h d) -> p h d", d=HD),
                        bvs[:].rearrange("p (h d) -> p h d", d=HD), ALU.add
                    ).then_inc(v_done, 1)

            def maxima(a, m):
                g = m // GH
                for q in range(TB):
                    n = 4 * m + q
                    dve.wait_ge(mx_ready, 64 * a + n + 1)
                    if m % GH == 0 and q == 0 and not (isinstance(a, int) and a == 0 and g < 2):
                        dve.wait_ge(tm_done, NG * a + g - 1)
                    dve.tensor_reduce(mneg[:, g % 2, m % GH * TB + q:m % GH * TB + q + 1],
                                      bank[4 + n % 2][:], AX.X, ALU.max, negate=True
                                      ).then_inc(max_done, 1)

            def split_max(a, g):
                G = NG * a + g
                dve.wait_ge(tm_done, G + 1)
                if not (isinstance(a, int) and a == 0 and g < 2):
                    dve.wait_ge(mrow_in[g % 2], 32 * (2 * a + g // 2))
                dve.tensor_copy(mparts[:, g % 2, 0, :], bank[7][0:GH * TB, 0:P]
                                ).then_inc(m1_done, 1)
                dve.wait_ge(m1_done, G + 1)
                dve.tensor_tensor(mparts[:, g % 2, 1, :], bank[7][0:GH * TB, 0:P],
                                  mparts[:, g % 2, 0, :], ALU.subtract).then_inc(m2_done, 1)

            def normalise(b, g):
                G = NG * b + g
                dve.wait_ge(turn_done, G + 1)
                if not (isinstance(b, int) and b == 0 and g == 0):
                    dve.wait_ge(on_done, G)
                sums = bank[7][:].rearrange("p (t j c) -> p t j c", t=TB, j=GH)
                dve.reciprocal(rden[:], sums[:, :, :, 0]).then_inc(rden_done, 1)
                dve.wait_ge(rden_done, G + 1)
                if g == 0 and not (isinstance(b, int) and b == 0):
                    dve.wait_ge(ont_done, KD * b)
                dve.tensor_tensor(
                    o_nat[:, :, g * GH * HD:(g + 1) * GH * HD].rearrange(
                        "p t (j d) -> p t j d", j=GH),
                    sums[:, :, :, 1:1 + HD],
                    rden[:].unsqueeze(3).to_broadcast([P, TB, GH, HD]), ALU.mult
                ).then_inc(on_done, 1)

            def add_out(b, i):
                dve.wait_ge(pj_done, 2 * b + i + 1)
                dve.wait_ge(xb_done, TB * (b + 1))
                t = tile(b, 2 * i, 2)
                dve.tensor_tensor(t, bank[7][:].rearrange("p (t d) -> p t d", t=2), t, ALU.add
                                  ).then_inc(x1_done, 1)

            def batch(b, par):
                prv, nxt, nxt2 = flags(b)
                for s in range(SLOTS):
                    m = s + AHEAD
                    if m < SLOTS:
                        maxima(b, m)
                    elif nxt:
                        maxima(b + 1, m - SLOTS)
                    if nxt2 and s == 0:
                        stats(b + 2, False)
                    if nxt2 and s == 1:
                        norm(b + 2)
                    if nxt and s in (1, 2):
                        copy_v(b + 1, 1 - par, s - 1)
                    if s % 4 == 1:
                        if s // 4 + 1 < NG:
                            split_max(b, s // 4 + 1)
                        elif nxt:
                            split_max(b + 1, 0)
                    if s % 4 == 2:
                        if s > 2:
                            normalise(b, s // 4 - 1)
                        elif prv:
                            normalise(b - 1, NG - 1)
                    if prv and s in (7, 8):
                        add_out(b - 1, s - 7)

            for i in range(2):
                dve.memset(KS[i][KS_ROWS:KM_ROWS], 1.0).then_inc(init, 1)
            for i in range(2):
                dve.memset(VO[i][:], 0.0).then_inc(init, 1)
            dve.wait_ge(init, 4)
            for i in range(2):
                dve.memset(VO[i][:, :, :, 0:1], 1.0).then_inc(init, 1)
            stats(0, True)
            norm(0)
            stats(1, True)
            norm(1)
            dve.wait_ge(w_in, 16 * 10)
            dve.wait_ge(init, 6)
            for i in range(2):
                copy_v(0, 0, i)
            for b in range(2, B):
                dve.wait_ge(x_in[b], 16)
            for m in range(AHEAD):
                maxima(0, m)
                if m == 4:
                    split_max(0, 0)
            batch(0, 0)
            with dve.Fori(0, 2) as i:
                for u in range(2):
                    batch(2 * i + 1 + u, (1 + u) % 2)
            for b in (5, 6, 7):
                batch(b, b % 2)
            normalise(B - 1, NG - 1)
            for i in range(2):
                add_out(B - 1, i)

            def row_stats(a, r):
                n = 2 * a + r
                if not (isinstance(a, int) and a == 0 and r == 0):
                    dve.wait_ge(f_mv, TB * n)
                    dve.wait_ge(f_norm, TB * n)
                else:
                    dve.wait_ge(mv_done, TB * B)
                    dve.wait_ge(norm_done, TB * B)
                    dve.wait_ge(x1_done, 2 * B)
                if r == 1:
                    dve.wait_ge(x2_done, TB * (a + 1))
                apart(dve)
                for t in range(TB):
                    dve.bn_stats(st[:, t, :], tile(a, t)[:, 0]).then_inc(f_bn, 1)
                dve.wait_ge(f_bn, TB * (n + 1))
                apart(dve)
                for t in range(TB):
                    dve.bn_aggr(mv[:, t, :], st[:, t, :]).then_inc(f_mv, 1)
                dve.wait_ge(f_mv, TB * (n + 1))
                if not (isinstance(a, int) and a == 0 and r == 0):
                    dve.wait_ge(f_rstd, n)
                else:
                    dve.wait_ge(rstd_done, B)
                dve.tensor_scalar(var[:], mv[:, :, 1], EPS, None, ALU.add).then_inc(f_var, 1)

            def row_norm(a, r):
                n = 2 * a + r
                dve.wait_ge(f_rstd, n + 1)
                if not (isinstance(a, int) and a == 0 and r == 0):
                    dve.wait_ge(f_tr, KD * n)
                else:
                    dve.wait_ge(tr_done, KD * B)
                for t in range(TB):
                    dve.tensor_scalar(xn[:, t, :], tile(a, t)[:, 0], mv[:, t, 0:1],
                                      rstd[:, t:t + 1], ALU.subtract, ALU.mult
                                      ).then_inc(f_norm, 1)

            NR = 15

            def route(a, par):
                def wide(v):
                    return v[:].unsqueeze(2).to_broadcast([P, TB, E])

                count = [NR * a]

                def step(ins):
                    ins.then_inc(rt_step, 1)
                    count[0] = count[0] + 1
                    dve.wait_ge(rt_step, count[0])

                dve.wait_ge(rt_mm, a + 1)
                logits = bank[6][:, 0:TB * E].rearrange("p (t e) -> p t e", e=E)
                step(dve.tensor_reduce(rc["m"][:], logits, AX.X, ALU.max))
                if not (isinstance(a, int) and a == 0):
                    dve.wait_ge(rt_e, a)
                dve.tensor_tensor(rt["d"][:], logits, wide(rc["m"]), ALU.subtract
                                  ).then_inc(rt_d, 1)
                dve.wait_ge(rt_e, a + 1)
                e = rt["e"]
                for i, src in (("1", e), ("2", rt["e2"])):
                    if i == "2":
                        step(dve.scalar_tensor_tensor(out=rt["e2"][:], in0=rt["oh1"][:],
                                                      scalar=-2.0, in1=e[:], op0=ALU.mult,
                                                      op1=ALU.add))
                    step(dve.tensor_reduce(rc["m" + i][:], src[:], AX.X, ALU.max))
                    step(dve.tensor_tensor(rt["eq" + i][:], src[:], wide(rc["m" + i]),
                                           ALU.is_equal))
                    step(dve.tensor_tensor(rt["s" + i][:], rt["eq" + i][:], rank[:], ALU.mult))
                    step(dve.tensor_reduce(rc["sm" + i][:], rt["s" + i][:], AX.X, ALU.max))
                    step(dve.tensor_tensor(rt["oh" + i][:], rt["s" + i][:],
                                           wide(rc["sm" + i]), ALU.is_equal))
                step(dve.tensor_tensor(rt["oh"][:], rt["oh1"][:], rt["oh2"][:], ALU.add))
                step(dve.tensor_tensor(rc["den"][:], rc["m1"][:], rc["m2"][:], ALU.add))
                step(dve.reciprocal(rc["r"][:], rc["den"][:]))
                assert isinstance(a, int) is False or count[0] == NR * a + NR
                if not (isinstance(a, int) and a == 0):
                    dve.wait_ge(cw_done, a)
                dve.tensor_tensor(rt["w"][:], rt["oh"][:], e[:], ALU.mult).then_inc(rt_w, 1)
                dve.wait_ge(rt_w, a + 1)
                dve.tensor_tensor(cw[:, par], rt["w"][:], wide(rc["r"]), ALU.mult
                                  ).then_inc(cw_done, 1)

            def front(a, par, step):
                if step == 0:
                    row_stats(a, 0)
                if step == 2:
                    dve.wait_ge(lg_done, a + 1)
                    if not (isinstance(a, int) and a == 0):
                        dve.wait_ge(px_done, TB * a)
                    dve.tensor_reduce(xm[:], bank[6][:, 0:TB * SC].rearrange("p (t s) -> p t s",
                                      s=SC), AX.X, ALU.max).then_inc(xm_done, 1)
                    dve.wait_ge(xm_done, 2 * a + 1)
                    dve.tensor_scalar(xb[:], xm[:], -(D ** -0.5), None, ALU.mult
                                      ).then_inc(xm_done, 1)
                if step == 3:
                    dve.wait_ge(px_done, TB * (a + 1))
                    if not (isinstance(a, int) and a == 0):
                        dve.wait_ge(x2_done, TB * a)
                    dve.reciprocal(xr[:], xsum[:]).then_inc(xr_done, 1)
                if step == 4:
                    dve.wait_ge(xr_done, a + 1)
                    for t in range(TB):
                        dve.wait_ge(xpv_done, 2 * a + t // 2 + 1)
                        xt = tile(a, t)[:, 0]
                        dve.scalar_tensor_tensor(
                            out=xt, in0=bank[6 + t // 2][:, t % 2 * D:(t % 2 + 1) * D],
                            scalar=xr[:, t:t + 1], in1=xt, op0=ALU.mult, op1=ALU.add
                        ).then_inc(x2_done, 1)
                if step == 5:
                    row_stats(a, 1)
                if step == 7:
                    route(a, par)

            def square(b, u):
                dve.wait_ge(relu_done, 2 * NU * b + 2 * u + 2)
                if not (isinstance(b, int) and b == 0 and u < 2):
                    dve.wait_ge(y_ready, 2 * (NU * b + u - 1))
                n = 2 * u + 1
                dve.tensor_tensor(hT[:, u % 2, 1, :], relu[:, n % 4, :], relu[:, n % 4, :],
                                  ALU.mult).then_inc(sq1_done, 1)

            def add_rows(b, par, u):
                for t in range(TB):
                    dve.wait_ge(y_ready, 2 * (NU * b + u) + t // 2 + 1)
                    if u > 0:
                        dve.wait_ge(y_done, TB * (NU * b + u - 1) + t + 1)
                    xt = tile(b, t)[:, 0]
                    y = bank[4 + t // 2][:, t % 2 * D:(t % 2 + 1) * D]
                    if u < 2:
                        ins = dve.tensor_tensor(xt, y, xt, ALU.add)
                    else:
                        if u == 2 and t == 0:
                            dve.wait_ge(cw_done, b + 1)
                        ins = dve.scalar_tensor_tensor(
                            out=xt, in0=y, scalar=cw[:, par, t, u - 2:u - 1], in1=xt,
                            op0=ALU.mult, op1=ALU.add)
                    ins.then_inc(y_done, 1)

            def moe_block(b, par):
                nxt = flags(b)[1]
                for u in range(NU):
                    if nxt and u in (1, 6):
                        row_norm(b + 1, u // 6)
                    if u + 1 < NU:
                        square(b, u + 1)
                    elif nxt:
                        square(b + 1, 0)
                    add_rows(b, par, u)
                    if nxt:
                        front(b + 1, 1 - par, u)

            for step in range(8):
                if step in (1, 6):
                    row_norm(0, step // 6)
                front(0, 0, step)
            square(0, 0)
            moe_block(0, 0)
            with dve.Fori(0, 3) as i:
                for u in range(2):
                    moe_block(2 * i + 1 + u, (1 + u) % 2)
            moe_block(7, 1)

        @block.gpsimd
        def _(pool):
            def inverse_std(a):
                pool.wait_ge(var_done, a + 1)
                if not (isinstance(a, int) and a == 0):
                    pool.wait_ge(norm_done, TB * a)
                pool.tensor_tensor(rstd[:], var[:], minus_half[:], ALU.pow
                                   ).then_inc(rstd_done, 1)

            def add_bias(a):
                pool.wait_ge(norm_done, TB * (a + 1))
                apart(pool)
                for t in range(TB):
                    xt = tile(a, t)[:, 0]
                    pool.tensor_tensor(xt, xt, bps[:], ALU.add).then_inc(xb_done, 1)

            def first_rest(a, c):
                pool.wait_ge(qk_done, 8 * a + 2 * c + 2)
                if not (isinstance(a, int) and a == 0):
                    pool.wait_ge(q3_done, 4 * (a - 1) + c + 1)
                    pool.wait_ge(q2_done, 4 * (a - 1) + c + 1)
                pool.tensor_tensor(rest[:, c, :], qk[:, c, :], parts[:, 0, c, :], ALU.subtract
                                   ).then_inc(r1_done, 1)

            def third_part(a, c):
                pool.wait_ge(q2_done, 4 * a + c + 1)
                pool.tensor_tensor(parts[:, 2, c, :], rest[:, c, :], parts[:, 1, c, :],
                                   ALU.subtract).then_inc(q3_done, 1)

            def batch(b, par):
                prv, nxt, nxt2 = flags(b)
                for s in range(SLOTS):
                    if nxt2 and s == 0:
                        inverse_std(b + 2)
                    if nxt2 and s == 2:
                        add_bias(b + 2)
                    if nxt2 and 5 <= s < 9:
                        first_rest(b + 2, s - 5)
                    if nxt2 and 6 <= s < 10:
                        third_part(b + 2, s - 6)

            pool.memset(minus_half[:], -0.5).then_inc(half_set, 1)
            pool.wait_ge(half_set, 1)
            pool.wait_ge(w_in, 16 * 10)
            inverse_std(0)
            add_bias(0)
            for c in range(4):
                first_rest(0, c)
            for c in range(4):
                third_part(0, c)
            inverse_std(1)
            add_bias(1)
            for c in range(4):
                first_rest(1, c)
            for c in range(4):
                third_part(1, c)
            batch(0, 0)
            with pool.Fori(0, 2) as i:
                for u in range(2):
                    batch(2 * i + 1 + u, (1 + u) % 2)
            for b in (5, 6, 7):
                batch(b, b % 2)

            def row_inverse_std(a, r):
                n = 2 * a + r
                pool.wait_ge(f_var, n + 1)
                if not (isinstance(a, int) and a == 0 and r == 0):
                    pool.wait_ge(f_norm, TB * n)
                else:
                    pool.wait_ge(norm_done, TB * B)
                pool.tensor_tensor(rstd[:], var[:], minus_half[:], ALU.pow
                                   ).then_inc(f_rstd, 1)

            def square(b, u):
                pool.wait_ge(relu_done, 2 * NU * b + 2 * u + 1)
                if not (isinstance(b, int) and b == 0 and u < 2):
                    pool.wait_ge(y_ready, 2 * (NU * b + u - 1))
                n = 2 * u
                pool.tensor_tensor(hT[:, u % 2, 0, :], relu[:, n % 4, :], relu[:, n % 4, :],
                                   ALU.mult).then_inc(sq0_done, 1)

            def moe_block(b, par):
                nxt = flags(b)[1]
                for u in range(NU):
                    if u + 1 < NU:
                        square(b, u + 1)
                    elif nxt:
                        square(b + 1, 0)
                    if nxt and u == 0:
                        row_inverse_std(b + 1, 0)
                    if nxt and u == 5:
                        row_inverse_std(b + 1, 1)

            row_inverse_std(0, 0)
            row_inverse_std(0, 1)
            square(0, 0)
            moe_block(0, 0)
            with pool.Fori(0, 3) as i:
                for u in range(2):
                    moe_block(2 * i + 1 + u, (1 + u) % 2)
            moe_block(7, 1)


def kernel(x, ctx_1024, L0_attn_qkv_w, L0_attn_qkv_b, L0_attn_proj_w, L0_attn_proj_b,
           L0_ffn_w_router, L0_ffn_w1_stack, L0_ffn_w2_stack, L0_ffn_ws1, L0_ffn_ws2):
    import numpy as np
    import concourse.bacc as bacc
    from concourse.bass_utils import run_bass_kernel_spmd

    qkv_w, proj_w = np.asarray(L0_attn_qkv_w), np.asarray(L0_attn_proj_w)
    qkv_b = np.asarray(L0_attn_qkv_b)
    rank = np.broadcast_to(np.arange(E, 0, -1, dtype=np.float32), (P, TB, E))

    def chunks(w):
        w = np.asarray(w)
        w = w.reshape(*w.shape[:-2], w.shape[-2] // P, P, w.shape[-1])
        return np.moveaxis(w, -2, 0)

    def turned(w):
        return np.swapaxes(np.asarray(w), -1, -2)

    ctx = np.asarray(ctx_1024)
    ins = {
        "x": np.asarray(x), "ctx_n": ctx.transpose(1, 0, 2),
        "ctx_t": chunks(turned(ctx)).transpose(0, 2, 1, 3),
        "wqk_t": chunks(qkv_w[:2 * D].T), "bqk": qkv_b[:2 * D].reshape(4, P).T,
        "wv_t": chunks(qkv_w[2 * D:].T), "bv": qkv_b[2 * D:],
        "wp_t": chunks(proj_w.T), "bp": np.asarray(L0_attn_proj_b),
        "wr_t": chunks(turned(L0_ffn_w_router)),
        "w1_t": chunks(turned(L0_ffn_w1_stack)), "w2_t": chunks(turned(L0_ffn_w2_stack)),
        "ws1_t": chunks(turned(L0_ffn_ws1)), "ws2_t": chunks(turned(L0_ffn_ws2)),
        "ident": np.eye(P, dtype=np.float32), "rank": rank,
    }
    ins = {"in_" + n: np.ascontiguousarray(a) for n, a in ins.items()}
    nc = bacc.Bacc("TRN2", target_bir_lowering=False, num_devices=1)
    args = [nc.dram_tensor(n, a.shape, F32, kind="ExternalInput").ap() for n, a in ins.items()]
    out = nc.dram_tensor("out", (B, S, D), F32, kind="ExternalOutput").ap()
    decoder_layer(nc, *args, out)
    r = run_bass_kernel_spmd(nc, [ins], core_ids=[0])
    return r.results[0]["out"]
```

```python
from contextlib import ExitStack

import concourse.bass as bass
from concourse import mybir

F32 = mybir.dt.float32
BF16 = mybir.dt.bfloat16
F32R = mybir.dt.float32r
I32 = mybir.dt.int32
ALU = mybir.AluOpType
ACT = mybir.ActivationFunctionType
AX = mybir.AxisListType

B, S, D = 8, 512, 256
H, HD = 16, 16
P = 128
TB = S // P
KD = D // P
GH = 4
NG = H // GH
SLOTS = NG * TB
AHEAD = 7
PARTS_Q = (0, 0, 0, 1, 1, 2)
PARTS_K = (0, 1, 2, 0, 1, 0)
NS = len(PARTS_Q)
KS_ROWS = NS * HD
KM_ROWS = KS_ROWS + 2
SC = 64
E, F = 8, 256
FS = 512
NFS = FS // P
ROOM = B * S + P
TILES = B * S * 2 // P + E
RING = 4
ROUTE_STEPS = 18
HB = S // 2
EPS = 1e-5


C_FIRST = TB * E
C_FIRSTP = C_FIRST + E
C_STEPS = C_FIRSTP + E
C_UPTO = C_STEPS + B * TB
NCONST = C_UPTO + E * E


def decoder_layer(nc, x, ctx_n, ctx_t, wqk_t, bqk, wv_t, bv, wp_t, bp, wr_t, w1_t, w2_t, ws1_t,
                  ws2_t, ident_d, tri_d, const_d, table_d, out):
    scratch = nc.dram_tensor("qk_parts", [2, 3, 4, P, S], BF16).ap()
    x_rows = nc.dram_tensor("x_rows", [E * ROOM, D], F32).ap()
    y_rows = nc.dram_tensor("y_rows", [TILES * P, D], F32).ap()
    x_turned = nc.dram_tensor("x_turned", [B, P, KD, S], F32).ap()
    with ExitStack() as stack:
        def sem(name):
            return stack.enter_context(nc.semaphore(name))

        bank = [stack.enter_context(nc.psum_tensor(f"bank{i}", [P, 512], F32)) for i in range(8)]

        mid, end = bank[3], bank[7]
        NSB = 3

        def sb(name, shape, dt=F32):
            return stack.enter_context(nc.sbuf_tensor(name, shape, dt))

        xs = sb("xs", [P, B * TB, D])
        ident = sb("ident", [P, P])
        tri = sb("tri", [P, 2, P], BF16)
        const = sb("const", [P, NCONST])
        rank = const[:, 0:TB * E].rearrange("p (t e) -> p t e", e=E)
        first = const[:, C_FIRST:C_FIRST + E]
        first_p = const[:, C_FIRSTP:C_FIRSTP + E]
        steps = const[:, C_STEPS:C_STEPS + B * TB]
        upto = const[:, C_UPTO:C_UPTO + E * E].rearrange("p (a b) -> p a b", b=E)
        chosen = sb("chosen", [P, 2, B * TB, E])
        place = sb("place", [P, 2, B * TB])
        weight = sb("weight", [P, 2, B * TB])
        next_row = sb("next_row", [P, E])
        minus_half = sb("minus_half", [P, TB])
        px = sb("px", [P, TB, SC])
        xm = sb("xm", [P, TB])
        xb = sb("xb", [P, TB])
        xsum = sb("xsum", [P, TB])
        xr = sb("xr", [P, TB])
        rt = {n: sb("rt_" + n, [P, TB, E]) for n in
              ("d", "e", "eq1", "s1", "oh1", "e2", "eq2", "s2", "oh2", "row", "p1", "p2")}
        rc = {n: sb("rc_" + n, [P, TB]) for n in ("m", "m1", "sm1", "m2", "sm2", "den", "r")}
        oh = sb("oh", [P, TB, E], BF16)
        rows_i = sb("rows_i", [P, 2, TB], I32)
        zero_i = sb("zero_i", [P, E], I32)
        zeros = sb("zeros", [P, D])
        st = [sb(f"st{i}", [P, TB, 6]) for i in range(2)]
        mv = [sb(f"mv{i}", [P, TB, 2]) for i in range(2)]
        var = [sb(f"var{i}", [P, TB]) for i in range(2)]
        rstd = [sb(f"rstd{i}", [P, TB]) for i in range(2)]
        expert_i = sb("expert_i", [1, TILES], I32)
        row_i = sb("row_i", [1, TILES], I32)
        result_i = sb("result_i", [P, 2, B * TB], I32)
        result_now = sb("result_now", [P, 2, TB], I32)
        tiles = sb("tiles", [P, E])
        incl = sb("incl", [P, E])
        excl = sb("excl", [P, E])
        shift = sb("shift", [P, E])
        counted = sb("counted", [P, E])

        with ExitStack() as phase:
            def sb1(name, shape, dt=F32):
                return phase.enter_context(nc.sbuf_tensor(name, shape, dt))

            QS, KS = [None] * 2, [None] * 2
            for i in range(2):
                QS[i] = sb1(f"QS{i}", [P, H, S], BF16)
                KS[i] = sb1(f"KS{i}", [P, H, S], BF16)
            VO = [sb1(f"VO{i}", [P, TB, H, 32]) for i in range(2)]
            probs = sb1("probs", [P, 2, GH, S])
            qk = sb1("qk", [P, 2, S])
            rest = sb1("rest", [P, 2, S])
            parts = sb1("parts", [P, 3, 4, S], BF16)
            xn = [sb1(f"xn{i}", [P, TB, D]) for i in range(3)]
            xnT = [sb1(f"xnT{i}", [P, KD, S]) for i in range(2)]
            xrT = sb1("xrT", [P, KD, S])
            wqk = sb1("wqk", [P, KD, 2 * D])
            bqks = sb1("bqks", [P, 4])
            wv = sb1("wv", [P, KD, D])
            bvs = sb1("bvs", [P, D])
            wp = sb1("wp", [P, KD, D])
            bps = sb1("bps", [P, D])
            mneg = sb1("mneg", [P, 2, GH * TB])
            mparts = sb1("mparts", [GH * TB, 2, 2, P], BF16)
            o_sb = sb1("o_sb", [P, S])
            rden = sb1("rden", [P, TB, GH])
            o_nat = sb1("o_nat", [P, TB, D])
            oT = sb1("oT", [P, KD, S])
            pT = sb1("pT", [P, S])
            ctxT = sb1("ctxT", [P, KD, SC])
            ctxN = sb1("ctxN", [SC, D])
            wr = sb1("wr", [P, KD, E])
            tri_f = sb1("tri_f", [P, 2, P])
        raws = ExitStack()
        w1raw = raws.enter_context(nc.sbuf_tensor("w1raw", [P, E, KD, F], F32))
        w2raw = raws.enter_context(nc.sbuf_tensor("w2raw", [P, E, KD, F], F32))
        raws.close()
        ws1 = [sb(f"ws1_{i}", [P, KD, FS], F32R) for i in range(2)]
        ws2 = [sb(f"ws2_{i}", [P, NFS, D], F32R) for i in range(2)]
        hs = [sb(f"hs{i}", [P, 2, NFS, HB], F32R) for i in range(2)]
        w1 = [sb(f"w1_{i}", [P, E, KD, F], F32R) for i in range(2)]
        w2 = [sb(f"w2_{i}", [P, E, KD, F], F32R) for i in range(2)]
        wsraw = sb("wsraw", [P, 2, 2 * FS])
        got = sb("got", [P, RING, 2, D])
        xt = sb("xt", [P, RING, D])
        yt = sb("yt", [P, RING, D])
        xT2 = [sb(f"xT2_{i}", [P, 2, KD, P], F32R) for i in range(2)]
        relu_t = sb("relu_t", [P, 2, F])
        sq_t = sb("sq_t", [P, 2, F])
        hT2 = [sb(f"hT2_{i}", [P, 2, F // P, P], F32R) for i in range(2)]
        xs3 = sb("xs3", [P, 2, KD, HB])
        xs2 = [sb(f"xs2_{i}", [P, 2, KD, HB], F32R) for i in range(2)]
        relu_s = sb("relu_s", [P, NFS, HB])
        sq_s = sb("sq_s", [P, NFS, HB])
        fin_a = sb("fin_a", [P, B * TB, E])
        fin_b = sb("fin_b", [P, B * TB, E])
        fin_c = sb("fin_c", [P, 2, B * TB])
        tab_t = sb("tab_t", [1, TILES])
        tab_a = sb("tab_a", [1, TILES, E])
        tab_b = sb("tab_b", [1, TILES, E])
        tab_c = sb("tab_c", [1, 2, TILES])
        tab_0 = sb("tab_0", [1, TILES])
        tab_n = sb("tab_n", [1, 2])

        x_in = [sem(f"x_in{i}") for i in range(B)]
        w_in = sem("w_in")
        init = sem("init")
        bn_done = sem("bn_done"); mv_done = sem("mv_done")
        rstd_done = sem("rstd_done"); norm_done = sem("norm_done"); xb_done = sem("xb_done")
        tr_done = sem("tr_done"); xnT_done = sem("xnT_done")
        qkmm_done = sem("qkmm_done"); qk_done = sem("qk_done"); q1_done = sem("q1_done")
        r1_done = sem("r1_done"); q2_done = sem("q2_done"); q3_done = sem("q3_done")
        scr_out = sem("scr_out"); stack_in = sem("stack_in")
        vmm_done = sem("vmm_done"); v_done = sem("v_done")
        mx_ready = sem("mx_ready"); max_done = sem("max_done")
        tm_done = sem("tm_done"); m1_done = sem("m1_done"); m2_done = sem("m2_done")
        mrow_in = [sem(f"mrow_in{i}") for i in range(2)]
        s_ready = sem("s_ready"); exp_done = sem("exp_done"); pv_done = sem("pv_done")
        o_done = sem("o_done"); turn_done = sem("turn_done"); rden_done = sem("rden_done")
        on_done = sem("on_done"); ont_done = sem("ont_done"); oT_done = sem("oT_done"); pj_done = sem("pj_done"); x1_done = sem("x1_done")
        tri_set = sem("tri_set"); half_set = sem("half_set"); zeros_set = sem("zeros_set")
        var_done = sem("var_done")
        ctx_in = sem("ctx_in")
        f_bn = sem("f_bn"); f_mv = sem("f_mv"); f_var = sem("f_var"); f_rstd = sem("f_rstd")
        f_norm = sem("f_norm"); f_tr = sem("f_tr"); f_T = sem("f_T")
        lg_done = sem("lg_done"); xm_done = sem("xm_done"); px_done = sem("px_done")
        xr_done = sem("xr_done"); pt_done = sem("pt_done"); pT_done = sem("pT_done")
        xpv_done = sem("xpv_done"); x2_done = sem("x2_done"); turned_out = sem("turned_out")
        rt_mm = sem("rt_mm"); rt_d = sem("rt_d"); rt_e = sem("rt_e"); rt_step = sem("rt_step")
        oh_done = sem("oh_done"); rk_mm = sem("rk_mm"); rk_step = sem("rk_step"); pos_step = sem("pos_step")
        rows_done = sem("rows_done"); rows_out = sem("rows_out")
        fin_step = sem("fin_step"); zero_done = sem("zero_done"); zero_out = sem("zero_out")
        table_done = sem("table_done"); result_done = sem("result_done")
        table_in = sem("table_in"); ws_in = sem("ws_in"); w1_in = sem("w1_in"); w2_in = sem("w2_in")
        w1_hi = sem("w1_hi"); w1_lo = sem("w1_lo"); w2_hi = sem("w2_hi"); w2_lo = sem("w2_lo")
        ws_hi = sem("ws_hi"); ws_lo = sem("ws_lo")
        xt_in = [sem(f"xt_in{i}") for i in range(RING)]
        yt_out = [sem(f"yt_out{i}") for i in range(RING)]
        tx_done = sem("tx_done"); xth_done = sem("xth_done"); xtl_done = sem("xtl_done")
        l1_done = sem("l1_done"); relut_done = sem("relut_done"); sqt_done = sem("sqt_done")
        th_done = sem("th_done"); hth_done = sem("hth_done"); htl_done = sem("htl_done")
        l2_done = sem("l2_done"); yt_done = sem("yt_done")
        xs3_in = [sem(f"xs3_in{i}") for i in range(2)]
        xsh_done = sem("xsh_done"); xsl_done = sem("xsl_done")
        up_done = sem("up_done"); relus_done = sem("relus_done"); sqs_done = sem("sqs_done")
        hsh_done = sem("hsh_done"); hsl_done = sem("hsl_done"); down_done = sem("down_done")
        now_done = sem("now_done"); got_in = [sem(f"got_in{i}") for i in range(RING)]
        shared_done = sem("shared_done"); add1_done = sem("add1_done"); add2_done = sem("add2_done")
        out_done = sem("out_done")

        def flags(b):
            if isinstance(b, int):
                return b >= 2, b >= 1, b + 1 < B, b + 2 < B
            return True, True, True, True

        def tile(b, t, n=1):
            return xs[:, bass.ds(b * TB + t, n), :]

        def apart(eng):
            eng.nop(nofuse=True)

        def own_copy(eng, b):
            if isinstance(b, int):
                return b
            reg = eng.alloc_register()
            eng.reg_mov(reg, b)
            return eng.snap(reg, min_val=2, max_val=B - 3)

        def finish(steps):
            for _ in steps:
                pass

        block = stack.enter_context(nc.Block())

        @block.sync
        def _(sp):
            for b in range(2):
                sp.dma_start(xs[:, b * TB:(b + 1) * TB, :], x[b].rearrange("(t p) d -> p t d", p=P)
                             ).then_inc(x_in[b], 16)
            for dst, src in (
                (ident[:], ident_d),
                (wqk[:], wqk_t), (bqks[:], bqk),
                (wv[:], wv_t),
                (wp[:], wp_t),
                (bvs[:], bv.partition_broadcast(P)), (bps[:], bp.partition_broadcast(P)),
                (const[:], const_d), (wr[:], wr_t), (tri_f[:], tri_d),
            ):
                sp.dma_start(dst, src).then_inc(w_in, 16)
            for b in range(2, B):
                sp.dma_start(xs[:, b * TB:(b + 1) * TB, :], x[b].rearrange("(t p) d -> p t d", p=P)
                             ).then_inc(x_in[b], 16)

            def scratch_out(a, par, c):
                sp.wait_ge(q3_done, 4 * a + c + 1)
                apart(sp)
                if c == 0 and not (isinstance(a, int) and a < 2):
                    sp.wait_ge(stack_in, 16 * 2 * NS * (a - 1))
                apart(sp)
                sp.dma_start(scratch[par, :, c].rearrange("n p s -> p n s"), parts[:, :, c, :]
                             ).then_inc(scr_out, 16)

            def stack_load(a, par):
                sp.wait_ge(scr_out, 64 * (a + 1))
                apart(sp)
                if not (isinstance(a, int) and a < 2):
                    sp.wait_ge(s_ready, 64 * (a - 1))
                apart(sp)
                for n in range(NS):
                    for dst, part, c in ((QS, PARTS_Q[n], 0), (KS, PARTS_K[n], 2)):
                        src = scratch[par, part, c:c + 2].rearrange(
                            "c (h d) s -> d (c h) s", d=HD)
                        sp.dma_start(dst[par][n * HD:(n + 1) * HD, :, :], src
                                     ).then_inc(stack_in, 16)

            def max_rows(a, par, g):
                sp.wait_ge(m2_done, NG * a + g + 1)
                apart(sp)
                for n in range(2):
                    sp.dma_start(QS[par][KS_ROWS + n:KS_ROWS + n + 1, g * GH:(g + 1) * GH, :],
                                 mparts[:, g % 2, n, :]).then_inc(mrow_in[g % 2], 16)

            def context_load(a):
                if not (isinstance(a, int) and a == 0):
                    sp.wait_ge(lg_done, a)
                    apart(sp)
                    sp.wait_ge(xpv_done, 2 * a)
                    apart(sp)
                sp.dma_start(ctxT[:], ctx_t[:, bass.ds(a, 1)].rearrange("p o k s -> p (o k) s")
                             ).then_inc(ctx_in, 16)
                sp.dma_start(ctxN[:], ctx_n[:, bass.ds(a, 1)].rearrange("p o d -> p (o d)")
                             ).then_inc(ctx_in, 16)

            def turned_store(a):
                sp.wait_ge(f_T, KD * (2 * a + 2))
                apart(sp)
                sp.dma_start(x_turned[bass.ds(a, 1)].rearrange("o p k s -> p (o k) s"), xrT[:]
                             ).then_inc(turned_out, 16)

            def batch(b, par):
                prv2, prv, nxt, nxt2 = flags(b)
                if nxt:
                    stack_load(b + 1, 1 - par)
                max_rows(b, par, 1)
                if prv2:
                    turned_store(b - 2)
                if prv:
                    context_load(b - 1)
                max_rows(b, par, 2)
                max_rows(b, par, 3)
                if nxt2:
                    for c in range(3):
                        scratch_out(b + 2, par, c)
                if nxt:
                    max_rows(b + 1, 1 - par, 0)
                if nxt2:
                    scratch_out(b + 2, par, 3)

            for c in range(4):
                scratch_out(0, 0, c)
            stack_load(0, 0)
            for c in range(4):
                scratch_out(1, 1, c)
            max_rows(0, 0, 0)
            batch(0, 0)
            batch(1, 1)
            with sp.Fori(0, 2) as i:
                for u in range(2):
                    batch(2 * i + 2 + u, u)
            sp.wait_ge(q3_done, 4 * B)
            sp.dma_start(wsraw[:, 0, :], ws1_t.rearrange("p k f -> p (k f)")).then_inc(ws_in, 16)
            sp.dma_start(wsraw[:, 1, :], ws2_t.rearrange("p k f -> p (k f)")).then_inc(ws_in, 16)
            batch(6, 0)
            sp.wait_ge(s_ready, 64 * 7)
            sp.dma_start(w1raw[:], w1_t).then_inc(w1_in, 16)
            sp.dma_start(w2raw[:], w2_t).then_inc(w2_in, 16)
            batch(7, 1)
            turned_store(B - 2)
            context_load(B - 1)
            turned_store(B - 1)
            sp.wait_ge(rows_done, B)
            sp.wait_ge(turned_out, 16 * B)
            sp.wait_ge(rows_out, 16 * 2 * TB * B)
            sp.dma_start(tab_0[:], table_d).then_inc(table_in, 16)

            def tile_load(t, i, u):
                if not (isinstance(t, int) and t < RING):
                    sp.wait_ge(tx_done, t - RING + 1)
                    apart(sp)
                row = sp.value_load(row_i[0:1, bass.ds(t, 1)], min_val=0,
                                    max_val=E * ROOM - P)
                sp.dma_start(xt[:, u, :], x_rows[bass.ds(row, P), :]).then_inc(xt_in[u], 16)

            def tile_store(t, i, u):
                sp.wait_ge(yt_done, t + 1)
                apart(sp)
                sp.dma_start(y_rows[bass.ds(P * t, P), :], yt[:, u, :]).then_inc(yt_out[u], 16)

            sp.wait_ge(table_done, 1)
            sp.wait_ge(zero_out, 16 * E)
            for t in range(RING):
                tile_load(t, 0, t)
            with sp.Fori(0, TILES // RING - 1) as i:
                for u in range(RING):
                    tile_load(RING * i + u + RING, i + 1, u)
                    tile_store(RING * i + u, i, u)
            for u in range(RING):
                tile_store(TILES - RING + u, TILES // RING - 1, u)

            def block_out(b):
                sp.wait_ge(add2_done, TB * (b + 1))
                apart(sp)
                sp.dma_start(out[bass.ds(b, 1)].rearrange("o (t p) d -> p (o t) d", p=P),
                             tile(b, 0, TB)).then_inc(out_done, 16)

            def half_load(b, h):
                if not (isinstance(b, int) and b == 0):
                    sp.wait_ge(xsl_done, 2 * b + h - 1)
                    apart(sp)
                src = x_turned[bass.ds(b, 1)].rearrange("o p k s -> p (o k) s")
                sp.dma_start(xs3[:, h], src[:, :, h * HB:(h + 1) * HB]).then_inc(xs3_in[h], 16)

            for h in range(2):
                half_load(0, h)
            with sp.Fori(0, B - 1) as b:
                for h in range(2):
                    half_load(b + 1, h)
                block_out(b)
            block_out(B - 1)
            sp.wait_ge(out_done, 16 * B)

        @block.tensor
        def _(pe):
            def misc_free(prev):
                if prev:
                    pe.wait_ge(prev[0], prev[1])

            def transposes(a, k, prev):
                pe.wait_ge(norm_done, TB * (a + 1))
                misc_free(prev)
                for t in range(TB):
                    mm = pe.transpose(mid[:, t * P:(t + 1) * P], xn[0][:, t, k * P:(k + 1) * P],
                                      ident[:])
                mm.then_inc(tr_done, 1)
                return xnT_done, KD * a + k + 1

            def project_qk(a, c, prev):
                pe.wait_ge(xnT_done, KD * (a + 1))
                misc_free(prev)
                for k in range(KD):
                    mm = pe.matmul(mid[:], wqk[:, k, c * P:(c + 1) * P], xnT[0][:, k, :],
                                   start=(k == 0), stop=(k == KD - 1))
                mm.then_inc(qkmm_done, 1)
                return qk_done, 4 * a + c + 1

            def project_v(a, i, prev):
                misc_free(prev)
                for t in range(2):
                    for k in range(KD):
                        mm = pe.matmul(mid[:, t * D:(t + 1) * D],
                                       xnT[0][:, k, (2 * i + t) * P:(2 * i + t + 1) * P],
                                       wv[:, k, :], start=(k == 0), stop=(k == KD - 1))
                mm.then_inc(vmm_done, 1)
                return v_done, 4 * a + 2 * i + 2

            def max_scores(a, par, m):
                if m == 0:
                    pe.wait_ge(stack_in, 16 * 2 * NS * (a + 1))
                for q in range(TB):
                    n = 4 * m + q
                    if not (isinstance(a, int) and a == 0 and n < 2):
                        pe.wait_ge(max_done, 64 * a + n - 1)
                    pe.matmul(bank[4 + n % 2][:], QS[par][0:KS_ROWS, m, q * P:(q + 1) * P],
                              KS[par][0:KS_ROWS, m, :], start=True, stop=True
                              ).then_inc(mx_ready, 1)
                    yield

            def turn_max(a, g, prev):
                pe.wait_ge(max_done, 64 * a + 16 * (g + 1))
                misc_free(prev)
                pe.transpose(end[0:GH * TB, 0:P], mneg[:, g % 2, :], ident[:]
                             ).then_inc(tm_done, 1)
                return m2_done, NG * a + g + 1

            def turn_sums(b, g, prev):
                pe.wait_ge(o_done, NG * b + g + 1)
                misc_free(prev)
                for t in range(TB):
                    mm = pe.transpose(end[:, t * P:(t + 1) * P], o_sb[:, t * P:(t + 1) * P],
                                      ident[:])
                mm.then_inc(turn_done, 1)
                return on_done, NG * b + g + 1

            def turn_heads(b, k, prev):
                pe.wait_ge(on_done, NG * (b + 1))
                misc_free(prev)
                for t in range(TB):
                    mm = pe.transpose(end[:, t * P:(t + 1) * P],
                                      o_nat[:, t, k * P:(k + 1) * P], ident[:])
                mm.then_inc(ont_done, 1)
                return oT_done, KD * b + k + 1

            def project_out(b, i, prev):
                pe.wait_ge(oT_done, KD * (b + 1))
                misc_free(prev)
                for t in range(2):
                    for k in range(KD):
                        mm = pe.matmul(end[:, t * D:(t + 1) * D],
                                       oT[:, k, (2 * i + t) * P:(2 * i + t + 1) * P],
                                       wp[:, k, :], start=(k == 0), stop=(k == KD - 1))
                mm.then_inc(pj_done, 1)
                return x1_done, 2 * b + i + 1

            def scores(b, par, s, j):
                g, kb = divmod(s, TB)
                if kb == 0 and j == 0:
                    pe.wait_ge(mrow_in[g % 2], 32 * (2 * b + g // 2 + 1))
                n = GH * s + j
                last = n - NSB if n >= NSB else (n - 1) % NSB - NSB
                if not (isinstance(b, int) and b == 0 and last < 0):
                    pe.wait_ge(exp_done, 64 * b + last + 1)
                h = g * GH + j
                pe.matmul(bank[n % NSB][:], KS[par][0:KM_ROWS, h, kb * P:(kb + 1) * P],
                          QS[par][0:KM_ROWS, h, :], start=True, stop=True).then_inc(s_ready, 1)

            def values(b, par, s):
                g, kb = divmod(s, TB)
                pe.wait_ge(exp_done, 64 * b + 4 * s + 4)
                if s == 0:
                    pe.wait_ge(v_done, 4 * (b + 1))
                if kb == 0 and not (isinstance(b, int) and b == 0 and s == 0):
                    pe.wait_ge(o_done, NG * b + g)
                for j in range(GH):
                    mm = pe.matmul(bank[6][32 * j:32 * j + 32, :], VO[par][:, kb, g * GH + j, :],
                                   probs[:, kb % 2, j, :], start=(kb == 0), stop=(kb == TB - 1))
                mm.then_inc(pv_done, 1)

            def front_transposes(a, r, k, prev):
                pe.wait_ge(f_norm, TB * (2 * a + r + 1))
                misc_free(prev)
                for t in range(TB):
                    mm = pe.transpose((end, mid)[r][:, t * P:(t + 1) * P],
                                      xn[1 + r][:, t, k * P:(k + 1) * P], ident[:])
                mm.then_inc(f_tr, 1)
                return f_T, KD * (2 * a + r) + k + 1

            def context_logits(a, prev):
                pe.wait_ge(f_T, KD * (2 * a + 1))
                pe.wait_ge(ctx_in, 32 * (a + 1))
                misc_free(prev)
                for t in range(TB):
                    for k in range(KD):
                        mm = pe.matmul(mid[:, t * SC:(t + 1) * SC],
                                       xnT[1][:, k, t * P:(t + 1) * P], ctxT[:, k, :],
                                       start=(k == 0), stop=(k == KD - 1))
                mm.then_inc(lg_done, 1)
                return px_done, TB * (a + 1)

            def turn_probs(a, prev):
                pe.wait_ge(px_done, TB * (a + 1))
                misc_free(prev)
                apart(pe)
                for t in range(TB):
                    mm = pe.transpose(mid[0:SC, t * P:(t + 1) * P], px[:, t, :], ident[:])
                mm.then_inc(pt_done, 1)
                return pT_done, a + 1

            def context_values(a, i, prev):
                pe.wait_ge(pT_done, a + 1)
                misc_free(prev)
                for t in (2 * i, 2 * i + 1):
                    mm = pe.matmul((mid, end)[i][:, t % 2 * D:(t % 2 + 1) * D],
                                   pT[0:SC, t * P:(t + 1) * P], ctxN[:],
                                   start=True, stop=True)
                mm.then_inc(xpv_done, 1)
                return x2_done, TB * a + 2 * i + 2

            def router(a, prev):
                pe.wait_ge(f_T, KD * (2 * a + 2))
                misc_free(prev)
                for t in range(TB):
                    for k in range(KD):
                        mm = pe.matmul(mid[:, t * E:(t + 1) * E],
                                       xrT[:, k, t * P:(t + 1) * P], wr[:, k, :],
                                       start=(k == 0), stop=(k == KD - 1))
                mm.then_inc(rt_mm, 1)
                return rt_d, a + 1

            def count_rows(a, prev):
                pe.wait_ge(oh_done, a + 1)
                misc_free(prev)
                for t in range(TB + 1):
                    dst = end[:, t * E:(t + 1) * E]
                    for v in range(min(t, TB - 1) + 1):
                        mm = pe.matmul(dst, tri[:, 0 if v == t else 1, :], oh[:, v, :],
                                       start=(v == 0), stop=(v == min(t, TB - 1)))
                mm.then_inc(rk_mm, 1)
                return rk_step, 2 * (a + 1)

            def batch(b, par):
                prv2, prv, nxt, nxt2 = flags(b)
                in_mid, in_end = last
                if prv2:
                    in_mid = x2_done, TB * (b - 2) + 2
                    in_end = x2_done, TB * (b - 1)
                for s in range(SLOTS):
                    if s % 4 == 0:
                        b = own_copy(pe, b)
                    m = s + AHEAD
                    ahead = iter(())
                    if m < SLOTS:
                        ahead = max_scores(b, par, m)
                    elif nxt:
                        ahead = max_scores(b + 1, 1 - par, m - SLOTS)
                    for j in range(GH):
                        scores(b, par, s, j)
                        next(ahead, None)
                        if j == 1:
                            if s > 0:
                                values(b, par, s - 1)
                            elif prv:
                                values(b - 1, 1 - par, SLOTS - 1)
                            if prv2 and s == 10:
                                in_end = count_rows(b - 2, in_end)
                        if j == 2:
                            if prv2 and s in (2, 3):
                                in_mid = front_transposes(b - 2, 1, s - 2, in_mid)
                            if prv2 and s == 4:
                                in_mid = router(b - 2, in_mid)
                            if nxt and s in (5, 6):
                                in_mid = project_v(b + 1, s - 5, in_mid)
                            if nxt2 and s in (7, 8):
                                in_mid = transposes(b + 2, s - 7, in_mid)
                            if nxt2 and 9 <= s < 13:
                                in_mid = project_qk(b + 2, s - 9, in_mid)
                            if prv and s == 13:
                                in_mid = context_logits(b - 1, in_mid)
                            if prv and s == 14:
                                in_mid = turn_probs(b - 1, in_mid)
                            if prv and s == 15:
                                in_mid = context_values(b - 1, 0, in_mid)
                    if s % 4 == 1:
                        g = s // 4 + 1
                        if g < NG:
                            in_end = turn_max(b, g, in_end)
                        elif nxt:
                            in_end = turn_max(b + 1, 0, in_end)
                    if s % 4 == 2:
                        if s > 2:
                            in_end = turn_sums(b, s // 4 - 1, in_end)
                        elif prv:
                            in_end = turn_sums(b - 1, NG - 1, in_end)
                    if prv and s in (3, 4):
                        in_end = turn_heads(b - 1, s - 3, in_end)
                    if prv and s in (7, 8):
                        in_end = project_out(b - 1, s - 7, in_end)
                    if prv and s in (11, 12):
                        in_end = front_transposes(b - 1, 0, s - 11, in_end)
                    if prv and s == 15:
                        in_end = context_values(b - 1, 1, in_end)
                return in_mid, in_end

            pe.wait_ge(w_in, 16 * 10)
            in_mid = in_end = None
            for a in range(2):
                for k in range(KD):
                    in_mid = transposes(a, k, in_mid)
                for c in range(4):
                    in_mid = project_qk(a, c, in_mid)
                if a == 0:
                    for i in range(2):
                        in_mid = project_v(0, i, in_mid)
            for m in range(AHEAD):
                for _ in max_scores(0, 0, m):
                    pass
                if m == 4:
                    in_end = turn_max(0, 0, in_end)
            last = in_mid, in_end
            last = batch(0, 0)
            last = batch(1, 1)
            with pe.Fori(0, 2) as i:
                for u in range(2):
                    batch(2 * i + 2 + u, u)
            batch(6, 0)
            in_mid, in_end = batch(7, 1)

            values(B - 1, 1, SLOTS - 1)
            in_end = turn_sums(B - 1, NG - 1, in_end)
            for k in range(KD):
                in_mid = front_transposes(B - 2, 1, k, in_mid)
            for k in range(KD):
                in_end = turn_heads(B - 1, k, in_end)
            in_mid = router(B - 2, in_mid)
            for i in range(2):
                in_end = project_out(B - 1, i, in_end)
            for k in range(KD):
                in_end = front_transposes(B - 1, 0, k, in_end)
            in_mid = context_logits(B - 1, in_mid)
            in_mid = turn_probs(B - 1, in_mid)
            in_mid = context_values(B - 1, 0, in_mid)
            in_end = context_values(B - 1, 1, in_end)
            in_end = count_rows(B - 2, in_end)
            for k in range(KD):
                in_mid = front_transposes(B - 1, 1, k, in_mid)
            in_mid = router(B - 1, in_mid)
            in_end = count_rows(B - 1, in_end)
            misc_free(in_mid)
            misc_free(in_end)

            def three_passes(dst, pairs):
                n = 0
                for a, b in pairs:
                    for i, j in ((0, 0), (0, 1), (1, 0)):
                        mm = pe.matmul(dst, a[i], b[j], start=(n == 0),
                                       stop=(n == 3 * len(pairs) - 1))
                        n += 1
                return mm

            def tile_turn(t, i, u):
                pe.wait_ge(xt_in[u % RING], 16 * (i + 1))
                if not (isinstance(t, int) and t < 2):
                    pe.wait_ge(xtl_done, t - 1)
                for k in range(KD):
                    mm = pe.transpose(bank[u % 2][:, k * P:(k + 1) * P],
                                      xt[:, u % RING, k * P:(k + 1) * P], ident[:])
                mm.then_inc(tx_done, 1)

            expert_of = [pe.alloc_register(name=f"expert{i}") for i in range(RING)]

            def load_expert(t, u):
                pe.load(expert_of[u % RING], expert_i[0:1, bass.ds(t, 1)])

            def tile_expert(u):
                return pe.snap(expert_of[u % RING], min_val=0, max_val=E - 1)

            def tile_up(t, u):
                pe.wait_ge(xtl_done, t + 1)
                if not (isinstance(t, int) and t < 2):
                    pe.wait_ge(relut_done, t - 1)
                e = tile_expert(u)
                three_passes(bank[2 + u % 2][:, 0:F], [
                    ([xT2[i][:, u % 2, k, :] for i in range(2)],
                     [w1[i][:, bass.ds(e, 1), k, :] for i in range(2)]) for k in range(KD)
                ]).then_inc(l1_done, 1)

            def tile_turn_hidden(t, u):
                pe.wait_ge(sqt_done, t + 1)
                if not (isinstance(t, int) and t < 2):
                    pe.wait_ge(htl_done, t - 1)
                for k in range(F // P):
                    mm = pe.transpose(bank[4 + u % 2][:, k * P:(k + 1) * P],
                                      sq_t[:, u % 2, k * P:(k + 1) * P], ident[:])
                mm.then_inc(th_done, 1)

            def tile_down(t, u):
                pe.wait_ge(htl_done, t + 1)
                if not (isinstance(t, int) and t < 2):
                    pe.wait_ge(yt_done, t - 1)
                e = tile_expert(u)
                three_passes(bank[6 + u % 2][:, 0:D], [
                    ([hT2[i][:, u % 2, k, :] for i in range(2)],
                     [w2[i][:, bass.ds(e, 1), k, :] for i in range(2)]) for k in range(F // P)
                ]).then_inc(l2_done, 1)

            def tile_step(s, i, u):
                before = not (isinstance(s, int) and s == 0)
                if before:
                    tile_turn_hidden(s - 1, u + RING - 1)
                if not (isinstance(s, int) and s >= TILES):
                    tile_up(s, u)
                if not (isinstance(s, int) and s + 1 >= TILES):
                    tile_turn(s + 1, i + (u == RING - 1), (u + 1) % RING)
                if before:
                    tile_down(s - 1, u + RING - 1)
                    if not (isinstance(s, int) and s + RING - 1 >= TILES):
                        load_expert(s + RING - 1, u + RING - 1)

            pe.wait_ge(table_done, 1)
            tile_turn(0, 0, 0)
            for t in range(RING):
                load_expert(t, t)
            pe.wait_ge(w1_hi, 4)
            pe.wait_ge(w1_lo, 4)
            pe.wait_ge(w2_hi, 4)
            pe.wait_ge(w2_lo, 4)
            for s in range(RING):
                tile_step(s, 0, s)
            with pe.Fori(1, TILES // RING - 1) as i:
                for u in range(RING):
                    tile_step(RING * i + u, i, u)
            for s in range(TILES - RING, TILES + 1):
                tile_step(s, s // RING, s % RING)

            def shared_up(b, h):
                pe.wait_ge(xsl_done, 2 * b + h + 1)
                for c in range(NFS):
                    if not (isinstance(b, int) and b == 0 and h == 0):
                        pe.wait_ge(relus_done, NFS * (2 * b + h - 1) + c + 1)
                    three_passes(bank[c][:, 0:HB], [
                        ([ws1[i][:, k, c * P:(c + 1) * P] for i in range(2)],
                         [xs2[i][:, h, k, :] for i in range(2)]) for k in range(KD)
                    ]).then_inc(up_done, 1)

            def shared_down(b, h):
                pe.wait_ge(hsl_done, NFS * (2 * b + h + 1))
                if not (isinstance(b, int) and b == 0):
                    pe.wait_ge(shared_done, 2 * b + h - 1)
                for t in range(2):
                    mm = three_passes(bank[4 + h][:, t * D:(t + 1) * D], [
                        ([hs[i][:, h, c, t * P:(t + 1) * P] for i in range(2)],
                         [ws2[i][:, c, :] for i in range(2)]) for c in range(NFS)])
                mm.then_inc(down_done, 1)

            pe.wait_ge(ws_hi, 2)
            pe.wait_ge(ws_lo, 2)
            pe.wait_ge(yt_done, TILES)
            pe.wait_ge(htl_done, TILES)
            shared_up(0, 0)
            shared_up(0, 1)
            shared_down(0, 0)

            def shared_block(b):
                shared_up(b, 0)
                shared_down(b - 1, 1)
                shared_up(b, 1)
                shared_down(b, 0)

            shared_block(1)
            with pe.Fori(2, B) as b:
                shared_block(b)
            shared_down(B - 1, 1)

        @block.scalar
        def _(act):
            def copy_xT(a, k):
                act.wait_ge(tr_done, KD * a + k + 1)
                if not (isinstance(a, int) and a == 0):
                    act.wait_ge(vmm_done, 2 * a)
                act.activation(xnT[0][:, k, :], mid[:], ACT.Copy).then_inc(xnT_done, 1)

            def copy_qk(a, c):
                act.wait_ge(qkmm_done, 4 * a + c + 1)
                if not (isinstance(a, int) and a == 0 and c < 2):
                    act.wait_ge(r1_done, 4 * a + c - 1)
                act.activation(qk[:, c % 2, :], mid[:], ACT.Identity, bias=bqks[:, c:c + 1]
                               ).then_inc(qk_done, 1)

            def second_part(a, c):
                act.wait_ge(r1_done, 4 * a + c + 1)
                if not (isinstance(a, int) and a == 0):
                    act.wait_ge(scr_out, 64 * a)
                act.activation(parts[:, 1, c, :], rest[:, c % 2, :], ACT.Copy).then_inc(q2_done, 1)

            def copy_o(b, g):
                act.wait_ge(pv_done, SLOTS * b + TB * (g + 1))
                if not (isinstance(b, int) and b == 0 and g == 0):
                    act.wait_ge(turn_done, NG * b + g)
                act.activation(o_sb[:], bank[6][:], ACT.Copy).then_inc(o_done, 1)

            def copy_oT(b, k):
                act.wait_ge(ont_done, KD * b + k + 1)
                if not (isinstance(b, int) and b == 0):
                    act.wait_ge(pj_done, 2 * b)
                act.activation(oT[:, k, :], end[:], ACT.Copy).then_inc(oT_done, 1)

            def copy_front(a, r, k):
                act.wait_ge(f_tr, KD * (2 * a + r) + k + 1)
                if r == 0:
                    if not (isinstance(a, int) and a == 0):
                        act.wait_ge(lg_done, a)
                    dst = xnT[1]
                else:
                    if not (isinstance(a, int) and a == 0):
                        act.wait_ge(rt_mm, a)
                        act.wait_ge(turned_out, 16 * a)
                    dst = xrT
                act.activation(dst[:, k, :], (end, mid)[r][:], ACT.Copy).then_inc(f_T, 1)

            def context_probs(a):
                act.wait_ge(xm_done, 2 * a + 2)
                if not (isinstance(a, int) and a == 0):
                    act.wait_ge(pt_done, a)
                    act.wait_ge(xr_done, a)
                for t in range(TB):
                    act.activation(px[:, t, :], mid[:, t * SC:(t + 1) * SC], ACT.Exp,
                                   bias=xb[:, t:t + 1], scale=D ** -0.5,
                                   accum_out=xsum[:, t:t + 1]).then_inc(px_done, 1)

            def copy_probs(a):
                act.wait_ge(pt_done, a + 1)
                if not (isinstance(a, int) and a == 0):
                    act.wait_ge(xpv_done, 2 * a)
                act.activation(pT[0:SC, :], mid[0:SC, :], ACT.Copy).then_inc(pT_done, 1)

            def router_exp(a):
                act.wait_ge(rt_d, a + 1)
                if not (isinstance(a, int) and a == 0):
                    act.wait_ge(rt_step, ROUTE_STEPS * a)
                act.activation(rt["e"][:], rt["d"][:], ACT.Exp).then_inc(rt_e, 1)

            def batch(b, par):
                prv2, prv, nxt, nxt2 = flags(b)
                for s in range(SLOTS):
                    u = SLOTS * b + s
                    for j in range(GH):
                        act.wait_ge(s_ready, 64 * b + 4 * s + j + 1)
                        if j == 0 and not (isinstance(b, int) and b == 0 and s < 2):
                            act.wait_ge(pv_done, u - 1)
                        act.activation(probs[:, s % 2, j, :], bank[(GH * s + j) % NSB][:], ACT.Exp,
                                       scale=HD ** -0.5).then_inc(exp_done, 1)
                        if prv2 and s == 5 and j == 1:
                            router_exp(b - 2)
                    if prv2 and s in (2, 3):
                        copy_front(b - 2, 1, s - 2)
                    if nxt2 and s in (7, 8):
                        copy_xT(b + 2, s - 7)
                    if nxt2 and 9 <= s < 13:
                        copy_qk(b + 2, s - 9)
                    if nxt2 and 11 <= s < 15:
                        second_part(b + 2, s - 11)
                    if s % 4 == 0:
                        if s > 0:
                            copy_o(b, s // 4 - 1)
                        elif prv:
                            copy_o(b - 1, NG - 1)
                    if prv and s in (3, 4):
                        copy_oT(b - 1, s - 3)
                    if prv and s in (11, 12):
                        copy_front(b - 1, 0, s - 11)
                    if prv and s == 13:
                        context_probs(b - 1)
                    if prv and s == 14:
                        copy_probs(b - 1)

            act.wait_ge(w_in, 16 * 10)
            for a in range(2):
                for k in range(KD):
                    copy_xT(a, k)
                for c in range(5):
                    if c < 4:
                        copy_qk(a, c)
                    if c > 0:
                        second_part(a, c - 1)
            batch(0, 0)
            batch(1, 1)
            with act.Fori(0, 2) as i:
                for u in range(2):
                    batch(2 * i + 2 + u, u)
            batch(6, 0)
            batch(7, 1)
            copy_o(B - 1, NG - 1)
            for k in range(KD):
                copy_front(B - 2, 1, k)
            for k in range(KD):
                copy_oT(B - 1, k)
            router_exp(B - 2)
            for k in range(KD):
                copy_front(B - 1, 0, k)
            context_probs(B - 1)
            copy_probs(B - 1)

            act.wait_ge(w1_in, 16)
            act.wait_ge(s_ready, 64 * B)
            for i in range(4):
                act.activation(w1[0][:, 2 * i:2 * i + 2], w1raw[:, 2 * i:2 * i + 2], ACT.Copy
                               ).then_inc(w1_hi, 1)
            for k in range(KD):
                copy_front(B - 1, 1, k)
            act.wait_ge(w2_in, 16)
            act.wait_ge(pv_done, SLOTS * B)
            for i in range(2):
                act.activation(w2[0][:, 2 * i:2 * i + 2], w2raw[:, 2 * i:2 * i + 2], ACT.Copy
                               ).then_inc(w2_hi, 1)
            router_exp(B - 1)
            for i in range(2, 4):
                act.activation(w2[0][:, 2 * i:2 * i + 2], w2raw[:, 2 * i:2 * i + 2], ACT.Copy
                               ).then_inc(w2_hi, 1)

            def tile_hi(t, u):
                act.wait_ge(tx_done, t + 1)
                if not (isinstance(t, int) and t < 2):
                    act.wait_ge(l1_done, t - 1)
                act.activation(xT2[0][:, u % 2].rearrange("p k s -> p (k s)"),
                               bank[u % 2][:, 0:D], ACT.Copy).then_inc(xth_done, 1)

            def tile_relu(t, u):
                act.wait_ge(l1_done, t + 1)
                if not (isinstance(t, int) and t < 2):
                    act.wait_ge(sqt_done, t - 1)
                act.activation(relu_t[:, u % 2, :], bank[2 + u % 2][:, 0:F], ACT.Relu
                               ).then_inc(relut_done, 1)

            def tile_hidden_hi(t, u):
                act.wait_ge(th_done, t + 1)
                if not (isinstance(t, int) and t < 2):
                    act.wait_ge(l2_done, t - 1)
                act.activation(hT2[0][:, u % 2].rearrange("p k s -> p (k s)"),
                               bank[4 + u % 2][:, 0:F], ACT.Copy).then_inc(hth_done, 1)

            def tile_result(t, i, u):
                act.wait_ge(l2_done, t + 1)
                if not (isinstance(t, int) and t < RING):
                    act.wait_ge(yt_out[u % RING], 16 * i)
                act.activation(yt[:, u % RING, :], bank[6 + u % 2][:, 0:D], ACT.Copy
                               ).then_inc(yt_done, 1)

            def tile_step(s, i, u):
                before = not (isinstance(s, int) and s == 0)
                if before:
                    tile_hidden_hi(s - 1, u + 1)
                if not (isinstance(s, int) and s >= TILES):
                    tile_relu(s, u)
                if not (isinstance(s, int) and s + 1 >= TILES):
                    tile_hi(s + 1, u + 1)
                if before:
                    tile_result(s - 1, i - (u == 0), (u + RING - 1) % RING)

            act.wait_ge(rows_out, 16 * 2 * TB * B)
            act.wait_ge(turned_out, 16 * B)
            tile_hi(0, 0)
            for s in range(2 * RING):
                tile_step(s, s // RING, s % RING)
            with act.Fori(2, TILES // RING - 1) as i:
                for u in range(RING):
                    tile_step(RING * i + u, i, u)
            for s in range(TILES - RING, TILES + 1):
                tile_step(s, s // RING, s % RING)

            def shared_hi(b, h):
                act.wait_ge(xs3_in[h], 16 * (b + 1))
                if not (isinstance(b, int) and b == 0):
                    act.wait_ge(up_done, NFS * (2 * b + h - 1))
                act.activation(xs2[0][:, h].rearrange("p k s -> p (k s)"),
                               xs3[:, h].rearrange("p k s -> p (k s)"), ACT.Copy
                               ).then_inc(xsh_done, 1)

            def shared_relu(b, h):
                n = NFS * (2 * b + h)
                for c in range(NFS):
                    act.wait_ge(up_done, n + c + 1)
                    if not (isinstance(b, int) and b == 0 and h == 0):
                        act.wait_ge(sqs_done, n - NFS + c + 1)
                    act.activation(relu_s[:, c, :], bank[c][:, 0:HB], ACT.Relu
                                   ).then_inc(relus_done, 1)

            def shared_hidden_hi(b, h):
                n = NFS * (2 * b + h)
                if not (isinstance(b, int) and b == 0):
                    act.wait_ge(down_done, 2 * b + h - 1)
                for c in range(NFS):
                    act.wait_ge(sqs_done, n + c + 1)
                    act.activation(hs[0][:, h, c, :], sq_s[:, c, :], ACT.Copy
                                   ).then_inc(hsh_done, 1)

            act.wait_ge(w2_lo, 4)
            act.wait_ge(ws_in, 32)
            act.activation(ws1[0][:].rearrange("p k f -> p (k f)"), wsraw[:, 0, :], ACT.Copy
                           ).then_inc(ws_hi, 1)
            act.activation(ws2[0][:].rearrange("p k f -> p (k f)"), wsraw[:, 1, :], ACT.Copy
                           ).then_inc(ws_hi, 1)
            for h in range(2):
                shared_hi(0, h)
            shared_relu(0, 0)
            shared_hidden_hi(0, 0)

            def shared_block(b):
                shared_relu(b - 1, 1)
                shared_hi(b, 0)
                shared_hidden_hi(b - 1, 1)
                shared_relu(b, 0)
                shared_hi(b, 1)
                shared_hidden_hi(b, 0)

            shared_block(1)
            with act.Fori(2, B) as b:
                shared_block(b)
            shared_relu(B - 1, 1)
            shared_hidden_hi(B - 1, 1)

        @block.vector
        def _(dve):
            def stats(a, first):
                if first:
                    dve.wait_ge(x_in[a], 16)
                if not (isinstance(a, int) and a == 0):
                    dve.wait_ge(mv_done, TB * a)
                apart(dve)
                for t in range(TB):
                    dve.bn_stats(st[0][:, t, :], tile(a, t)[:, 0]).then_inc(bn_done, 1)
                    yield
                if not (isinstance(a, int) and a == 0):
                    dve.wait_ge(norm_done, TB * a)
                dve.wait_ge(bn_done, TB * (a + 1))
                apart(dve)
                for t in range(TB):
                    dve.bn_aggr(mv[0][:, t, :], st[0][:, t, :]).then_inc(mv_done, 1)
                yield
                dve.wait_ge(mv_done, TB * (a + 1))
                if not (isinstance(a, int) and a == 0):
                    dve.wait_ge(rstd_done, a)
                dve.tensor_scalar(var[0][:], mv[0][:, :, 1], EPS, None, ALU.add).then_inc(var_done, 1)

            def norm(a):
                dve.wait_ge(rstd_done, a + 1)
                if not (isinstance(a, int) and a == 0):
                    dve.wait_ge(tr_done, KD * a)
                for t in range(TB):
                    dve.tensor_scalar(xn[0][:, t, :], tile(a, t)[:, 0], mv[0][:, t, 0:1],
                                      rstd[0][:, t:t + 1], ALU.subtract, ALU.mult
                                      ).then_inc(norm_done, 1)
                    yield

            def first_part(a, c):
                dve.wait_ge(qk_done, 4 * a + c + 1)
                if not (isinstance(a, int) and a == 0):
                    dve.wait_ge(scr_out, 64 * a)
                apart(dve)
                dve.tensor_copy(parts[:, 0, c, :], qk[:, c % 2, :]).then_inc(q1_done, 1)

            def copy_v(a, par, i):
                dve.wait_ge(vmm_done, 2 * a + i + 1)
                if i == 0 and not (isinstance(a, int) and a < 2):
                    dve.wait_ge(pv_done, SLOTS * (a - 1))
                for t in range(2):
                    dve.tensor_tensor(
                        VO[par][:, 2 * i + t, :, 1:1 + HD],
                        mid[:, t * D:(t + 1) * D].rearrange("p (h d) -> p h d", d=HD),
                        bvs[:].rearrange("p (h d) -> p h d", d=HD), ALU.add
                    ).then_inc(v_done, 1)

            def maxima(a, m):
                g = m // GH
                for q in range(TB):
                    n = 4 * m + q
                    dve.wait_ge(mx_ready, 64 * a + n + 1)
                    if m % GH == 0 and q == 0 and not (isinstance(a, int) and a == 0 and g < 2):
                        dve.wait_ge(tm_done, NG * a + g - 1)
                    dve.tensor_reduce(mneg[:, g % 2, m % GH * TB + q:m % GH * TB + q + 1],
                                      bank[4 + n % 2][:], AX.X, ALU.max, negate=True
                                      ).then_inc(max_done, 1)
                    yield q

            def split_max(a, g):
                G = NG * a + g
                dve.wait_ge(tm_done, G + 1)
                if not (isinstance(a, int) and a == 0 and g < 2):
                    dve.wait_ge(mrow_in[g % 2], 32 * (2 * a + g // 2))
                dve.tensor_copy(mparts[:, g % 2, 0, :], end[0:GH * TB, 0:P]
                                ).then_inc(m1_done, 1)
                dve.wait_ge(m1_done, G + 1)
                dve.tensor_tensor(mparts[:, g % 2, 1, :], end[0:GH * TB, 0:P],
                                  mparts[:, g % 2, 0, :], ALU.subtract).then_inc(m2_done, 1)

            def normalise(b, g):
                G = NG * b + g
                dve.wait_ge(turn_done, G + 1)
                if not (isinstance(b, int) and b == 0 and g == 0):
                    dve.wait_ge(on_done, G)
                sums = end[:].rearrange("p (t j c) -> p t j c", t=TB, j=GH)
                dve.reciprocal(rden[:], sums[:, :, :, 0]).then_inc(rden_done, 1)
                dve.wait_ge(rden_done, G + 1)
                if g == 0 and not (isinstance(b, int) and b == 0):
                    dve.wait_ge(ont_done, KD * b)
                dve.tensor_tensor(
                    o_nat[:, :, g * GH * HD:(g + 1) * GH * HD].rearrange(
                        "p t (j d) -> p t j d", j=GH),
                    sums[:, :, :, 1:1 + HD],
                    rden[:].unsqueeze(3).to_broadcast([P, TB, GH, HD]), ALU.mult
                ).then_inc(on_done, 1)

            def add_out(b, i):
                dve.wait_ge(pj_done, 2 * b + i + 1)
                dve.wait_ge(xb_done, TB * (b + 1))
                t = tile(b, 2 * i, 2)
                dve.tensor_tensor(t, end[:].rearrange("p (t d) -> p t d", t=2), t, ALU.add
                                  ).then_inc(x1_done, 1)

            def row_stats(a, r):
                n = 2 * a + r
                if r == 0:
                    dve.wait_ge(x1_done, 2 * (a + 1))
                else:
                    dve.wait_ge(x2_done, TB * (a + 1))
                if not (isinstance(a, int) and a == 0 and r == 0):
                    dve.wait_ge(f_mv, TB * n)
                    dve.wait_ge(f_norm, TB * n)
                apart(dve)
                for t in range(TB):
                    dve.bn_stats(st[1][:, t, :], tile(a, t)[:, 0]).then_inc(f_bn, 1)
                    yield
                dve.wait_ge(f_bn, TB * (n + 1))
                apart(dve)
                for t in range(TB):
                    dve.bn_aggr(mv[1][:, t, :], st[1][:, t, :]).then_inc(f_mv, 1)
                yield
                dve.wait_ge(f_mv, TB * (n + 1))
                if not (isinstance(a, int) and a == 0 and r == 0):
                    dve.wait_ge(f_rstd, n)
                dve.tensor_scalar(var[1][:], mv[1][:, :, 1], EPS, None, ALU.add
                                  ).then_inc(f_var, 1)

            def row_norm(a, r):
                n = 2 * a + r
                dve.wait_ge(f_rstd, n + 1)
                if not (isinstance(a, int) and a == 0 and r == 0):
                    dve.wait_ge(f_tr, KD * n)
                if r == 1 and not (isinstance(a, int) and a == 0):
                    dve.wait_ge(rows_out, 16 * 2 * TB * a)
                for t in range(TB):
                    dve.tensor_scalar(xn[1 + r][:, t, :], tile(a, t)[:, 0], mv[1][:, t, 0:1],
                                      rstd[1][:, t:t + 1], ALU.subtract, ALU.mult
                                      ).then_inc(f_norm, 1)
                    yield

            def context_max(a):
                dve.wait_ge(lg_done, a + 1)
                if not (isinstance(a, int) and a == 0):
                    dve.wait_ge(px_done, TB * a)
                dve.tensor_reduce(xm[:], mid[:, 0:TB * SC].rearrange("p (t s) -> p t s", s=SC),
                                  AX.X, ALU.max).then_inc(xm_done, 1)
                dve.wait_ge(xm_done, 2 * a + 1)
                dve.tensor_scalar(xb[:], xm[:], -(D ** -0.5), None, ALU.mult
                                  ).then_inc(xm_done, 1)

            def context_invert(a):
                dve.wait_ge(px_done, TB * (a + 1))
                if not (isinstance(a, int) and a == 0):
                    dve.wait_ge(x2_done, TB * a)
                dve.reciprocal(xr[:], xsum[:]).then_inc(xr_done, 1)

            def context_add(a, i):
                dve.wait_ge(xr_done, a + 1)
                dve.wait_ge(xpv_done, 2 * a + i + 1)
                for t in (2 * i, 2 * i + 1):
                    xt_ = tile(a, t)[:, 0]
                    dve.scalar_tensor_tensor(
                        out=xt_, in0=(mid, end)[i][:, t % 2 * D:(t % 2 + 1) * D],
                        scalar=xr[:, t:t + 1], in1=xt_, op0=ALU.mult, op1=ALU.add
                    ).then_inc(x2_done, 1)

            def wide(v, n=TB):
                return v.unsqueeze(2).to_broadcast([P, n, E])

            def chain(s, start):
                count = [start]

                def done():
                    dve.wait_ge(s, count[0])

                def put(ins):
                    ins.then_inc(s, 1)
                    count[0] = count[0] + 1

                def step(ins):
                    put(ins)
                    done()
                return step, put, done

            def router_logits(a):
                step, _, _ = chain(rt_step, ROUTE_STEPS * a)
                dve.wait_ge(rt_mm, a + 1)
                logits = mid[:, 0:TB * E].rearrange("p (t e) -> p t e", e=E)
                step(dve.tensor_reduce(rc["m"][:], logits, AX.X, ALU.max))
                if not (isinstance(a, int) and a == 0):
                    dve.wait_ge(rt_e, a)
                dve.tensor_tensor(rt["d"][:], logits, wide(rc["m"][:]), ALU.subtract
                                  ).then_inc(rt_d, 1)

            def route(a):
                _, put, done = chain(rt_step, ROUTE_STEPS * a + 1)
                dve.wait_ge(rt_e, a + 1)
                e = rt["e"]
                for i, src in (("1", e), ("2", rt["e2"])):
                    if i == "2":
                        put(dve.scalar_tensor_tensor(out=rt["e2"][:], in0=rt["oh1"][:],
                                                      scalar=-2.0, in1=e[:], op0=ALU.mult,
                                                      op1=ALU.add))
                        yield
                        done()
                    put(dve.tensor_reduce(rc["m" + i][:], src[:], AX.X, ALU.max))
                    yield
                    done()
                    put(dve.tensor_tensor(rt["eq" + i][:], src[:], wide(rc["m" + i][:]),
                                           ALU.is_equal))
                    yield
                    done()
                    put(dve.tensor_tensor(rt["s" + i][:], rt["eq" + i][:], rank, ALU.mult))
                    yield
                    done()
                    put(dve.tensor_reduce(rc["sm" + i][:], rt["s" + i][:], AX.X, ALU.max))
                    yield
                    done()
                    put(dve.tensor_tensor(rt["oh" + i][:], rt["s" + i][:],
                                           wide(rc["sm" + i][:]), ALU.is_equal))
                    yield
                    done()
                if not (isinstance(a, int) and a == 0):
                    dve.wait_ge(rk_mm, a)
                dve.tensor_tensor(oh[:], rt["oh1"][:], rt["oh2"][:], ALU.add
                                  ).then_inc(oh_done, 1)
                put(dve.tensor_tensor(rc["den"][:], rc["m1"][:], rc["m2"][:], ALU.add))
                yield
                done()
                put(dve.reciprocal(rc["r"][:], rc["den"][:]))
                yield
                done()
                for i in range(2):
                    put(dve.tensor_tensor(weight[:, i, bass.ds(a * TB, TB)],
                                           rc[f"m{i + 1}"][:], rc["r"][:], ALU.mult))
                    yield
                    done()
                for i in range(2):
                    put(dve.tensor_scalar(chosen[:, i, bass.ds(a * TB, TB), :],
                                           rt[f"oh{i + 1}"][:], 0.0, None, ALU.add))
                    yield
                    done()

            def count_on(a):
                dve.wait_ge(rk_mm, a + 1)
                if not (isinstance(a, int) and a == 0):
                    dve.wait_ge(rk_step, 2 * a)
                    dve.wait_ge(rows_done, a)
                count = end[:, 0:TB * E].rearrange("p (t e) -> p t e", e=E)
                dve.tensor_tensor(rt["row"][:], count,
                                  next_row[:].unsqueeze(1).to_broadcast([P, TB, E]), ALU.add
                                  ).then_inc(rk_step, 1)
                dve.wait_ge(rk_step, 2 * a + 1)
                dve.tensor_tensor(next_row[:], end[:, TB * E:(TB + 1) * E], next_row[:],
                                  ALU.add).then_inc(rk_step, 1)

            def send_rows(a):
                dve.wait_ge(rk_step, 2 * (a + 1))
                _, put, done = chain(pos_step, 4 * a)
                for i in range(2):
                    put(dve.tensor_tensor(rt[f"p{i + 1}"][:], rt["row"][:],
                                           rt[f"oh{i + 1}"][:], ALU.mult))
                    yield
                    done()
                    apart(dve)
                    put(dve.tensor_reduce(place[:, i, bass.ds(a * TB, TB)],
                                           rt[f"p{i + 1}"][:], AX.X, ALU.add))
                    yield
                    done()
                if not (isinstance(a, int) and a == 0):
                    dve.wait_ge(rows_out, 16 * 2 * TB * a)
                apart(dve)
                dve.tensor_copy(rows_i[:], place[:, :, bass.ds(a * TB, TB)]
                                ).then_inc(rows_done, 1)

            def batch(b, par):
                prv2, prv, nxt, nxt2 = flags(b)
                routing = iter(())
                for s in range(SLOTS):
                    if s % 4 == 0:
                        b = own_copy(dve, b)
                    between = iter(())
                    start = 0
                    if prv2 and s == 0:
                        between = row_stats(b - 2, 1)
                    if prv2 and s == 1:
                        between, start = row_norm(b - 2, 1), 1
                    if nxt2 and s == 2:
                        between = stats(b + 2, False)
                    if nxt2 and s == 3:
                        between, start = norm(b + 2), 3
                    if prv2 and s == 5:
                        routing, start = route(b - 2), 2
                    if s in (5, 6, 7, 8):
                        between = routing
                    if prv and s == 9:
                        between = row_stats(b - 1, 0)
                    if prv and s == 10:
                        between, start = row_norm(b - 1, 0), 1
                    if prv2 and s == 11:
                        between = send_rows(b - 2)
                    m = s + AHEAD
                    ahead = range(TB)
                    if m < SLOTS:
                        ahead = maxima(b, m)
                    elif nxt:
                        ahead = maxima(b + 1, m - SLOTS)
                    for q in ahead:
                        if nxt2 and 10 <= s < 14 and q == 0:
                            first_part(b + 2, s - 10)
                        if q >= start:
                            next(between, None)
                        if prv2 and s == 10 and q == 2:
                            count_on(b - 2)
                    if s in (6, 7):
                        next(between, None)
                    elif s != 5:
                        finish(between)
                    if nxt and s in (5, 6):
                        copy_v(b + 1, 1 - par, s - 5)
                    if prv2 and s == 4:
                        router_logits(b - 2)
                    if s % 4 == 1:
                        if s // 4 + 1 < NG:
                            split_max(b, s // 4 + 1)
                        elif nxt:
                            split_max(b + 1, 0)
                    if s % 4 == 2:
                        if s > 2:
                            normalise(b, s // 4 - 1)
                        elif prv:
                            normalise(b - 1, NG - 1)
                    if prv and s in (7, 8):
                        add_out(b - 1, s - 7)
                    if prv and s == 13:
                        context_max(b - 1)
                    if prv and s == 14:
                        context_invert(b - 1)
                    if prv and s == 15:
                        for i in range(2):
                            context_add(b - 1, i)

            for i in range(2):
                dve.memset(KS[i][KS_ROWS:KM_ROWS], 1.0).then_inc(init, 1)
            for i in range(2):
                dve.memset(VO[i][:], 0.0).then_inc(init, 1)
            dve.wait_ge(init, 4)
            for i in range(2):
                dve.memset(VO[i][:, :, :, 0:1], 1.0).then_inc(init, 1)
            dve.memset(zeros[:], 0.0).then_inc(zeros_set, 1)
            for a in range(2):
                finish(stats(a, True))
                finish(norm(a))
            dve.wait_ge(w_in, 16 * 10)
            dve.wait_ge(init, 6)
            dve.tensor_copy(tri[:], tri_f[:]).then_inc(tri_set, 1)
            dve.tensor_copy(next_row[:], first).then_inc(tri_set, 1)
            dve.wait_ge(tri_set, 2)
            for a in range(2):
                for c in range(4):
                    first_part(a, c)
                if a == 0:
                    for i in range(2):
                        copy_v(0, 0, i)
            for b in range(2, B):
                dve.wait_ge(x_in[b], 16)
            for m in range(AHEAD):
                finish(maxima(0, m))
                if m == 4:
                    split_max(0, 0)
            batch(0, 0)
            batch(1, 1)
            with dve.Fori(0, 2) as i:
                for u in range(2):
                    batch(2 * i + 2 + u, u)
            batch(6, 0)
            batch(7, 1)
            finish(row_stats(B - 2, 1))
            normalise(B - 1, NG - 1)
            finish(row_norm(B - 2, 1))
            router_logits(B - 2)
            for i in range(2):
                add_out(B - 1, i)
            finish(row_stats(B - 1, 0))
            finish(row_norm(B - 1, 0))
            finish(route(B - 2))
            context_max(B - 1)
            context_invert(B - 1)
            for i in range(2):
                context_add(B - 1, i)
            finish(row_stats(B - 1, 1))
            count_on(B - 2)
            finish(send_rows(B - 2))
            finish(row_norm(B - 1, 1))

            def split_lo(dst, raw, hi, i, s_hi, s_lo):
                dve.wait_ge(s_hi, i + 1)
                dve.tensor_tensor(dst[:, 2 * i:2 * i + 2], raw[:, 2 * i:2 * i + 2],
                                  hi[:, 2 * i:2 * i + 2].bitcast(F32), ALU.subtract
                                  ).then_inc(s_lo, 1)

            for i in range(2):
                split_lo(w1[1], w1raw, w1[0], i, w1_hi, w1_lo)
            router_logits(B - 1)
            for i in range(2, 4):
                split_lo(w1[1], w1raw, w1[0], i, w1_hi, w1_lo)
            finish(route(B - 1))
            count_on(B - 1)
            finish(send_rows(B - 1))

            step, _, _ = chain(fin_step, 0)
            dve.wait_ge(turned_out, 16 * B)
            dve.wait_ge(table_in, 16)
            step(dve.tensor_tensor(counted[:], next_row[:], first, ALU.subtract))
            dve.tensor_tensor(zero_i[:], counted[:], first_p, ALU.add).then_inc(zero_done, 1)
            over = fin_a[:].rearrange("p a b -> p (a b)").rearrange("p (e j) -> p e j", e=E)
            step(dve.tensor_tensor(over, counted[:].unsqueeze(2).to_broadcast([P, E, B * TB]),
                                   steps.unsqueeze(1).to_broadcast([P, E, B * TB]), ALU.is_gt))
            step(dve.tensor_reduce(tiles[:], over, AX.X, ALU.add))
            sums = fin_b[:, 0:E, :]
            step(dve.tensor_tensor(sums, tiles[:].unsqueeze(1).to_broadcast([P, E, E]), upto,
                                   ALU.mult))
            step(dve.tensor_reduce(incl[:], sums, AX.X, ALU.add))
            step(dve.tensor_tensor(excl[:], incl[:], tiles[:], ALU.subtract))
            step(dve.scalar_tensor_tensor(out=shift[:], in0=excl[:], scalar=-float(P), in1=first,
                                          op0=ALU.mult, op1=ALU.add))
            step(dve.tensor_scalar(tab_n[:, 0:1], incl[0:1, E - 1:E], -1.0, None, ALU.add))
            step(dve.tensor_scalar(tab_t[:], tab_0[:], tab_n[:, 0:1], None, ALU.min))
            step(dve.tensor_tensor(tab_a[:], tab_t[:].unsqueeze(2).to_broadcast([1, TILES, E]),
                                   incl[0:1, :].unsqueeze(1).to_broadcast([1, TILES, E]),
                                   ALU.is_ge))
            step(dve.tensor_reduce(tab_c[:, 0], tab_a[:], AX.X, ALU.add))
            step(dve.tensor_copy(expert_i[:], tab_c[:, 0]))
            step(dve.tensor_scalar(fin_c[0:1, 0, 0:E], tiles[0:1, :], -float(P), float(ROOM),
                                   ALU.mult, ALU.add))
            step(dve.tensor_tensor(tab_b[:], tab_a[:],
                                   fin_c[0:1, 0, 0:E].unsqueeze(1).to_broadcast([1, TILES, E]),
                                   ALU.mult))
            step(dve.tensor_reduce(tab_c[:, 1], tab_b[:], AX.X, ALU.add))
            step(dve.scalar_tensor_tensor(out=row_i[:], in0=tab_t[:], scalar=float(P),
                                          in1=tab_c[:, 1], op0=ALU.mult, op1=ALU.add))
            dve.tensor_copy(tab_n[:, 1:2], tab_n[:, 0:1]).then_inc(table_done, 1)
            for i in range(4):
                split_lo(w2[1], w2raw, w2[0], i, w2_hi, w2_lo)

            def tile_lo(t, u):
                dve.wait_ge(xth_done, t + 1)
                if not (isinstance(t, int) and t < 2):
                    dve.wait_ge(l1_done, t - 1)
                dve.tensor_tensor(xT2[1][:, u % 2].rearrange("p k s -> p (k s)"),
                                  bank[u % 2][:, 0:D],
                                  xT2[0][:, u % 2].rearrange("p k s -> p (k s)").bitcast(F32),
                                  ALU.subtract).then_inc(xtl_done, 1)

            def tile_square(t, u):
                dve.wait_ge(relut_done, t + 1)
                if not (isinstance(t, int) and t < 2):
                    dve.wait_ge(th_done, t - 1)
                dve.tensor_tensor(sq_t[:, u % 2, :], relu_t[:, u % 2, :], relu_t[:, u % 2, :],
                                  ALU.mult).then_inc(sqt_done, 1)

            def tile_hidden_lo(t, u):
                dve.wait_ge(hth_done, t + 1)
                if not (isinstance(t, int) and t < 2):
                    dve.wait_ge(l2_done, t - 1)
                dve.tensor_tensor(hT2[1][:, u % 2].rearrange("p k s -> p (k s)"),
                                  bank[4 + u % 2][:, 0:F],
                                  hT2[0][:, u % 2].rearrange("p k s -> p (k s)").bitcast(F32),
                                  ALU.subtract).then_inc(htl_done, 1)

            def tile_step(s, u):
                if not (isinstance(s, int) and s == 0):
                    tile_hidden_lo(s - 1, u + 1)
                if not (isinstance(s, int) and s >= TILES):
                    tile_square(s, u)
                if not (isinstance(s, int) and s + 1 >= TILES):
                    tile_lo(s + 1, u + 1)

            dve.wait_ge(rows_out, 16 * 2 * TB * B)
            tile_lo(0, 0)
            for s in range(RING):
                tile_step(s, s)
            for i in range(2):
                step(dve.tensor_tensor(fin_a[:], chosen[:, i],
                                       shift[:].unsqueeze(1).to_broadcast([P, B * TB, E]),
                                       ALU.mult))
                step(dve.tensor_reduce(fin_c[:, i], fin_a[:], AX.X, ALU.add))
            step(dve.tensor_tensor(result_i[:], place[:], fin_c[:], ALU.subtract))
            dve.tensor_copy(result_now[:], result_i[:, :, 0:TB]).then_inc(now_done, 1)
            with dve.Fori(1, TILES // RING - 1) as i:
                for u in range(RING):
                    tile_step(RING * i + u, u)
            for s in range(TILES - RING, TILES + 1):
                tile_step(s, s % RING)

            def shared_lo(b, h):
                dve.wait_ge(xsh_done, 2 * b + h + 1)
                if not (isinstance(b, int) and b == 0):
                    dve.wait_ge(up_done, NFS * (2 * b + h - 1))
                dve.tensor_tensor(xs2[1][:, h].rearrange("p k s -> p (k s)"),
                                  xs3[:, h].rearrange("p k s -> p (k s)"),
                                  xs2[0][:, h].rearrange("p k s -> p (k s)").bitcast(F32),
                                  ALU.subtract).then_inc(xsl_done, 1)

            def shared_square(b, h):
                n = NFS * (2 * b + h)
                for c in range(NFS):
                    dve.wait_ge(relus_done, n + c + 1)
                    if not (isinstance(b, int) and b == 0 and h == 0):
                        dve.wait_ge(hsl_done, n - NFS + c + 1)
                    dve.tensor_tensor(sq_s[:, c, :], relu_s[:, c, :], relu_s[:, c, :], ALU.mult
                                      ).then_inc(sqs_done, 1)

            def shared_hidden_lo(b, h):
                n = NFS * (2 * b + h)
                if not (isinstance(b, int) and b == 0):
                    dve.wait_ge(down_done, 2 * b + h - 1)
                for c in range(NFS):
                    dve.wait_ge(hsh_done, n + c + 1)
                    dve.tensor_tensor(hs[1][:, h, c, :], sq_s[:, c, :],
                                      hs[0][:, h, c, :].bitcast(F32), ALU.subtract
                                      ).then_inc(hsl_done, 1)

            def shared_add(b, h):
                dve.wait_ge(down_done, 2 * b + h + 1)
                x2 = tile(b, 2 * h, 2)
                dve.tensor_tensor(x2, bank[4 + h][:].rearrange("p (t d) -> p t d", t=2), x2,
                                  ALU.add).then_inc(shared_done, 1)

            def experts_add(b, h):
                dve.wait_ge(shared_done, 2 * b + h + 1)
                for t in (2 * h, 2 * h + 1):
                    dve.wait_ge(got_in[t], 32 * (b + 1))
                    x1 = tile(b, t)[:, 0]
                    dve.scalar_tensor_tensor(
                        out=x1, in0=got[:, t, 0, :],
                        scalar=weight[:, 0, bass.ds(b * TB + t, 1)],
                        in1=x1, op0=ALU.mult, op1=ALU.add).then_inc(add1_done, 1)
                for t in (2 * h, 2 * h + 1):
                    dve.wait_ge(add1_done, TB * b + t + 1)
                    x1 = tile(b, t)[:, 0]
                    dve.scalar_tensor_tensor(
                        out=x1, in0=got[:, t, 1, :],
                        scalar=weight[:, 1, bass.ds(b * TB + t, 1)],
                        in1=x1, op0=ALU.mult, op1=ALU.add).then_inc(add2_done, 1)

            def next_results(b):
                for t in range(TB):
                    dve.wait_ge(got_in[t], 32 * b)
                apart(dve)
                dve.tensor_copy(result_now[:], result_i[:, :, bass.ds(b * TB, TB)]
                                ).then_inc(now_done, 1)

            for i in range(2):
                dve.wait_ge(ws_hi, i + 1)
                (ws, raw) = ((ws1, wsraw[:, 0, :]), (ws2, wsraw[:, 1, :]))[i]
                dve.tensor_tensor(ws[1][:].rearrange("p k f -> p (k f)"), raw,
                                  ws[0][:].rearrange("p k f -> p (k f)").bitcast(F32),
                                  ALU.subtract).then_inc(ws_lo, 1)
            for h in range(2):
                shared_lo(0, h)
            shared_square(0, 0)
            shared_hidden_lo(0, 0)

            def shared_block(b):
                shared_square(b - 1, 1)
                shared_lo(b, 0)
                shared_hidden_lo(b - 1, 1)
                shared_add(b - 1, 0)
                experts_add(b - 1, 0)
                shared_square(b, 0)
                shared_lo(b, 1)
                shared_hidden_lo(b, 0)
                shared_add(b - 1, 1)
                experts_add(b - 1, 1)
                next_results(b)

            shared_block(1)
            with dve.Fori(2, B) as b:
                shared_block(b)
            shared_square(B - 1, 1)
            shared_hidden_lo(B - 1, 1)
            for h in range(2):
                shared_add(B - 1, h)
                experts_add(B - 1, h)

        @block.gpsimd
        def _(pool):
            def inverse_std(a):
                pool.wait_ge(var_done, a + 1)
                if not (isinstance(a, int) and a == 0):
                    pool.wait_ge(norm_done, TB * a)
                pool.tensor_tensor(rstd[0][:], var[0][:], minus_half[:], ALU.pow
                                   ).then_inc(rstd_done, 1)

            def add_bias(a):
                pool.wait_ge(norm_done, TB * (a + 1))
                apart(pool)
                for t in range(TB):
                    xt = tile(a, t)[:, 0]
                    pool.tensor_tensor(xt, xt, bps[:], ALU.add).then_inc(xb_done, 1)

            def first_rest(a, c):
                pool.wait_ge(q1_done, 4 * a + c + 1)
                if not (isinstance(a, int) and a == 0 and c < 2):
                    pool.wait_ge(q3_done, 4 * a + c - 1)
                    pool.wait_ge(q2_done, 4 * a + c - 1)
                pool.tensor_tensor(rest[:, c % 2, :], qk[:, c % 2, :], parts[:, 0, c, :],
                                   ALU.subtract).then_inc(r1_done, 1)

            def third_part(a, c):
                pool.wait_ge(q2_done, 4 * a + c + 1)
                pool.tensor_tensor(parts[:, 2, c, :], rest[:, c % 2, :], parts[:, 1, c, :],
                                   ALU.subtract).then_inc(q3_done, 1)

            def row_inverse_std(a, r):
                n = 2 * a + r
                pool.wait_ge(f_var, n + 1)
                if not (isinstance(a, int) and a == 0 and r == 0):
                    pool.wait_ge(f_norm, TB * n)
                pool.tensor_tensor(rstd[1][:], var[1][:], minus_half[:], ALU.pow
                                   ).then_inc(f_rstd, 1)

            def scatter_rows(a, tiles=range(TB)):
                if tiles[0] == 0:
                    pool.wait_ge(rows_done, a + 1)
                    apart(pool)
                for t in tiles:
                    for i in range(2):
                        pool.indirect_dma_start(
                            x_rows, bass.IndirectOffsetOnAxis(ap=rows_i[:, i, t:t + 1], axis=0),
                            xn[2][:, t, :], None).then_inc(rows_out, 16)

            def batch(b, par):
                prv2, prv, nxt, nxt2 = flags(b)
                for s in range(SLOTS):
                    if prv2 and s == 0:
                        row_inverse_std(b - 2, 1)
                    if nxt2 and s == 2:
                        inverse_std(b + 2)
                    if nxt2 and s == 4:
                        add_bias(b + 2)
                    if prv and s == 9:
                        row_inverse_std(b - 1, 0)
                    if nxt2 and 10 <= s < 14:
                        first_rest(b + 2, s - 10)
                    if nxt2 and 11 <= s < 15:
                        third_part(b + 2, s - 11)
                    if prv2 and s >= 12:
                        scatter_rows(b - 2, [s - 12])

            pool.memset(minus_half[:], -0.5).then_inc(half_set, 1)
            pool.wait_ge(half_set, 1)
            pool.wait_ge(w_in, 16 * 10)
            for a in range(2):
                inverse_std(a)
            for a in range(2):
                add_bias(a)
            for a in range(2):
                for c in range(5):
                    if c < 4:
                        first_rest(a, c)
                    if c > 0:
                        third_part(a, c - 1)
            batch(0, 0)
            batch(1, 1)
            with pool.Fori(0, 2) as i:
                for u in range(2):
                    batch(2 * i + 2 + u, u)
            batch(6, 0)
            batch(7, 1)

            row_inverse_std(B - 2, 1)
            row_inverse_std(B - 1, 0)
            scatter_rows(B - 2)
            row_inverse_std(B - 1, 1)
            scatter_rows(B - 1)
            pool.wait_ge(zero_done, 1)
            pool.wait_ge(zeros_set, 1)
            for e in range(E):
                pool.indirect_dma_start(
                    x_rows, bass.IndirectOffsetOnAxis(ap=zero_i[:, e:e + 1], axis=0), zeros[:],
                    None).then_inc(zero_out, 16)

            def fetch_results(b):
                pool.wait_ge(now_done, b + 1)
                apart(pool)
                for t in range(TB):
                    if not (isinstance(b, int) and b == 0):
                        pool.wait_ge(add2_done, TB * (b - 1) + t + 1)
                        apart(pool)
                    for i in range(2):
                        pool.indirect_dma_start(
                            got[:, t, i, :], None, y_rows,
                            bass.IndirectOffsetOnAxis(ap=result_now[:, i, t:t + 1], axis=0)
                        ).then_inc(got_in[t], 16)

            for u in range(RING):
                pool.wait_ge(yt_out[u], 16 * (TILES // RING))
            fetch_results(0)
            with pool.Fori(1, B) as b:
                fetch_results(b)


def kernel(x, ctx_1024, L0_attn_qkv_w, L0_attn_qkv_b, L0_attn_proj_w, L0_attn_proj_b,
           L0_ffn_w_router, L0_ffn_w1_stack, L0_ffn_w2_stack, L0_ffn_ws1, L0_ffn_ws2):
    import numpy as np
    import concourse.bacc as bacc
    from concourse.bass_utils import run_bass_kernel_spmd

    qkv_w, proj_w = np.asarray(L0_attn_qkv_w), np.asarray(L0_attn_proj_w)
    qkv_b = np.asarray(L0_attn_qkv_b)
    p, e = np.arange(P, dtype=np.float32), np.arange(E, dtype=np.float32)
    const = np.concatenate([
        np.broadcast_to(E - e, (P, TB, E)).reshape(P, TB * E),
        np.broadcast_to(e * ROOM, (P, E)), e * ROOM + p[:, None],
        np.broadcast_to(P * np.arange(B * TB, dtype=np.float32), (P, B * TB)),
        np.broadcast_to((e <= e[:, None]).astype(np.float32).reshape(E * E), (P, E * E)),
    ], axis=1).astype(np.float32)
    tri = np.stack([np.triu(np.ones((P, P), np.float32), 1), np.ones((P, P), np.float32)], axis=1)

    def chunks(w):
        w = np.asarray(w)
        w = w.reshape(*w.shape[:-2], w.shape[-2] // P, P, w.shape[-1])
        return np.moveaxis(w, -2, 0)

    def turned(w):
        return np.swapaxes(np.asarray(w), -1, -2)

    ctx = np.asarray(ctx_1024)
    ins = {
        "x": np.asarray(x), "ctx_n": ctx.transpose(1, 0, 2),
        "ctx_t": chunks(turned(ctx)),
        "wqk_t": chunks(qkv_w[:2 * D].T), "bqk": qkv_b[:2 * D].reshape(4, P).T,
        "wv_t": chunks(qkv_w[2 * D:].T), "bv": qkv_b[2 * D:],
        "wp_t": chunks(proj_w.T), "bp": np.asarray(L0_attn_proj_b),
        "wr_t": chunks(turned(L0_ffn_w_router)),
        "w1_t": chunks(turned(L0_ffn_w1_stack)), "w2_t": chunks(turned(L0_ffn_w2_stack)),
        "ws1_t": chunks(turned(L0_ffn_ws1)), "ws2_t": chunks(turned(L0_ffn_ws2)),
        "ident": np.eye(P, dtype=np.float32), "tri": tri, "const": const,
        "table": np.arange(TILES, dtype=np.float32)[None],
    }
    ins = {"in_" + n: np.ascontiguousarray(a) for n, a in ins.items()}
    nc = bacc.Bacc("TRN2", target_bir_lowering=False, num_devices=1)
    args = [nc.dram_tensor(n, a.shape, F32, kind="ExternalInput").ap() for n, a in ins.items()]
    out = nc.dram_tensor("out", (B, S, D), F32, kind="ExternalOutput").ap()
    decoder_layer(nc, *args, out)
    r = run_bass_kernel_spmd(nc, [ins], core_ids=[0])
    return r.results[0]["out"]
```

```python
from contextlib import ExitStack

import concourse.bass as bass
from concourse import mybir

F32 = mybir.dt.float32
BF16 = mybir.dt.bfloat16
F32R = mybir.dt.float32r
I32 = mybir.dt.int32
ALU = mybir.AluOpType
ACT = mybir.ActivationFunctionType
AX = mybir.AxisListType

B, S, D = 8, 512, 256
H, HD = 16, 16
P = 128
TB = S // P
KD = D // P
GH = 4
NG = H // GH
NSB = 3
SLOTS = NG * TB
AHEAD = 7
PARTS_Q = (0, 0, 0, 1, 1, 2)
PARTS_K = (0, 1, 2, 0, 1, 0)
NS = len(PARTS_Q)
KS_ROWS = NS * HD
KM_ROWS = KS_ROWS + 2
SC = 64
E, F = 8, 256
FS = 512
NFS = FS // P
ROOM = B * S + P
TILES = B * S * 2 // P + E
RING = 4
LAG = 2
ROUTE_STEPS = 18
HB = S // 2
EPS = 1e-5


C_FIRST = TB * E
C_STEPS = C_FIRST + E
C_UPTO = C_STEPS + B * TB
NCONST = C_UPTO + E * E


def decoder_layer(nc, x, ctx_n, ctx_t, wqk_t, bqk, wv_t, bv, wp_t, bp, wr_t, w1_t, w2_t, ws1_t,
                  ws2_t, ident_d, tri_d, const_d, table_d, out):
    scratch = nc.dram_tensor("qk_parts", [2, 3, 4, P, S], BF16).ap()
    x_rows = nc.dram_tensor("x_rows", [E * ROOM, D], F32).ap()
    y_rows = nc.dram_tensor("y_rows", [TILES * P, D], F32).ap()
    x_turned = nc.dram_tensor("x_turned", [B, P, KD, S], F32).ap()
    with ExitStack() as stack:
        def sem(name):
            return stack.enter_context(nc.semaphore(name))

        bank = [stack.enter_context(nc.psum_tensor(f"bank{i}", [P, 512], F32)) for i in range(8)]

        mid, end = bank[3], bank[7]

        def sb(name, shape, dt=F32):
            return stack.enter_context(nc.sbuf_tensor(name, shape, dt))

        xs = sb("xs", [P, B * TB, D])
        ident = sb("ident", [P, P])
        tri = sb("tri", [P, 2, P], BF16)
        const = sb("const", [P, NCONST])
        rank = const[:, 0:TB * E].rearrange("p (t e) -> p t e", e=E)
        first = const[:, C_FIRST:C_FIRST + E]
        steps = const[:, C_STEPS:C_STEPS + B * TB]
        upto = const[:, C_UPTO:C_UPTO + E * E].rearrange("p (a b) -> p a b", b=E)
        chosen = sb("chosen", [P, 2, B * TB, E])
        place = sb("place", [P, 2, B * TB])
        weight = sb("weight", [P, 2, B * TB])
        next_row = sb("next_row", [P, E])
        minus_half = sb("minus_half", [P, TB])
        px = sb("px", [P, TB, SC])
        xm = sb("xm", [P, TB])
        xb = sb("xb", [P, TB])
        xsum = sb("xsum", [P, TB])
        xr = sb("xr", [P, TB])
        rt = {n: sb("rt_" + n, [P, TB, E]) for n in
              ("d", "e", "eq1", "s1", "oh1", "e2", "eq2", "s2", "oh2", "row", "p1", "p2")}
        rc = {n: sb("rc_" + n, [P, TB]) for n in ("m", "m1", "sm1", "m2", "sm2", "den", "r")}
        oh = sb("oh", [P, TB, E], BF16)
        rows_i = sb("rows_i", [P, 2, TB], I32)
        zero_i = sb("zero_i", [1, E], I32)
        zeros = sb("zeros", [P, D])
        st = [sb(f"st{i}", [P, TB, 6]) for i in range(2)]
        mv = [sb(f"mv{i}", [P, TB, 2]) for i in range(2)]
        var = [sb(f"var{i}", [P, TB]) for i in range(2)]
        rstd = [sb(f"rstd{i}", [P, TB]) for i in range(2)]
        offset = [sb(f"offset{i}", [P, TB]) for i in range(2)]
        expert_i = sb("expert_i", [1, TILES], I32)
        row_i = sb("row_i", [1, TILES], I32)
        result_i = sb("result_i", [P, 2, B * TB], I32)
        result_now = sb("result_now", [P, 2, 2, TB], I32)
        tiles = sb("tiles", [P, E])
        incl = sb("incl", [P, E])
        excl = sb("excl", [P, E])
        shift = sb("shift", [P, E])
        counted = sb("counted", [P, E])

        with ExitStack() as phase:
            def sb1(name, shape, dt=F32):
                return phase.enter_context(nc.sbuf_tensor(name, shape, dt))

            QS, KS = [None] * 2, [None] * 2
            for i in range(2):
                QS[i] = sb1(f"QS{i}", [P, H, S], BF16)
                KS[i] = sb1(f"KS{i}", [P, H, S], BF16)
            VO = [sb1(f"VO{i}", [P, TB, H, 32]) for i in range(2)]
            probs = sb1("probs", [P, 2, GH, S])
            qk = sb1("qk", [P, 2, S])
            rest = sb1("rest", [P, 2, S])
            parts = sb1("parts", [P, 3, 4, S], BF16)
            xn, xnT = [sb1("xn0", [P, TB, D])], [sb1("xnT0", [P, KD, S])]
            xn += [sb1(f"xn{i}", [P, TB, D]) for i in range(1, 3)]
            xnT += [sb1("xnT1", [P, KD, S])]
            xrT = sb1("xrT", [P, KD, S])
            wqk = sb1("wqk", [P, KD, 2 * D])
            bqks = sb1("bqks", [P, 4])
            wv = sb1("wv", [P, KD, D])
            bvs = sb1("bvs", [P, D])
            wp = sb1("wp", [P, KD, D])
            bps = sb1("bps", [P, D])
            mneg = sb1("mneg", [P, 2, GH * TB])
            mparts = sb1("mparts", [GH * TB, 2, 2, P], BF16)
            o_sb = sb1("o_sb", [P, S])
            rden = sb1("rden", [P, TB, GH])
            o_nat = sb1("o_nat", [P, TB, D])
            oT = sb1("oT", [P, KD, S])
            pT = sb1("pT", [P, S])
            ctxT = sb1("ctxT", [P, KD, SC])
            ctxN = sb1("ctxN", [SC, D])
            wr = sb1("wr", [P, KD, E])
            tri_f = sb1("tri_f", [P, 2, P])
        raws = ExitStack()
        w1raw = raws.enter_context(nc.sbuf_tensor("w1raw", [P, E, KD, F], F32))
        w2raw = raws.enter_context(nc.sbuf_tensor("w2raw", [P, E, KD, F], F32))
        raws.close()
        ws1 = [sb(f"ws1_{i}", [P, KD, FS], F32R) for i in range(2)]
        ws2 = [sb(f"ws2_{i}", [P, NFS, D], F32R) for i in range(2)]
        hs = [sb(f"hs{i}", [P, 2, NFS, HB], F32R) for i in range(2)]
        w1 = [sb(f"w1_{i}", [P, E, KD, F], F32R) for i in range(2)]
        w2 = [sb(f"w2_{i}", [P, E, KD, F], F32R) for i in range(2)]
        wsraw = sb("wsraw", [P, 2, 2 * FS])
        got = sb("got", [P, RING, 2, D])
        fin_a = sb("fin_a", [P, B * TB, E])
        fin_b = sb("fin_b", [P, B * TB, E])
        fin_c = sb("fin_c", [P, 2, B * TB])
        tab_t = sb("tab_t", [1, TILES])
        tab_a = sb("tab_a", [1, TILES, E])
        tab_b = sb("tab_b", [1, TILES, E])
        tab_c = sb("tab_c", [1, 2, TILES])
        tab_0 = sb("tab_0", [1, TILES])
        tab_n = sb("tab_n", [1, 2])
        xt = sb("xt", [P, RING, D])
        yt = sb("yt", [P, RING, D])
        xT2 = [sb(f"xT2_{i}", [P, 2, KD, P], F32R) for i in range(2)]
        relu_t = sb("relu_t", [P, 2, F])
        sq_t = sb("sq_t", [P, 2, F])
        hT2 = [sb(f"hT2_{i}", [P, 2, F // P, P], F32R) for i in range(2)]
        xs3 = sb("xs3", [P, 2, KD, HB])
        xs2 = [sb(f"xs2_{i}", [P, 2, KD, HB], F32R) for i in range(2)]
        relu_s = sb("relu_s", [P, NFS, HB])
        sq_s = sb("sq_s", [P, NFS, HB])

        x_in = [sem(f"x_in{i}") for i in range(B)]
        w_in = sem("w_in")
        init = sem("init"); ones_in = sem("ones_in")
        bn_done = sem("bn_done"); mv_done = sem("mv_done")
        rstd_done = sem("rstd_done"); norm_done = sem("norm_done"); xb_done = sem("xb_done")
        tr_done = sem("tr_done"); xnT_done = sem("xnT_done")
        qkmm_done = sem("qkmm_done"); qk_done = sem("qk_done"); q1_done = sem("q1_done")
        r1_done = sem("r1_done"); q2_done = sem("q2_done"); q3_done = sem("q3_done")
        scr_out = sem("scr_out"); stack_in = sem("stack_in")
        vmm_done = sem("vmm_done"); v_done = sem("v_done")
        mx_ready = sem("mx_ready"); max_done = sem("max_done")
        tm_done = sem("tm_done"); m1_done = sem("m1_done"); m2_done = sem("m2_done")
        mrow_in = [sem(f"mrow_in{i}") for i in range(2)]
        s_ready = sem("s_ready"); exp_done = sem("exp_done"); pv_done = sem("pv_done")
        o_done = sem("o_done"); turn_done = sem("turn_done"); rden_done = sem("rden_done")
        on_done = sem("on_done"); ont_done = sem("ont_done"); oT_done = sem("oT_done")
        pj_done = sem("pj_done"); x1_done = sem("x1_done")
        tri_set = sem("tri_set"); half_set = sem("half_set"); zeros_set = sem("zeros_set")
        var_done = sem("var_done"); offset_done = sem("offset_done"); f_offset = sem("f_offset")
        ctx_in = sem("ctx_in")
        f_bn = sem("f_bn"); f_mv = sem("f_mv"); f_var = sem("f_var"); f_rstd = sem("f_rstd")
        f_norm = sem("f_norm"); f_tr = sem("f_tr"); f_T = sem("f_T")
        lg_done = sem("lg_done"); xm_done = sem("xm_done"); px_done = sem("px_done")
        xr_done = sem("xr_done"); pt_done = sem("pt_done"); pT_done = sem("pT_done")
        xpv_done = sem("xpv_done"); x2_done = sem("x2_done"); turned_out = sem("turned_out")
        rt_mm = sem("rt_mm"); rt_d = sem("rt_d"); rt_e = sem("rt_e"); rt_step = sem("rt_step")
        oh_done = sem("oh_done"); rk_mm = sem("rk_mm"); rk_step = sem("rk_step")
        pos_step = sem("pos_step")
        rows_done = sem("rows_done"); rows_out = sem("rows_out")
        fin_step = sem("fin_step"); zero_done = sem("zero_done"); zero_out = sem("zero_out")
        table_done = sem("table_done")
        table_in = sem("table_in"); ws_in = sem("ws_in"); w1_in = sem("w1_in"); w2_in = sem("w2_in")
        w1_hi = sem("w1_hi"); w1_lo = sem("w1_lo"); w2_hi = sem("w2_hi"); w2_lo = sem("w2_lo")
        ws_hi = sem("ws_hi"); ws_lo = sem("ws_lo")
        xt_in = [sem(f"xt_in{i}") for i in range(RING)]
        yt_out = [sem(f"yt_out{i}") for i in range(RING)]
        tx_done = sem("tx_done"); xth_done = sem("xth_done"); xtl_done = sem("xtl_done")
        l1_done = sem("l1_done"); relut_done = sem("relut_done"); sqt_done = sem("sqt_done")
        th_done = sem("th_done"); hth_done = sem("hth_done"); htl_done = sem("htl_done")
        l2_done = sem("l2_done"); yt_done = sem("yt_done")
        xs3_in = [sem(f"xs3_in{i}") for i in range(2)]
        xsh_done = sem("xsh_done"); xsl_done = sem("xsl_done")
        up_done = sem("up_done"); relus_done = sem("relus_done"); sqs_done = sem("sqs_done")
        hsh_done = sem("hsh_done"); hsl_done = sem("hsl_done"); down_done = sem("down_done")
        now_done = sem("now_done"); got_in = [sem(f"got_in{i}") for i in range(RING)]
        shared_done = sem("shared_done"); add1_done = sem("add1_done"); add2_done = sem("add2_done")
        out_done = sem("out_done")

        def flags(b):
            if isinstance(b, int):
                return b >= 2, b >= 1, b + 1 < B, b + 2 < B
            return True, True, True, True

        def tile(b, t, n=1):
            return xs[:, bass.ds(b * TB + t, n), :]

        def apart(eng):
            eng.nop(nofuse=True)

        def own_copy(eng, b):
            if isinstance(b, int):
                return b
            reg = eng.alloc_register()
            eng.reg_mov(reg, b)
            return eng.snap(reg, min_val=2, max_val=B - 3)

        def projected(a, i):
            return end if isinstance(a, int) and a < 2 and i % 2 else mid

        def value_place(a, i):
            return end if isinstance(a, int) and a == 0 and i % 2 else mid

        def either(a, i, usual):
            if isinstance(a, int) and a == B - 1 and i % 2:
                return mid if usual is end else end
            return usual

        def normed(a, r):
            return xn[1] if isinstance(a, int) and a == B - 1 else xn[1 + r]

        def finish(steps):
            for _ in steps:
                pass

        block = stack.enter_context(nc.Block())

        @block.sync
        def _(sp):
            for b in range(2):
                sp.dma_start(xs[:, b * TB:(b + 1) * TB, :], x[b].rearrange("(t p) d -> p t d", p=P)
                             ).then_inc(x_in[b], 16)
            for dst, src in (
                (ident[:], ident_d),
                (wqk[:], wqk_t), (bqks[:], bqk),
                (wv[:], wv_t),
                (wp[:], wp_t),
                (bvs[:], bv.partition_broadcast(P)), (bps[:], bp.partition_broadcast(P)),
                (const[:], const_d), (wr[:], wr_t), (tri_f[:], tri_d),
            ):
                sp.dma_start(dst, src).then_inc(w_in, 16)

            def scratch_out(a, par, c):
                sp.wait_ge(q3_done, 4 * a + c + 1)
                apart(sp)
                if c == 0 and not (isinstance(a, int) and a < 2):
                    sp.wait_ge(stack_in, 16 * 2 * NS * (a - 1))
                apart(sp)
                sp.dma_start(scratch[par, :, c].rearrange("n p s -> p n s"), parts[:, :, c, :]
                             ).then_inc(scr_out, 16)

            def stack_load(a, par):
                sp.wait_ge(scr_out, 64 * (a + 1))
                apart(sp)
                if not (isinstance(a, int) and a < 2):
                    sp.wait_ge(s_ready, 64 * (a - 1))
                apart(sp)
                for n in range(NS):
                    for dst, part, c in ((QS, PARTS_Q[n], 0), (KS, PARTS_K[n], 2)):
                        src = scratch[par, part, c:c + 2].rearrange(
                            "c (h d) s -> d (c h) s", d=HD)
                        sp.dma_start(dst[par][n * HD:(n + 1) * HD, :, :], src
                                     ).then_inc(stack_in, 16)

            def max_rows(a, par, g):
                sp.wait_ge(m2_done, NG * a + g + 1)
                apart(sp)
                for n in range(2):
                    sp.dma_start(QS[par][KS_ROWS + n:KS_ROWS + n + 1, g * GH:(g + 1) * GH, :],
                                 mparts[:, g % 2, n, :]).then_inc(mrow_in[g % 2], 16)

            def context_load(a):
                if not (isinstance(a, int) and a == 0):
                    sp.wait_ge(lg_done, a)
                    apart(sp)
                    sp.wait_ge(xpv_done, 2 * a)
                    apart(sp)
                sp.dma_start(ctxT[:], ctx_t[:, bass.ds(a, 1)].rearrange("p o k s -> p (o k) s")
                             ).then_inc(ctx_in, 16)
                sp.dma_start(ctxN[:], ctx_n[:, bass.ds(a, 1)].rearrange("p o d -> p (o d)")
                             ).then_inc(ctx_in, 16)

            def turned_store(a):
                sp.wait_ge(f_T, KD * (2 * a + 2))
                apart(sp)
                sp.dma_start(x_turned[bass.ds(a, 1)].rearrange("o p k s -> p (o k) s"), xrT[:]
                             ).then_inc(turned_out, 16)

            def batch(b, par):
                prv2, prv, nxt, nxt2 = flags(b)
                if nxt:
                    stack_load(b + 1, 1 - par)
                max_rows(b, par, 1)
                if prv2:
                    turned_store(b - 2)
                if prv:
                    context_load(b - 1)
                max_rows(b, par, 2)
                max_rows(b, par, 3)
                if nxt2:
                    for c in range(3):
                        scratch_out(b + 2, par, c)
                if nxt:
                    max_rows(b + 1, 1 - par, 0)
                if nxt2:
                    scratch_out(b + 2, par, 3)

            sp.wait_ge(tri_set, 1)
            for i in range(2):
                sp.dma_start(KS[i][KS_ROWS:KM_ROWS], tri[:, 1, :]).then_inc(ones_in, 16)
            for c in range(4):
                scratch_out(0, 0, c)
            stack_load(0, 0)
            for c in range(4):
                scratch_out(1, 1, c)
            for b in range(2, B):
                sp.dma_start(xs[:, b * TB:(b + 1) * TB, :], x[b].rearrange("(t p) d -> p t d", p=P)
                             ).then_inc(x_in[b], 16)
            max_rows(0, 0, 0)
            batch(0, 0)
            batch(1, 1)
            with sp.Fori(0, 2) as i:
                for u in range(2):
                    batch(2 * i + 2 + u, u)
            sp.wait_ge(q3_done, 4 * B)
            sp.dma_start(wsraw[:, 0, :], ws1_t.rearrange("p k f -> p (k f)")).then_inc(ws_in, 16)
            sp.dma_start(wsraw[:, 1, :], ws2_t.rearrange("p k f -> p (k f)")).then_inc(ws_in, 16)
            batch(6, 0)
            sp.wait_ge(s_ready, 64 * 7)
            sp.dma_start(w1raw[:], w1_t).then_inc(w1_in, 16)
            sp.dma_start(w2raw[:], w2_t).then_inc(w2_in, 16)
            batch(7, 1)
            sp.wait_ge(vmm_done, 2 * B)
            sp.wait_ge(scr_out, 64 * B)
            sp.dma_start(tab_0[:], table_d).then_inc(table_in, 16)
            turned_store(B - 2)
            context_load(B - 1)
            turned_store(B - 1)
            sp.wait_ge(zero_done, 1)
            apart(sp)
            for e in range(E):
                row = sp.value_load(zero_i[0:1, e:e + 1], min_val=0, max_val=E * ROOM - P)
                sp.dma_start(x_rows[bass.ds(row, P), :], zeros[:]).then_inc(zero_out, 16)

            def tile_row(t):
                return sp.value_load(row_i[0:1, bass.ds(t, 1)], min_val=0,
                                     max_val=E * ROOM - P)

            def tile_load(t, u, row):
                if not (isinstance(t, int) and t < RING):
                    sp.wait_ge(tx_done, t - RING + 1)
                    apart(sp)
                sp.dma_start(xt[:, u, :], x_rows[bass.ds(row, P), :]).then_inc(xt_in[u], 16)

            def tile_store(t, i, u):
                sp.wait_ge(yt_done, t + 1)
                apart(sp)
                sp.dma_start(y_rows[bass.ds(P * t, P), :], yt[:, u, :]).then_inc(yt_out[u], 16)

            def half_load(b, h):
                if not (isinstance(b, int) and b == 0):
                    sp.wait_ge(xsl_done, 2 * b + h - 1)
                    apart(sp)
                src = x_turned[bass.ds(b, 1)].rearrange("o p k s -> p (o k) s")
                sp.dma_start(xs3[:, h], src[:, :, h * HB:(h + 1) * HB]).then_inc(xs3_in[h], 16)

            sp.wait_ge(table_done, 1)
            apart(sp)
            rows = [tile_row(t) for t in range(RING)]
            sp.wait_ge(zero_out, 16 * E)
            sp.wait_ge(turned_out, 16 * B)
            sp.wait_ge(rt_mm, B)
            sp.wait_ge(rows_out, 16 * 2 * TB * B)
            for t in range(RING):
                tile_load(t, t, rows[t])
            for h in range(2):
                half_load(0, h)
            for t in range(RING, 2 * RING):
                tile_load(t, t - RING, tile_row(t))
                if t - RING >= LAG:
                    tile_store(t - RING - LAG, 0, t - RING - LAG)
            with sp.Fori(1, TILES // RING - 1) as i:
                for u in range(RING):
                    tile_load(RING * i + u + RING, u, tile_row(RING * i + u + RING))
                    tile_store(RING * i + u - LAG, i, (u - LAG) % RING)
            for t in range(TILES - RING - LAG, TILES):
                tile_store(t, t // RING, t % RING)

            def block_out(b):
                sp.wait_ge(add2_done, TB * (b + 1))
                apart(sp)
                sp.dma_start(out[bass.ds(b, 1)].rearrange("o (t p) d -> p (o t) d", p=P),
                             tile(b, 0, TB)).then_inc(out_done, 16)

            for h in range(2):
                half_load(1, h)
            with sp.Fori(0, B - 2) as b:
                for h in range(2):
                    half_load(b + 2, h)
                block_out(b)
            for b in range(B - 2, B):
                block_out(b)
            sp.wait_ge(out_done, 16 * B)

        @block.tensor
        def _(pe):
            def misc_free(prev):
                if prev:
                    pe.wait_ge(prev[0], prev[1])

            def transposes(a, k, prev):
                pe.wait_ge(norm_done, TB * (a + 1))
                misc_free(prev)
                for t in range(TB):
                    mm = pe.transpose(projected(a, k)[:, t * P:(t + 1) * P],
                                      xn[0][:, t, k * P:(k + 1) * P],
                                      ident[:])
                mm.then_inc(tr_done, 1)
                return xnT_done, KD * a + k + 1

            def project_qk(a, c, prev):
                pe.wait_ge(xnT_done, KD * (a + 1))
                misc_free(prev)
                for k in range(KD):
                    mm = pe.matmul(projected(a, c)[:], wqk[:, k, c * P:(c + 1) * P],
                                   xnT[0][:, k, :],
                                   start=(k == 0), stop=(k == KD - 1))
                mm.then_inc(qkmm_done, 1)
                return qk_done, 4 * a + c + 1

            def project_v(a, i, prev):
                misc_free(prev)
                for t in range(2):
                    for k in range(KD):
                        mm = pe.matmul(value_place(a, i)[:, t * D:(t + 1) * D],
                                       xnT[0][:, k, (2 * i + t) * P:(2 * i + t + 1) * P],
                                       wv[:, k, :], start=(k == 0), stop=(k == KD - 1))
                mm.then_inc(vmm_done, 1)
                return v_done, 4 * a + 2 * i + 2

            def max_scores(a, par, m):
                if m == 0:
                    pe.wait_ge(stack_in, 16 * 2 * NS * (a + 1))
                for q in range(TB):
                    n = 4 * m + q
                    if not (isinstance(a, int) and a == 0 and n < 2):
                        pe.wait_ge(max_done, 64 * a + n - 1)
                    pe.matmul(bank[4 + n % 2][:], QS[par][0:KS_ROWS, m, q * P:(q + 1) * P],
                              KS[par][0:KS_ROWS, m, :], start=True, stop=True
                              ).then_inc(mx_ready, 1)
                    yield

            def turn_max(a, g, prev):
                pe.wait_ge(max_done, 64 * a + 16 * (g + 1))
                misc_free(prev)
                pe.transpose(end[0:GH * TB, 0:P], mneg[:, g % 2, :], ident[:]
                             ).then_inc(tm_done, 1)
                return m2_done, NG * a + g + 1

            def turn_sums(b, g, prev):
                pe.wait_ge(o_done, NG * b + g + 1)
                misc_free(prev)
                for t in range(TB):
                    mm = pe.transpose(end[:, t * P:(t + 1) * P], o_sb[:, t * P:(t + 1) * P],
                                      ident[:])
                mm.then_inc(turn_done, 1)
                return on_done, NG * b + g + 1

            def turn_heads(b, k, prev):
                pe.wait_ge(on_done, NG * (b + 1))
                misc_free(prev)
                for t in range(TB):
                    mm = pe.transpose(either(b, k, end)[:, t * P:(t + 1) * P],
                                      o_nat[:, t, k * P:(k + 1) * P], ident[:])
                mm.then_inc(ont_done, 1)
                return oT_done, KD * b + k + 1

            def project_out(b, i, prev):
                pe.wait_ge(oT_done, KD * (b + 1))
                misc_free(prev)
                for t in range(2):
                    for k in range(KD):
                        mm = pe.matmul(either(b, i, end)[:, t * D:(t + 1) * D],
                                       oT[:, k, (2 * i + t) * P:(2 * i + t + 1) * P],
                                       wp[:, k, :], start=(k == 0), stop=(k == KD - 1))
                mm.then_inc(pj_done, 1)
                return x1_done, 2 * b + i + 1

            def scores(b, par, s, j):
                g, kb = divmod(s, TB)
                if kb == 0 and j == 0:
                    pe.wait_ge(mrow_in[g % 2], 32 * (2 * b + g // 2 + 1))
                    if isinstance(b, int) and b == 0 and g == 0:
                        pe.wait_ge(ones_in, 32)
                n = GH * s + j
                last = n - NSB if n >= NSB else (n - 1) % NSB - NSB
                if not (isinstance(b, int) and b == 0 and last < 0):
                    pe.wait_ge(exp_done, 64 * b + last + 1)
                h = g * GH + j
                pe.matmul(bank[n % NSB][:], KS[par][0:KM_ROWS, h, kb * P:(kb + 1) * P],
                          QS[par][0:KM_ROWS, h, :], start=True, stop=True).then_inc(s_ready, 1)

            def values(b, par, s):
                g, kb = divmod(s, TB)
                pe.wait_ge(exp_done, 64 * b + 4 * s + 4)
                if s == 0:
                    pe.wait_ge(v_done, 4 * (b + 1))
                if kb == 0 and not (isinstance(b, int) and b == 0 and s == 0):
                    pe.wait_ge(o_done, NG * b + g)
                for j in range(GH):
                    mm = pe.matmul(bank[6][32 * j:32 * j + 32, :], VO[par][:, kb, g * GH + j, :],
                                   probs[:, kb % 2, j, :], start=(kb == 0), stop=(kb == TB - 1))
                mm.then_inc(pv_done, 1)

            def front_transposes(a, r, k, prev):
                pe.wait_ge(f_norm, TB * (2 * a + r + 1))
                misc_free(prev)
                for t in range(TB):
                    mm = pe.transpose(either(a, k, (end, mid)[r])[:, t * P:(t + 1) * P],
                                      normed(a, r)[:, t, k * P:(k + 1) * P], ident[:])
                mm.then_inc(f_tr, 1)
                return f_T, KD * (2 * a + r) + k + 1

            def context_logits(a, prev):
                pe.wait_ge(f_T, KD * (2 * a + 1))
                pe.wait_ge(ctx_in, 32 * (a + 1))
                misc_free(prev)
                for t in range(TB):
                    for k in range(KD):
                        mm = pe.matmul(mid[:, t * SC:(t + 1) * SC],
                                       xnT[1][:, k, t * P:(t + 1) * P], ctxT[:, k, :],
                                       start=(k == 0), stop=(k == KD - 1))
                mm.then_inc(lg_done, 1)
                return px_done, TB * (a + 1)

            def turn_probs(a, prev):
                pe.wait_ge(px_done, TB * (a + 1))
                misc_free(prev)
                apart(pe)
                for t in range(TB):
                    mm = pe.transpose(mid[0:SC, t * P:(t + 1) * P], px[:, t, :], ident[:])
                mm.then_inc(pt_done, 1)
                return pT_done, a + 1

            def context_values(a, i, prev):
                pe.wait_ge(pT_done, a + 1)
                misc_free(prev)
                for t in (2 * i, 2 * i + 1):
                    mm = pe.matmul((mid, end)[i][:, t % 2 * D:(t % 2 + 1) * D],
                                   pT[0:SC, t * P:(t + 1) * P], ctxN[:],
                                   start=True, stop=True)
                mm.then_inc(xpv_done, 1)
                return x2_done, TB * a + 2 * i + 2

            def router(a, prev):
                pe.wait_ge(f_T, KD * (2 * a + 2))
                misc_free(prev)
                for t in range(TB):
                    for k in range(KD):
                        mm = pe.matmul(mid[:, t * E:(t + 1) * E],
                                       xrT[:, k, t * P:(t + 1) * P], wr[:, k, :],
                                       start=(k == 0), stop=(k == KD - 1))
                mm.then_inc(rt_mm, 1)
                return rt_d, a + 1

            def count_rows(a, prev):
                pe.wait_ge(oh_done, a + 1)
                misc_free(prev)
                for t in range(TB + 1):
                    dst = end[:, t * E:(t + 1) * E]
                    for v in range(min(t, TB - 1) + 1):
                        mm = pe.matmul(dst, tri[:, 0 if v == t else 1, :], oh[:, v, :],
                                       start=(v == 0), stop=(v == min(t, TB - 1)))
                mm.then_inc(rk_mm, 1)
                return rk_step, 2 * (a + 1)

            def batch(b, par):
                prv2, prv, nxt, nxt2 = flags(b)
                in_mid, in_end = last
                if prv2:
                    in_mid = x2_done, TB * (b - 2) + 2
                    in_end = x2_done, TB * (b - 1)
                for s in range(SLOTS):
                    if s % 4 == 0:
                        b = own_copy(pe, b)
                    m = s + AHEAD
                    ahead = iter(())
                    if m < SLOTS:
                        ahead = max_scores(b, par, m)
                    elif nxt:
                        ahead = max_scores(b + 1, 1 - par, m - SLOTS)
                    for j in range(GH):
                        scores(b, par, s, j)
                        next(ahead, None)
                        if j == 1:
                            if s > 0:
                                values(b, par, s - 1)
                            elif prv:
                                values(b - 1, 1 - par, SLOTS - 1)
                            if prv2 and s == 10:
                                in_end = count_rows(b - 2, in_end)
                        if j == 2:
                            if prv2 and s in (2, 3):
                                in_mid = front_transposes(b - 2, 1, s - 2, in_mid)
                            if prv2 and s == 4:
                                in_mid = router(b - 2, in_mid)
                            if nxt and s in (5, 6):
                                in_mid = project_v(b + 1, s - 5, in_mid)
                            if nxt2 and s in (7, 8):
                                in_mid = transposes(b + 2, s - 7, in_mid)
                            if nxt2 and 9 <= s < 13:
                                in_mid = project_qk(b + 2, s - 9, in_mid)
                            if prv and s == 13:
                                in_mid = context_logits(b - 1, in_mid)
                            if prv and s == 14:
                                in_mid = turn_probs(b - 1, in_mid)
                            if prv and s == 15:
                                in_mid = context_values(b - 1, 0, in_mid)
                    if s % 4 == 1:
                        g = s // 4 + 1
                        if g < NG:
                            in_end = turn_max(b, g, in_end)
                        elif nxt:
                            in_end = turn_max(b + 1, 0, in_end)
                    if s % 4 == 2:
                        if s > 2:
                            in_end = turn_sums(b, s // 4 - 1, in_end)
                        elif prv:
                            in_end = turn_sums(b - 1, NG - 1, in_end)
                    if prv and s in (3, 4):
                        in_end = turn_heads(b - 1, s - 3, in_end)
                    if prv and s in (7, 8):
                        in_end = project_out(b - 1, s - 7, in_end)
                    if prv and s in (11, 12):
                        in_end = front_transposes(b - 1, 0, s - 11, in_end)
                    if prv and s == 15:
                        in_end = context_values(b - 1, 1, in_end)
                return in_mid, in_end

            pe.wait_ge(w_in, 16 * 10)
            used = [None, None]
            for a in range(2):
                for k in range(KD):
                    used[k % 2] = transposes(a, k, used[k % 2])
                for c in range(4):
                    used[c % 2] = project_qk(a, c, used[c % 2])
                if a == 0:
                    for i in range(2):
                        used[i % 2] = project_v(0, i, used[i % 2])
            in_mid, in_end = used
            for m in range(AHEAD):
                for _ in max_scores(0, 0, m):
                    pass
                if m == 4:
                    in_end = turn_max(0, 0, in_end)
            last = in_mid, in_end
            last = batch(0, 0)
            last = batch(1, 1)
            with pe.Fori(0, 2) as i:
                for u in range(2):
                    batch(2 * i + 2 + u, u)
            batch(6, 0)
            in_mid, in_end = batch(7, 1)

            values(B - 1, 1, SLOTS - 1)
            in_end = turn_sums(B - 1, NG - 1, in_end)
            in_end = turn_heads(B - 1, 0, in_end)
            in_mid = turn_heads(B - 1, 1, in_mid)
            in_end = project_out(B - 1, 0, in_end)
            in_mid = project_out(B - 1, 1, in_mid)
            for k in range(KD):
                in_mid = front_transposes(B - 2, 1, k, in_mid)
            in_mid = router(B - 2, in_mid)
            in_end = front_transposes(B - 1, 0, 0, in_end)
            in_mid = front_transposes(B - 1, 0, 1, in_mid)
            in_mid = context_logits(B - 1, in_mid)
            in_end = count_rows(B - 2, in_end)
            in_mid = turn_probs(B - 1, in_mid)
            in_mid = context_values(B - 1, 0, in_mid)
            in_end = context_values(B - 1, 1, in_end)
            in_mid = front_transposes(B - 1, 1, 0, in_mid)
            in_end = front_transposes(B - 1, 1, 1, in_end)
            in_mid = router(B - 1, in_mid)
            in_end = count_rows(B - 1, in_end)
            misc_free(in_mid)
            misc_free(in_end)

            def three_passes(dst, pairs):
                n = 0
                for a, b in pairs:
                    for i, j in ((0, 0), (0, 1), (1, 0)):
                        mm = pe.matmul(dst, a[i], b[j], start=(n == 0),
                                       stop=(n == 3 * len(pairs) - 1))
                        n += 1
                return mm

            def tile_turn(t, i, u):
                pe.wait_ge(xt_in[u % RING], 16 * (i + 1))
                if not (isinstance(t, int) and t < 2):
                    pe.wait_ge(xtl_done, t - 1)
                for k in range(KD):
                    mm = pe.transpose(bank[u % 2][:, k * P:(k + 1) * P],
                                      xt[:, u % RING, k * P:(k + 1) * P], ident[:])
                mm.then_inc(tx_done, 1)

            expert_of = [pe.alloc_register(name=f"expert{i}") for i in range(RING)]

            def load_expert(t, u):
                pe.load(expert_of[u % RING], expert_i[0:1, bass.ds(t, 1)])

            def tile_expert(u):
                return pe.snap(expert_of[u % RING], min_val=0, max_val=E - 1)

            def tile_up(t, u):
                pe.wait_ge(xtl_done, t + 1)
                if not (isinstance(t, int) and t < 2):
                    pe.wait_ge(relut_done, t - 1)
                e = tile_expert(u)
                three_passes(bank[2 + u % 2][:, 0:F], [
                    ([xT2[i][:, u % 2, k, :] for i in range(2)],
                     [w1[i][:, bass.ds(e, 1), k, :] for i in range(2)]) for k in range(KD)
                ]).then_inc(l1_done, 1)

            def tile_turn_hidden(t, u):
                pe.wait_ge(sqt_done, t + 1)
                if not (isinstance(t, int) and t < 2):
                    pe.wait_ge(htl_done, t - 1)
                for k in range(F // P):
                    mm = pe.transpose(bank[4 + u % 2][:, k * P:(k + 1) * P],
                                      sq_t[:, u % 2, k * P:(k + 1) * P], ident[:])
                mm.then_inc(th_done, 1)

            def tile_down(t, u):
                pe.wait_ge(htl_done, t + 1)
                if not (isinstance(t, int) and t < 2):
                    pe.wait_ge(yt_done, t - 1)
                e = tile_expert(u)
                three_passes(bank[6 + u % 2][:, 0:D], [
                    ([hT2[i][:, u % 2, k, :] for i in range(2)],
                     [w2[i][:, bass.ds(e, 1), k, :] for i in range(2)]) for k in range(F // P)
                ]).then_inc(l2_done, 1)

            def tile_step(s, i, u):
                if not (isinstance(s, int) and s + 1 >= TILES):
                    tile_turn(s + 1, i + (u == RING - 1), (u + 1) % RING)
                if not (isinstance(s, int) and s >= TILES):
                    tile_up(s, u)
                if not (isinstance(s, int) and not 1 <= s <= TILES):
                    tile_turn_hidden(s - 1, u + RING - 1)
                if not (isinstance(s, int) and s < 2):
                    tile_down(s - 2, u + RING - 2)
                    if not (isinstance(s, int) and s + RING - 2 >= TILES):
                        load_expert(s + RING - 2, u + RING - 2)

            pe.wait_ge(table_done, 1)
            tile_turn(0, 0, 0)
            for t in range(RING):
                load_expert(t, t)
            pe.wait_ge(w1_hi, 4)
            pe.wait_ge(w1_lo, 4)
            pe.wait_ge(w2_hi, 4)
            pe.wait_ge(w2_lo, 4)
            for s in range(2 * RING):
                tile_step(s, s // RING, s % RING)
            with pe.Fori(1, TILES // RING // 2 - 1) as k:
                for i in (2 * k, 2 * k + 1):
                    for u in range(RING):
                        tile_step(RING * i + u, i, u)
            for s in range(TILES - 2 * RING, TILES + 2):
                tile_step(s, s // RING, s % RING)

            def shared_up(b, h):
                pe.wait_ge(xsl_done, 2 * b + h + 1)
                for c in range(NFS):
                    if not (isinstance(b, int) and b == 0 and h == 0):
                        pe.wait_ge(relus_done, NFS * (2 * b + h - 1) + c + 1)
                    three_passes(bank[c][:, 0:HB], [
                        ([ws1[i][:, k, c * P:(c + 1) * P] for i in range(2)],
                         [xs2[i][:, h, k, :] for i in range(2)]) for k in range(KD)
                    ]).then_inc(up_done, 1)

            def shared_down(b, h):
                pe.wait_ge(hsl_done, NFS * (2 * b + h + 1))
                if not (isinstance(b, int) and b == 0):
                    pe.wait_ge(shared_done, 2 * b + h - 1)
                for t in range(2):
                    mm = three_passes(bank[4 + h][:, t * D:(t + 1) * D], [
                        ([hs[i][:, h, c, t * P:(t + 1) * P] for i in range(2)],
                         [ws2[i][:, c, :] for i in range(2)]) for c in range(NFS)])
                mm.then_inc(down_done, 1)

            pe.wait_ge(ws_hi, 2)
            pe.wait_ge(ws_lo, 2)
            pe.wait_ge(yt_done, TILES)
            pe.wait_ge(htl_done, TILES)
            for h in range(2):
                shared_up(0, h)

            def shared_block(b):
                for h in range(2):
                    shared_up(b, h)
                    shared_down(b - 1, h)

            shared_block(1)
            with pe.Fori(2, B) as b:
                shared_block(b)
            for h in range(2):
                shared_down(B - 1, h)

        @block.scalar
        def _(act):
            def norm(a):
                act.wait_ge(offset_done, a + 1)
                if not (isinstance(a, int) and a == 0):
                    act.wait_ge(tr_done, KD * a)
                apart(act)
                for t in range(TB):
                    act.activation(xn[0][:, t, :], tile(a, t)[:, 0], ACT.Identity,
                                   bias=offset[0][:, t:t + 1], scale=rstd[0][:, t:t + 1]
                                   ).then_inc(norm_done, 1)

            def row_norm(a, r):
                n = 2 * a + r
                act.wait_ge(f_offset, n + 1)
                if not (isinstance(a, int) and a == 0 and r == 0):
                    act.wait_ge(f_tr, KD * n)
                if r == 1 and not (isinstance(a, int) and a in (0, B - 1)):
                    act.wait_ge(rows_out, 16 * 2 * TB * a)
                apart(act)
                for t in range(TB):
                    act.activation(normed(a, r)[:, t, :], tile(a, t)[:, 0], ACT.Identity,
                                   bias=offset[1][:, t:t + 1], scale=rstd[1][:, t:t + 1]
                                   ).then_inc(f_norm, 1)

            def copy_xT(a, k):
                act.wait_ge(tr_done, KD * a + k + 1)
                if not (isinstance(a, int) and a == 0):
                    act.wait_ge(vmm_done, 2 * a)
                act.activation(xnT[0][:, k, :], projected(a, k)[:], ACT.Copy).then_inc(xnT_done, 1)

            def copy_qk(a, c):
                act.wait_ge(qkmm_done, 4 * a + c + 1)
                if not (isinstance(a, int) and a == 0 and c < 2):
                    act.wait_ge(r1_done, 4 * a + c - 1)
                act.activation(qk[:, c % 2, :], projected(a, c)[:], ACT.Identity,
                               bias=bqks[:, c:c + 1]).then_inc(qk_done, 1)

            def second_part(a, c):
                act.wait_ge(r1_done, 4 * a + c + 1)
                if not (isinstance(a, int) and a == 0):
                    act.wait_ge(scr_out, 64 * a)
                act.activation(parts[:, 1, c, :], rest[:, c % 2, :], ACT.Copy).then_inc(q2_done, 1)

            def copy_o(b, g):
                act.wait_ge(pv_done, SLOTS * b + TB * (g + 1))
                if not (isinstance(b, int) and b == 0 and g == 0):
                    act.wait_ge(turn_done, NG * b + g)
                act.activation(o_sb[:], bank[6][:], ACT.Copy).then_inc(o_done, 1)

            def copy_oT(b, k):
                act.wait_ge(ont_done, KD * b + k + 1)
                if not (isinstance(b, int) and b == 0):
                    act.wait_ge(pj_done, 2 * b)
                act.activation(oT[:, k, :], either(b, k, end)[:], ACT.Copy).then_inc(oT_done, 1)

            def copy_front(a, r, k):
                act.wait_ge(f_tr, KD * (2 * a + r) + k + 1)
                if r == 0:
                    if not (isinstance(a, int) and a == 0):
                        act.wait_ge(lg_done, a)
                    dst = xnT[1]
                else:
                    if not (isinstance(a, int) and a == 0):
                        act.wait_ge(rt_mm, a)
                        act.wait_ge(turned_out, 16 * a)
                    dst = xrT
                act.activation(dst[:, k, :], either(a, k, (end, mid)[r])[:], ACT.Copy
                               ).then_inc(f_T, 1)

            def context_probs(a):
                act.wait_ge(xm_done, 2 * a + 2)
                if not (isinstance(a, int) and a == 0):
                    act.wait_ge(pt_done, a)
                    act.wait_ge(xr_done, a)
                for t in range(TB):
                    act.activation(px[:, t, :], mid[:, t * SC:(t + 1) * SC], ACT.Exp,
                                   bias=xb[:, t:t + 1], scale=D ** -0.5,
                                   accum_out=xsum[:, t:t + 1]).then_inc(px_done, 1)

            def copy_probs(a):
                act.wait_ge(pt_done, a + 1)
                if not (isinstance(a, int) and a == 0):
                    act.wait_ge(xpv_done, 2 * a)
                act.activation(pT[0:SC, :], mid[0:SC, :], ACT.Copy).then_inc(pT_done, 1)

            def router_exp(a):
                act.wait_ge(rt_d, a + 1)
                if not (isinstance(a, int) and a == 0):
                    act.wait_ge(rt_step, ROUTE_STEPS * a)
                act.activation(rt["e"][:], rt["d"][:], ACT.Exp).then_inc(rt_e, 1)

            def batch(b, par):
                prv2, prv, nxt, nxt2 = flags(b)
                for s in range(SLOTS):
                    u = SLOTS * b + s
                    for j in range(GH):
                        act.wait_ge(s_ready, 64 * b + 4 * s + j + 1)
                        if j == 0 and not (isinstance(b, int) and b == 0 and s < 2):
                            act.wait_ge(pv_done, u - 1)
                        act.activation(probs[:, s % 2, j, :], bank[(GH * s + j) % NSB][:], ACT.Exp,
                                       scale=HD ** -0.5).then_inc(exp_done, 1)
                        if prv2 and s == 5 and j == 1:
                            router_exp(b - 2)
                    if prv2 and s == 1:
                        row_norm(b - 2, 1)
                    if nxt2 and s == 6:
                        norm(b + 2)
                    if prv and s == 10:
                        row_norm(b - 1, 0)
                    if prv2 and s in (2, 3):
                        copy_front(b - 2, 1, s - 2)
                    if nxt2 and s in (7, 8):
                        copy_xT(b + 2, s - 7)
                    if nxt2 and 9 <= s < 13:
                        copy_qk(b + 2, s - 9)
                    if nxt2 and 11 <= s < 15:
                        second_part(b + 2, s - 11)
                    if s % 4 == 0:
                        if s > 0:
                            copy_o(b, s // 4 - 1)
                        elif prv:
                            copy_o(b - 1, NG - 1)
                    if prv and s in (3, 4):
                        copy_oT(b - 1, s - 3)
                    if prv and s in (11, 12):
                        copy_front(b - 1, 0, s - 11)
                    if prv and s == 13:
                        context_probs(b - 1)
                    if prv and s == 14:
                        copy_probs(b - 1)

            for b in range(2):
                act.wait_ge(x_in[b], 16)
            norm(0)
            act.wait_ge(w_in, 16 * 10)
            for a in range(2):
                for k in range(KD):
                    copy_xT(a, k)
                if a == 0:
                    norm(1)
                for c in range(5):
                    if c < 4:
                        copy_qk(a, c)
                    if c > 0:
                        second_part(a, c - 1)
            batch(0, 0)
            batch(1, 1)
            with act.Fori(0, 2) as i:
                for u in range(2):
                    batch(2 * i + 2 + u, u)
            batch(6, 0)
            batch(7, 1)
            copy_o(B - 1, NG - 1)
            for k in range(KD):
                copy_oT(B - 1, k)
            row_norm(B - 2, 1)
            for k in range(KD):
                copy_front(B - 2, 1, k)
            row_norm(B - 1, 0)
            router_exp(B - 2)
            for k in range(KD):
                copy_front(B - 1, 0, k)
            context_probs(B - 1)
            copy_probs(B - 1)

            act.wait_ge(w1_in, 16)
            act.wait_ge(s_ready, 64 * B)
            for i in range(4):
                act.activation(w1[0][:, 2 * i:2 * i + 2], w1raw[:, 2 * i:2 * i + 2], ACT.Copy
                               ).then_inc(w1_hi, 1)
            act.wait_ge(w2_in, 16)
            act.wait_ge(pv_done, SLOTS * B)
            for i in range(4):
                act.activation(w2[0][:, 2 * i:2 * i + 2], w2raw[:, 2 * i:2 * i + 2], ACT.Copy
                               ).then_inc(w2_hi, 1)
            row_norm(B - 1, 1)
            for k in range(KD):
                copy_front(B - 1, 1, k)
            router_exp(B - 1)

            def tile_hi(t, u):
                act.wait_ge(tx_done, t + 1)
                if not (isinstance(t, int) and t < 2):
                    act.wait_ge(l1_done, t - 1)
                act.activation(xT2[0][:, u % 2].rearrange("p k s -> p (k s)"),
                               bank[u % 2][:, 0:D], ACT.Copy).then_inc(xth_done, 1)

            def tile_relu(t, u):
                act.wait_ge(l1_done, t + 1)
                if not (isinstance(t, int) and t < 2):
                    act.wait_ge(sqt_done, t - 1)
                act.activation(relu_t[:, u % 2, :], bank[2 + u % 2][:, 0:F], ACT.Relu
                               ).then_inc(relut_done, 1)

            def tile_hidden_hi(t, u):
                act.wait_ge(th_done, t + 1)
                if not (isinstance(t, int) and t < 2):
                    act.wait_ge(l2_done, t - 1)
                act.activation(hT2[0][:, u % 2].rearrange("p k s -> p (k s)"),
                               bank[4 + u % 2][:, 0:F], ACT.Copy).then_inc(hth_done, 1)

            def tile_result(t, i, u):
                act.wait_ge(l2_done, t + 1)
                if not (isinstance(t, int) and t < RING):
                    act.wait_ge(yt_out[u % RING], 16 * i)
                act.activation(yt[:, u % RING, :], bank[6 + u % 2][:, 0:D], ACT.Copy
                               ).then_inc(yt_done, 1)

            def tile_step(s, i, u):
                if not (isinstance(s, int) and s + 1 >= TILES):
                    tile_hi(s + 1, u + 1)
                if not (isinstance(s, int) and s >= TILES):
                    tile_relu(s, u)
                if not (isinstance(s, int) and not 1 <= s <= TILES):
                    tile_hidden_hi(s - 1, u + 1)
                if not (isinstance(s, int) and s < 2):
                    tile_result(s - 2, i - (u < 2), (u + RING - 2) % RING)

            def shared_weights_hi(i):
                act.wait_ge(w2_lo, 4)
                act.wait_ge(ws_in, 32)
                act.activation((ws1, ws2)[i][0][:].rearrange("p k f -> p (k f)"),
                               wsraw[:, i, :], ACT.Copy).then_inc(ws_hi, 1)

            act.wait_ge(rows_out, 16 * 2 * TB * B)
            act.wait_ge(turned_out, 16 * B)
            tile_hi(0, 0)
            for s in range(2 * RING):
                if s in (3, 4):
                    shared_weights_hi(s - 3)
                tile_step(s, s // RING, s % RING)
            with act.Fori(1, TILES // RING // 2 - 1) as k:
                for i in (2 * k, 2 * k + 1):
                    for u in range(RING):
                        tile_step(RING * i + u, i, u)
            for s in range(TILES - 2 * RING, TILES + 2):
                tile_step(s, s // RING, s % RING)

            def shared_hi(b, h):
                act.wait_ge(xs3_in[h], 16 * (b + 1))
                if not (isinstance(b, int) and b == 0):
                    act.wait_ge(up_done, NFS * (2 * b + h - 1))
                act.activation(xs2[0][:, h].rearrange("p k s -> p (k s)"),
                               xs3[:, h].rearrange("p k s -> p (k s)"), ACT.Copy
                               ).then_inc(xsh_done, 1)

            def shared_relu(b, h):
                n = NFS * (2 * b + h)
                for c in range(NFS):
                    act.wait_ge(up_done, n + c + 1)
                    if not (isinstance(b, int) and b == 0 and h == 0):
                        act.wait_ge(sqs_done, n - NFS + c + 1)
                    act.activation(relu_s[:, c, :], bank[c][:, 0:HB], ACT.Relu
                                   ).then_inc(relus_done, 1)

            def shared_square(b, h):
                n = NFS * (2 * b + h)
                for c in range(NFS):
                    act.wait_ge(relus_done, n + c + 1)
                    if not (isinstance(b, int) and b == 0 and h == 0):
                        act.wait_ge(hsl_done, n - NFS + c + 1)
                    act.activation(sq_s[:, c, :], relu_s[:, c, :], ACT.Square
                                   ).then_inc(sqs_done, 1)

            def shared_hidden_hi(b, h):
                n = NFS * (2 * b + h)
                if not (isinstance(b, int) and b == 0):
                    act.wait_ge(down_done, 2 * b + h - 1)
                for c in range(NFS):
                    act.wait_ge(sqs_done, n + c + 1)
                    act.activation(hs[0][:, h, c, :], sq_s[:, c, :], ACT.Copy
                                   ).then_inc(hsh_done, 1)

            shared_hi(0, 0)

            def shared_block(b, more=True):
                for h in range(2):
                    shared_relu(b, h)
                    if h == 0:
                        shared_hi(b, 1)
                    elif more:
                        shared_hi(b + 1, 0)
                    shared_square(b, h)
                    shared_hidden_hi(b, h)

            shared_block(0)
            with act.Fori(1, B - 1) as b:
                shared_block(b)
            shared_block(B - 1, False)

        @block.vector
        def _(dve):
            def stats(a, first):
                if first:
                    dve.wait_ge(x_in[a], 16)
                if not (isinstance(a, int) and a == 0):
                    dve.wait_ge(mv_done, TB * a)
                apart(dve)
                for t in range(TB):
                    dve.bn_stats(st[0][:, t, :], tile(a, t)[:, 0]).then_inc(bn_done, 1)
                    yield
                if not (isinstance(a, int) and a == 0):
                    dve.wait_ge(offset_done, a)
                dve.wait_ge(bn_done, TB * (a + 1))
                apart(dve)
                for t in range(TB):
                    dve.bn_aggr(mv[0][:, t, :], st[0][:, t, :]).then_inc(mv_done, 1)
                yield
                dve.wait_ge(mv_done, TB * (a + 1))
                if not (isinstance(a, int) and a == 0):
                    dve.wait_ge(rstd_done, a)
                dve.tensor_scalar(var[0][:], mv[0][:, :, 1], EPS, None, ALU.add
                                  ).then_inc(var_done, 1)

            def norm_offset(a):
                dve.wait_ge(rstd_done, a + 1)
                if not (isinstance(a, int) and a == 0):
                    dve.wait_ge(norm_done, TB * a)
                dve.scalar_tensor_tensor(out=offset[0][:], in0=mv[0][:, :, 0], scalar=-1.0,
                                         in1=rstd[0][:], op0=ALU.mult, op1=ALU.mult
                                         ).then_inc(offset_done, 1)

            def first_part(a, c):
                dve.wait_ge(qk_done, 4 * a + c + 1)
                if not (isinstance(a, int) and a == 0):
                    dve.wait_ge(scr_out, 64 * a)
                apart(dve)
                dve.tensor_copy(parts[:, 0, c, :], qk[:, c % 2, :]).then_inc(q1_done, 1)

            def copy_v(a, par, i):
                dve.wait_ge(vmm_done, 2 * a + i + 1)
                if i == 0 and not (isinstance(a, int) and a < 2):
                    dve.wait_ge(pv_done, SLOTS * (a - 1))
                for t in range(2):
                    dve.tensor_tensor(
                        VO[par][:, 2 * i + t, :, 1:1 + HD],
                        value_place(a, i)[:, t * D:(t + 1) * D].rearrange("p (h d) -> p h d", d=HD),
                        bvs[:].rearrange("p (h d) -> p h d", d=HD), ALU.add
                    ).then_inc(v_done, 1)

            def maxima(a, m):
                g = m // GH
                for q in range(TB):
                    n = 4 * m + q
                    dve.wait_ge(mx_ready, 64 * a + n + 1)
                    if m % GH == 0 and q == 0 and not (isinstance(a, int) and a == 0 and g < 2):
                        dve.wait_ge(tm_done, NG * a + g - 1)
                    dve.tensor_reduce(mneg[:, g % 2, m % GH * TB + q:m % GH * TB + q + 1],
                                      bank[4 + n % 2][:], AX.X, ALU.max, negate=True
                                      ).then_inc(max_done, 1)
                    yield q

            def split_max(a, g):
                G = NG * a + g
                dve.wait_ge(tm_done, G + 1)
                if not (isinstance(a, int) and a == 0 and g < 2):
                    dve.wait_ge(mrow_in[g % 2], 32 * (2 * a + g // 2))
                dve.tensor_copy(mparts[:, g % 2, 0, :], end[0:GH * TB, 0:P]
                                ).then_inc(m1_done, 1)
                dve.wait_ge(m1_done, G + 1)
                dve.tensor_tensor(mparts[:, g % 2, 1, :], end[0:GH * TB, 0:P],
                                  mparts[:, g % 2, 0, :], ALU.subtract).then_inc(m2_done, 1)

            def normalise(b, g):
                G = NG * b + g
                dve.wait_ge(turn_done, G + 1)
                if not (isinstance(b, int) and b == 0 and g == 0):
                    dve.wait_ge(on_done, G)
                sums = end[:].rearrange("p (t j c) -> p t j c", t=TB, j=GH)
                dve.reciprocal(rden[:], sums[:, :, :, 0]).then_inc(rden_done, 1)
                dve.wait_ge(rden_done, G + 1)
                if g == 0 and not (isinstance(b, int) and b == 0):
                    dve.wait_ge(ont_done, KD * b)
                dve.tensor_tensor(
                    o_nat[:, :, g * GH * HD:(g + 1) * GH * HD].rearrange(
                        "p t (j d) -> p t j d", j=GH),
                    sums[:, :, :, 1:1 + HD],
                    rden[:].unsqueeze(3).to_broadcast([P, TB, GH, HD]), ALU.mult
                ).then_inc(on_done, 1)

            def add_out(b, i):
                dve.wait_ge(pj_done, 2 * b + i + 1)
                dve.wait_ge(xb_done, TB * (b + 1))
                t = tile(b, 2 * i, 2)
                dve.tensor_tensor(t, either(b, i, end)[:].rearrange("p (t d) -> p t d", t=2),
                                  t, ALU.add
                                  ).then_inc(x1_done, 1)

            def row_stats(a, r):
                n = 2 * a + r
                if r == 0:
                    dve.wait_ge(x1_done, 2 * (a + 1))
                else:
                    dve.wait_ge(x2_done, TB * (a + 1))
                if not (isinstance(a, int) and a == 0 and r == 0):
                    dve.wait_ge(f_mv, TB * n)
                    dve.wait_ge(f_offset, n)
                apart(dve)
                for t in range(TB):
                    dve.bn_stats(st[1][:, t, :], tile(a, t)[:, 0]).then_inc(f_bn, 1)
                    yield
                dve.wait_ge(f_bn, TB * (n + 1))
                apart(dve)
                for t in range(TB):
                    dve.bn_aggr(mv[1][:, t, :], st[1][:, t, :]).then_inc(f_mv, 1)
                yield
                dve.wait_ge(f_mv, TB * (n + 1))
                if not (isinstance(a, int) and a == 0 and r == 0):
                    dve.wait_ge(f_rstd, n)
                dve.tensor_scalar(var[1][:], mv[1][:, :, 1], EPS, None, ALU.add
                                  ).then_inc(f_var, 1)

            def row_offset(a, r):
                n = 2 * a + r
                dve.wait_ge(f_rstd, n + 1)
                if not (isinstance(a, int) and a == 0 and r == 0):
                    dve.wait_ge(f_norm, TB * n)
                dve.scalar_tensor_tensor(out=offset[1][:], in0=mv[1][:, :, 0], scalar=-1.0,
                                         in1=rstd[1][:], op0=ALU.mult, op1=ALU.mult
                                         ).then_inc(f_offset, 1)

            def context_max(a):
                dve.wait_ge(lg_done, a + 1)
                if not (isinstance(a, int) and a == 0):
                    dve.wait_ge(px_done, TB * a)
                dve.tensor_reduce(xm[:], mid[:, 0:TB * SC].rearrange("p (t s) -> p t s", s=SC),
                                  AX.X, ALU.max).then_inc(xm_done, 1)
                dve.wait_ge(xm_done, 2 * a + 1)
                dve.tensor_scalar(xb[:], xm[:], -(D ** -0.5), None, ALU.mult
                                  ).then_inc(xm_done, 1)

            def context_invert(a):
                dve.wait_ge(px_done, TB * (a + 1))
                if not (isinstance(a, int) and a == 0):
                    dve.wait_ge(x2_done, TB * a)
                dve.reciprocal(xr[:], xsum[:]).then_inc(xr_done, 1)

            def context_add(a, i):
                dve.wait_ge(xr_done, a + 1)
                dve.wait_ge(xpv_done, 2 * a + i + 1)
                for t in (2 * i, 2 * i + 1):
                    xt_ = tile(a, t)[:, 0]
                    dve.scalar_tensor_tensor(
                        out=xt_, in0=(mid, end)[i][:, t % 2 * D:(t % 2 + 1) * D],
                        scalar=xr[:, t:t + 1], in1=xt_, op0=ALU.mult, op1=ALU.add
                    ).then_inc(x2_done, 1)

            def wide(v, n=TB):
                return v.unsqueeze(2).to_broadcast([P, n, E])

            def chain(s, start):
                count = [start]

                def done():
                    dve.wait_ge(s, count[0])

                def put(ins):
                    ins.then_inc(s, 1)
                    count[0] = count[0] + 1

                def step(ins):
                    put(ins)
                    done()
                return step, put, done, count

            def router_logits(a):
                step, _, _, _ = chain(rt_step, ROUTE_STEPS * a)
                dve.wait_ge(rt_mm, a + 1)
                logits = mid[:, 0:TB * E].rearrange("p (t e) -> p t e", e=E)
                step(dve.tensor_reduce(rc["m"][:], logits, AX.X, ALU.max))
                if not (isinstance(a, int) and a == 0):
                    dve.wait_ge(rt_e, a)
                dve.tensor_tensor(rt["d"][:], logits, wide(rc["m"][:]), ALU.subtract
                                  ).then_inc(rt_d, 1)

            def route(a):
                _, put, done, _ = chain(rt_step, ROUTE_STEPS * a + 1)
                dve.wait_ge(rt_e, a + 1)
                e = rt["e"]
                for i, src in (("1", e), ("2", rt["e2"])):
                    if i == "2":
                        put(dve.scalar_tensor_tensor(out=rt["e2"][:], in0=rt["oh1"][:],
                                                      scalar=-2.0, in1=e[:], op0=ALU.mult,
                                                      op1=ALU.add))
                        yield
                        done()
                    put(dve.tensor_reduce(rc["m" + i][:], src[:], AX.X, ALU.max))
                    yield
                    done()
                    put(dve.tensor_tensor(rt["eq" + i][:], src[:], wide(rc["m" + i][:]),
                                           ALU.is_equal))
                    yield
                    done()
                    put(dve.tensor_tensor(rt["s" + i][:], rt["eq" + i][:], rank, ALU.mult))
                    yield
                    done()
                    put(dve.tensor_reduce(rc["sm" + i][:], rt["s" + i][:], AX.X, ALU.max))
                    yield
                    done()
                    put(dve.tensor_tensor(rt["oh" + i][:], rt["s" + i][:],
                                           wide(rc["sm" + i][:]), ALU.is_equal))
                    yield
                    done()
                if not (isinstance(a, int) and a == 0):
                    dve.wait_ge(rk_mm, a)
                dve.tensor_tensor(oh[:], rt["oh1"][:], rt["oh2"][:], ALU.add
                                  ).then_inc(oh_done, 1)
                put(dve.tensor_tensor(rc["den"][:], rc["m1"][:], rc["m2"][:], ALU.add))
                yield
                done()
                put(dve.reciprocal(rc["r"][:], rc["den"][:]))
                yield
                done()
                for i in range(2):
                    put(dve.tensor_tensor(weight[:, i, bass.ds(a * TB, TB)],
                                           rc[f"m{i + 1}"][:], rc["r"][:], ALU.mult))
                    yield
                    done()
                for i in range(2):
                    put(dve.tensor_scalar(chosen[:, i, bass.ds(a * TB, TB), :],
                                           rt[f"oh{i + 1}"][:], 0.0, None, ALU.add))
                    yield
                    done()

            def count_on(a):
                dve.wait_ge(rk_mm, a + 1)
                if not (isinstance(a, int) and a == 0):
                    dve.wait_ge(rk_step, 2 * a)
                    dve.wait_ge(rows_done, a)
                count = end[:, 0:TB * E].rearrange("p (t e) -> p t e", e=E)
                dve.tensor_tensor(rt["row"][:], count,
                                  next_row[:].unsqueeze(1).to_broadcast([P, TB, E]), ALU.add
                                  ).then_inc(rk_step, 1)
                dve.wait_ge(rk_step, 2 * a + 1)
                dve.tensor_tensor(next_row[:], end[:, TB * E:(TB + 1) * E], next_row[:],
                                  ALU.add).then_inc(rk_step, 1)

            def send_rows(a):
                dve.wait_ge(rk_step, 2 * (a + 1))
                _, put, done, _ = chain(pos_step, 4 * a)
                for i in range(2):
                    put(dve.tensor_tensor(rt[f"p{i + 1}"][:], rt["row"][:],
                                           rt[f"oh{i + 1}"][:], ALU.mult))
                    yield
                    done()
                    apart(dve)
                    put(dve.tensor_reduce(place[:, i, bass.ds(a * TB, TB)],
                                           rt[f"p{i + 1}"][:], AX.X, ALU.add))
                    yield
                    done()
                if not (isinstance(a, int) and a == 0):
                    dve.wait_ge(rows_out, 16 * 2 * TB * a)
                apart(dve)
                dve.tensor_copy(rows_i[:], place[:, :, bass.ds(a * TB, TB)]
                                ).then_inc(rows_done, 1)

            def batch(b, par):
                prv2, prv, nxt, nxt2 = flags(b)
                routing = iter(())
                for s in range(SLOTS):
                    if s % 4 == 0:
                        b = own_copy(dve, b)
                    between = iter(())
                    start = 0
                    if prv2 and s == 0:
                        between = row_stats(b - 2, 1)
                    if nxt2 and s == 4:
                        between = stats(b + 2, False)
                    if prv2 and s == 5:
                        routing, start = route(b - 2), 2
                    if s in (5, 6, 7, 8):
                        between = routing
                    if prv and s == 9:
                        between = row_stats(b - 1, 0)
                    if prv2 and s == 11:
                        between = send_rows(b - 2)
                    m = s + AHEAD
                    ahead = range(TB)
                    if m < SLOTS:
                        ahead = maxima(b, m)
                    elif nxt:
                        ahead = maxima(b + 1, m - SLOTS)
                    for q in ahead:
                        if nxt2 and 10 <= s < 14 and q == 1:
                            first_part(b + 2, s - 10)
                        for _ in range((0, 2, 1, 1)[q] if q >= start else 0):
                            next(between, None)
                        if prv2 and s == 1 and q == 1:
                            row_offset(b - 2, 1)
                        if nxt2 and s == 5 and q == 3:
                            norm_offset(b + 2)
                        if prv and s == 10 and q == 1:
                            row_offset(b - 1, 0)
                        if prv2 and s == 10 and q == 2:
                            count_on(b - 2)
                    if s in (6, 7):
                        next(between, None)
                    elif s != 5:
                        finish(between)
                    if nxt and s in (5, 6):
                        copy_v(b + 1, 1 - par, s - 5)
                    if prv2 and s == 4:
                        router_logits(b - 2)
                    if s % 4 == 1:
                        if s // 4 + 1 < NG:
                            split_max(b, s // 4 + 1)
                        elif nxt:
                            split_max(b + 1, 0)
                    if s % 4 == 2:
                        if s > 2:
                            normalise(b, s // 4 - 1)
                        elif prv:
                            normalise(b - 1, NG - 1)
                    if prv and s in (7, 8):
                        add_out(b - 1, s - 7)
                    if prv and s == 13:
                        context_max(b - 1)
                    if prv and s == 14:
                        context_invert(b - 1)
                    if prv and s == 15:
                        for i in range(2):
                            context_add(b - 1, i)

            finish(stats(0, True))
            norm_offset(0)
            finish(stats(1, True))
            for i in range(2):
                dve.memset(VO[i][:], 0.0).then_inc(init, 1)
            norm_offset(1)
            dve.wait_ge(init, 2)
            for i in range(2):
                dve.memset(VO[i][:, :, :, 0:1], 1.0).then_inc(init, 1)
            dve.wait_ge(w_in, 16 * 10)
            dve.wait_ge(init, 4)
            dve.tensor_copy(tri[:], tri_f[:]).then_inc(tri_set, 1)
            dve.tensor_copy(next_row[:], first).then_inc(tri_set, 1)
            dve.memset(zeros[:], 0.0).then_inc(zeros_set, 1)
            dve.wait_ge(tri_set, 2)
            for c in range(4):
                first_part(0, c)
            for i in range(2):
                copy_v(0, 0, i)
            for c in range(4):
                first_part(1, c)
            for m in range(AHEAD):
                finish(maxima(0, m))
                if m == 4:
                    split_max(0, 0)
            for b in range(2, B):
                dve.wait_ge(x_in[b], 16)
            batch(0, 0)
            batch(1, 1)
            with dve.Fori(0, 2) as i:
                for u in range(2):
                    batch(2 * i + 2 + u, u)
            batch(6, 0)
            batch(7, 1)
            normalise(B - 1, NG - 1)
            finish(row_stats(B - 2, 1))
            row_offset(B - 2, 1)
            for i in range(2):
                add_out(B - 1, i)
            finish(row_stats(B - 1, 0))
            row_offset(B - 1, 0)
            router_logits(B - 2)
            finish(route(B - 2))
            context_max(B - 1)
            context_invert(B - 1)
            count_on(B - 2)
            for i in range(2):
                context_add(B - 1, i)
            finish(row_stats(B - 1, 1))
            row_offset(B - 1, 1)
            finish(send_rows(B - 2))

            def split_lo(dst, raw, hi, i, s_hi, s_lo):
                dve.wait_ge(s_hi, i + 1)
                dve.tensor_tensor(dst[:, 2 * i:2 * i + 2], raw[:, 2 * i:2 * i + 2],
                                  hi[:, 2 * i:2 * i + 2].bitcast(F32), ALU.subtract
                                  ).then_inc(s_lo, 1)

            for i in range(2):
                split_lo(w1[1], w1raw, w1[0], i, w1_hi, w1_lo)
            router_logits(B - 1)
            for i in range(2, 4):
                split_lo(w1[1], w1raw, w1[0], i, w1_hi, w1_lo)
            finish(route(B - 1))
            count_on(B - 1)
            finish(send_rows(B - 1))

            step, _, _, count = chain(fin_step, 0)
            dve.wait_ge(scr_out, 64 * B)
            dve.wait_ge(table_in, 16)
            dve.wait_ge(zeros_set, 1)
            step(dve.tensor_tensor(counted[:], next_row[:], first, ALU.subtract))
            dve.tensor_copy(zero_i[:], next_row[0:1, :]).then_inc(zero_done, 1)
            over = fin_a[:].rearrange("p a b -> p (a b)").rearrange("p (e j) -> p e j", e=E)
            step(dve.tensor_tensor(over, counted[:].unsqueeze(2).to_broadcast([P, E, B * TB]),
                                   steps.unsqueeze(1).to_broadcast([P, E, B * TB]), ALU.is_gt))
            step(dve.tensor_reduce(tiles[:], over, AX.X, ALU.add))
            sums = fin_b[:, 0:E, :]
            step(dve.tensor_tensor(sums, tiles[:].unsqueeze(1).to_broadcast([P, E, E]), upto,
                                   ALU.mult))
            step(dve.tensor_reduce(incl[:], sums, AX.X, ALU.add))
            step(dve.tensor_tensor(excl[:], incl[:], tiles[:], ALU.subtract))
            step(dve.scalar_tensor_tensor(out=shift[:], in0=excl[:], scalar=-float(P), in1=first,
                                          op0=ALU.mult, op1=ALU.add))
            step(dve.tensor_scalar(tab_n[:, 0:1], incl[0:1, E - 1:E], -1.0, None, ALU.add))
            step(dve.tensor_scalar(tab_t[:], tab_0[:], tab_n[:, 0:1], None, ALU.min))
            step(dve.tensor_tensor(tab_a[:], tab_t[:].unsqueeze(2).to_broadcast([1, TILES, E]),
                                   incl[0:1, :].unsqueeze(1).to_broadcast([1, TILES, E]),
                                   ALU.is_ge))
            step(dve.tensor_reduce(tab_c[:, 0], tab_a[:], AX.X, ALU.add))
            step(dve.tensor_copy(expert_i[:], tab_c[:, 0]))
            step(dve.tensor_scalar(fin_c[0:1, 0, 0:E], tiles[0:1, :], -float(P), float(ROOM),
                                   ALU.mult, ALU.add))
            step(dve.tensor_tensor(tab_b[:], tab_a[:],
                                   fin_c[0:1, 0, 0:E].unsqueeze(1).to_broadcast([1, TILES, E]),
                                   ALU.mult))
            step(dve.tensor_reduce(tab_c[:, 1], tab_b[:], AX.X, ALU.add))
            step(dve.scalar_tensor_tensor(out=row_i[:], in0=tab_t[:], scalar=float(P),
                                          in1=tab_c[:, 1], op0=ALU.mult, op1=ALU.add))
            dve.tensor_copy(tab_n[:, 1:2], tab_n[:, 0:1]).then_inc(table_done, 1)

            def tile_lo(t, u):
                dve.wait_ge(xth_done, t + 1)
                if not (isinstance(t, int) and t < 2):
                    dve.wait_ge(l1_done, t - 1)
                dve.tensor_tensor(xT2[1][:, u % 2].rearrange("p k s -> p (k s)"),
                                  bank[u % 2][:, 0:D],
                                  xT2[0][:, u % 2].rearrange("p k s -> p (k s)").bitcast(F32),
                                  ALU.subtract).then_inc(xtl_done, 1)

            def tile_square(t, u):
                dve.wait_ge(relut_done, t + 1)
                if not (isinstance(t, int) and t < 2):
                    dve.wait_ge(th_done, t - 1)
                dve.tensor_tensor(sq_t[:, u % 2, :], relu_t[:, u % 2, :], relu_t[:, u % 2, :],
                                  ALU.mult).then_inc(sqt_done, 1)

            def tile_hidden_lo(t, u):
                dve.wait_ge(hth_done, t + 1)
                if not (isinstance(t, int) and t < 2):
                    dve.wait_ge(l2_done, t - 1)
                dve.tensor_tensor(hT2[1][:, u % 2].rearrange("p k s -> p (k s)"),
                                  bank[4 + u % 2][:, 0:F],
                                  hT2[0][:, u % 2].rearrange("p k s -> p (k s)").bitcast(F32),
                                  ALU.subtract).then_inc(htl_done, 1)

            def tile_step(s, u):
                if not (isinstance(s, int) and s + 1 >= TILES):
                    tile_lo(s + 1, u + 1)
                if not (isinstance(s, int) and s >= TILES):
                    tile_square(s, u)
                if not (isinstance(s, int) and s == 0):
                    tile_hidden_lo(s - 1, u + 1)

            for i in range(4):
                split_lo(w2[1], w2raw, w2[0], i, w2_hi, w2_lo)

            dve.wait_ge(rows_out, 16 * 2 * TB * B)
            tile_lo(0, 0)
            def beside_tiles():
                _, put, done, _ = chain(fin_step, count[0])
                for i in range(2):
                    put(dve.tensor_tensor(fin_a[:], chosen[:, i],
                                          shift[:].unsqueeze(1).to_broadcast([P, B * TB, E]),
                                          ALU.mult))
                    yield
                    done()
                    put(dve.tensor_reduce(fin_c[:, i], fin_a[:], AX.X, ALU.add))
                    if i == 0:
                        done()
                    else:
                        yield
                        done()
                for i in range(2):
                    dve.wait_ge(ws_hi, i + 1)
                    ws = (ws1, ws2)[i]
                    dve.tensor_tensor(ws[1][:].rearrange("p k f -> p (k f)"), wsraw[:, i, :],
                                      ws[0][:].rearrange("p k f -> p (k f)").bitcast(F32),
                                      ALU.subtract).then_inc(ws_lo, 1)
                    yield
                put(dve.tensor_tensor(result_i[:], place[:], fin_c[:], ALU.subtract))
                yield
                done()
                for b in range(2):
                    dve.tensor_copy(result_now[:, b], result_i[:, :, b * TB:(b + 1) * TB]
                                    ).then_inc(now_done, 1)

            beside = beside_tiles()
            for s in range(2 * RING):
                tile_step(s, s % RING)
                next(beside, None)
            with dve.Fori(1, TILES // RING // 2 - 1) as k:
                for i in (2 * k, 2 * k + 1):
                    for u in range(RING):
                        tile_step(RING * i + u, u)
            for s in range(TILES - 2 * RING, TILES + 1):
                tile_step(s, s % RING)

            def shared_lo(b, h):
                dve.wait_ge(xsh_done, 2 * b + h + 1)
                if not (isinstance(b, int) and b == 0):
                    dve.wait_ge(up_done, NFS * (2 * b + h - 1))
                dve.tensor_tensor(xs2[1][:, h].rearrange("p k s -> p (k s)"),
                                  xs3[:, h].rearrange("p k s -> p (k s)"),
                                  xs2[0][:, h].rearrange("p k s -> p (k s)").bitcast(F32),
                                  ALU.subtract).then_inc(xsl_done, 1)

            def shared_hidden_lo(b, h):
                n = NFS * (2 * b + h)
                if not (isinstance(b, int) and b == 0):
                    dve.wait_ge(down_done, 2 * b + h - 1)
                for c in range(NFS):
                    dve.wait_ge(hsh_done, n + c + 1)
                    dve.tensor_tensor(hs[1][:, h, c, :], sq_s[:, c, :],
                                      hs[0][:, h, c, :].bitcast(F32), ALU.subtract
                                      ).then_inc(hsl_done, 1)

            def shared_add(b, h):
                dve.wait_ge(down_done, 2 * b + h + 1)
                x2 = tile(b, 2 * h, 2)
                dve.tensor_tensor(x2, bank[4 + h][:].rearrange("p (t d) -> p t d", t=2), x2,
                                  ALU.add).then_inc(shared_done, 1)

            def experts_add(b, h):
                dve.wait_ge(shared_done, 2 * b + h + 1)
                for t in (2 * h, 2 * h + 1):
                    dve.wait_ge(got_in[t], 32 * (b + 1))
                    x1 = tile(b, t)[:, 0]
                    dve.scalar_tensor_tensor(
                        out=x1, in0=got[:, t, 0, :],
                        scalar=weight[:, 0, bass.ds(b * TB + t, 1)],
                        in1=x1, op0=ALU.mult, op1=ALU.add).then_inc(add1_done, 1)
                for t in (2 * h, 2 * h + 1):
                    dve.wait_ge(add1_done, TB * b + t + 1)
                    x1 = tile(b, t)[:, 0]
                    dve.scalar_tensor_tensor(
                        out=x1, in0=got[:, t, 1, :],
                        scalar=weight[:, 1, bass.ds(b * TB + t, 1)],
                        in1=x1, op0=ALU.mult, op1=ALU.add).then_inc(add2_done, 1)

            def next_results(b, par):
                for t in range(TB):
                    dve.wait_ge(got_in[t], 32 * (b - 1))
                apart(dve)
                dve.tensor_copy(result_now[:, par], result_i[:, :, bass.ds(b * TB, TB)]
                                ).then_inc(now_done, 1)

            shared_lo(0, 0)

            def shared_block(b, par):
                for h in range(2):
                    if h == 0:
                        shared_lo(b, 1)
                    elif not (isinstance(b, int) and b == B - 1):
                        shared_lo(b + 1, 0)
                    if not (isinstance(b, int) and b == 0):
                        shared_add(b - 1, h)
                        experts_add(b - 1, h)
                    shared_hidden_lo(b, h)
                if not (isinstance(b, int) and b in (0, B - 1)):
                    next_results(b + 1, 1 - par)

            for b in range(2):
                shared_block(b, b)
            with dve.Fori(1, B // 2 - 1) as i:
                for u in range(2):
                    shared_block(2 * i + u, u)
            for b in range(B - 2, B):
                shared_block(b, b % 2)
            for h in range(2):
                shared_add(B - 1, h)
                experts_add(B - 1, h)

        @block.gpsimd
        def _(pool):
            def inverse_std(a):
                pool.wait_ge(var_done, a + 1)
                if not (isinstance(a, int) and a == 0):
                    pool.wait_ge(norm_done, TB * a)
                pool.tensor_tensor(rstd[0][:], var[0][:], minus_half[:], ALU.pow
                                   ).then_inc(rstd_done, 1)

            def add_bias(a):
                pool.wait_ge(norm_done, TB * (a + 1))
                apart(pool)
                for t in range(TB):
                    xt = tile(a, t)[:, 0]
                    pool.tensor_tensor(xt, xt, bps[:], ALU.add).then_inc(xb_done, 1)

            def first_rest(a, c):
                pool.wait_ge(q1_done, 4 * a + c + 1)
                if not (isinstance(a, int) and a == 0 and c < 2):
                    pool.wait_ge(q3_done, 4 * a + c - 1)
                    pool.wait_ge(q2_done, 4 * a + c - 1)
                pool.tensor_tensor(rest[:, c % 2, :], qk[:, c % 2, :], parts[:, 0, c, :],
                                   ALU.subtract).then_inc(r1_done, 1)

            def third_part(a, c):
                pool.wait_ge(q2_done, 4 * a + c + 1)
                pool.tensor_tensor(parts[:, 2, c, :], rest[:, c % 2, :], parts[:, 1, c, :],
                                   ALU.subtract).then_inc(q3_done, 1)

            def row_inverse_std(a, r):
                n = 2 * a + r
                pool.wait_ge(f_var, n + 1)
                if not (isinstance(a, int) and a == 0 and r == 0):
                    pool.wait_ge(f_norm, TB * n)
                pool.tensor_tensor(rstd[1][:], var[1][:], minus_half[:], ALU.pow
                                   ).then_inc(f_rstd, 1)

            def scatter_rows(a, tiles=range(TB)):
                if tiles[0] == 0:
                    pool.wait_ge(rows_done, a + 1)
                    apart(pool)
                for t in tiles:
                    for i in range(2):
                        pool.indirect_dma_start(
                            x_rows, bass.IndirectOffsetOnAxis(ap=rows_i[:, i, t:t + 1], axis=0),
                            normed(a, 1)[:, t, :], None).then_inc(rows_out, 16)

            def batch(b, par):
                prv2, prv, nxt, nxt2 = flags(b)
                for s in range(SLOTS):
                    if prv2 and s == 0:
                        row_inverse_std(b - 2, 1)
                    if nxt2 and s == 5:
                        inverse_std(b + 2)
                    if nxt2 and s == 7:
                        add_bias(b + 2)
                    if prv and s == 9:
                        row_inverse_std(b - 1, 0)
                    if nxt2 and 10 <= s < 14:
                        first_rest(b + 2, s - 10)
                    if nxt2 and 11 <= s < 15:
                        third_part(b + 2, s - 11)
                    if prv2 and s >= 12:
                        scatter_rows(b - 2, [s - 12])

            pool.memset(minus_half[:], -0.5).then_inc(half_set, 1)
            pool.wait_ge(half_set, 1)
            for a in range(2):
                inverse_std(a)
            pool.wait_ge(w_in, 16 * 10)
            for a in range(2):
                add_bias(a)
                for c in range(5):
                    if c < 4:
                        first_rest(a, c)
                    if c > 0:
                        third_part(a, c - 1)
            batch(0, 0)
            batch(1, 1)
            with pool.Fori(0, 2) as i:
                for u in range(2):
                    batch(2 * i + 2 + u, u)
            batch(6, 0)
            batch(7, 1)

            row_inverse_std(B - 2, 1)
            row_inverse_std(B - 1, 0)
            row_inverse_std(B - 1, 1)
            scatter_rows(B - 2)
            scatter_rows(B - 1)

            def fetch_results(b, par):
                pool.wait_ge(now_done, b + 1)
                apart(pool)
                for t in range(TB):
                    if not (isinstance(b, int) and b == 0):
                        pool.wait_ge(add2_done, TB * (b - 1) + t + 1)
                        apart(pool)
                    for i in range(2):
                        pool.indirect_dma_start(
                            got[:, t, i, :], None, y_rows,
                            bass.IndirectOffsetOnAxis(ap=result_now[:, par, i, t:t + 1],
                                                       axis=0)
                        ).then_inc(got_in[t], 16)

            for u in range(RING):
                pool.wait_ge(yt_out[u], 16 * (TILES // RING))
            for b in range(2):
                fetch_results(b, b)
            with pool.Fori(1, B // 2) as i:
                for u in range(2):
                    fetch_results(2 * i + u, u)


def kernel(x, ctx_1024, L0_attn_qkv_w, L0_attn_qkv_b, L0_attn_proj_w, L0_attn_proj_b,
           L0_ffn_w_router, L0_ffn_w1_stack, L0_ffn_w2_stack, L0_ffn_ws1, L0_ffn_ws2):
    import numpy as np
    import concourse.bacc as bacc
    from concourse.bass_utils import run_bass_kernel_spmd

    qkv_w, proj_w = np.asarray(L0_attn_qkv_w), np.asarray(L0_attn_proj_w)
    qkv_b = np.asarray(L0_attn_qkv_b)
    e = np.arange(E, dtype=np.float32)
    const = np.concatenate([
        np.broadcast_to(E - e, (P, TB, E)).reshape(P, TB * E),
        np.broadcast_to(e * ROOM, (P, E)),
        np.broadcast_to(P * np.arange(B * TB, dtype=np.float32), (P, B * TB)),
        np.broadcast_to((e <= e[:, None]).astype(np.float32).reshape(E * E), (P, E * E)),
    ], axis=1).astype(np.float32)
    tri = np.stack([np.triu(np.ones((P, P), np.float32), 1), np.ones((P, P), np.float32)], axis=1)

    def chunks(w):
        w = np.asarray(w)
        w = w.reshape(*w.shape[:-2], w.shape[-2] // P, P, w.shape[-1])
        return np.moveaxis(w, -2, 0)

    def turned(w):
        return np.swapaxes(np.asarray(w), -1, -2)

    ctx = np.asarray(ctx_1024)
    ins = {
        "x": np.asarray(x), "ctx_n": ctx.transpose(1, 0, 2),
        "ctx_t": chunks(turned(ctx)),
        "wqk_t": chunks(qkv_w[:2 * D].T), "bqk": qkv_b[:2 * D].reshape(4, P).T,
        "wv_t": chunks(qkv_w[2 * D:].T), "bv": qkv_b[2 * D:],
        "wp_t": chunks(proj_w.T), "bp": np.asarray(L0_attn_proj_b),
        "wr_t": chunks(turned(L0_ffn_w_router)),
        "w1_t": chunks(turned(L0_ffn_w1_stack)), "w2_t": chunks(turned(L0_ffn_w2_stack)),
        "ws1_t": chunks(turned(L0_ffn_ws1)), "ws2_t": chunks(turned(L0_ffn_ws2)),
        "ident": np.eye(P, dtype=np.float32), "tri": tri, "const": const,
        "table": np.arange(TILES, dtype=np.float32)[None],
    }
    ins = {"in_" + n: np.ascontiguousarray(a) for n, a in ins.items()}
    nc = bacc.Bacc("TRN2", target_bir_lowering=False, num_devices=1)
    args = [nc.dram_tensor(n, a.shape, F32, kind="ExternalInput").ap() for n, a in ins.items()]
    out = nc.dram_tensor("out", (B, S, D), F32, kind="ExternalOutput").ap()
    decoder_layer(nc, *args, out)
    r = run_bass_kernel_spmd(nc, [ins], core_ids=[0])
    return r.results[0]["out"]
```
